# Optimizing a Trainium2 kernel written in Bass

```python
import numpy as np
import jax
import jax.numpy as jnp

def _softmax(x, axis=-1):
    return jax.nn.softmax(x, axis=axis)

def _gelu(x):
    return jax.nn.gelu(x, approximate=True)

def _silu(x):
    return jax.nn.silu(x)

def _sigmoid(x):
    return jax.nn.sigmoid(x)

def _layernorm(x, axis=-1, eps=1e-05):
    m = jnp.mean(x, axis=axis, keepdims=True)
    v = jnp.var(x, axis=axis, keepdims=True)
    return (x - m) / jnp.sqrt(v + eps)

def _scatter_add(tgt, idx, src, axis=0):
    return tgt.at[idx].add(src)

def _segment_sum(src, seg, n):
    return jax.ops.segment_sum(src, seg, n)
kernel_name = 'mk_gnn_resnorm_d4_gnn_r64_1dfcb5'

def setup_inputs(seed: int=0):
    np.random.seed(seed)
    _w = jnp.asarray

    def _rec_inputs():
        import jax
        import jax.numpy as jnp
        _gk = jax.random.key(seed)
        x = -0.000202 + 1 * jax.random.normal(jax.random.fold_in(_gk, 1), (100000, 64), jnp.float32)
        src = jax.random.randint(jax.random.fold_in(_gk, 2), (50000,), 0, 100000, jnp.int32)
        dst = jax.random.randint(jax.random.fold_in(_gk, 3), (50000,), 0, 100000, jnp.int32)
        _o = jnp.argsort(dst, stable=True)
        src = src[_o]
        dst = dst[_o]
        edge_type_200 = jax.random.randint(jax.random.fold_in(_gk, 12), (50000,), 0, 200, jnp.int32)
        edge_weight = jax.random.uniform(jax.random.fold_in(_gk, 13), (50000,), jnp.float32, 0.0, 1)
        return (x, src, dst, edge_type_200, edge_weight)
    x, src, dst, edge_type_200, edge_weight = _rec_inputs()

    def _L0_gnn_setup():
        import jax, jax.numpy as jnp
        import numpy as np
        N_ENTITIES = 100000
        N_EDGES = 500000
        N_RELATIONS = 200
        DIM = 64
        HEADS = 4
        POW_ITER = 5
        ALPHA = 0.1
        LEAKY_SLOPE = 0.01
        EPS = 1e-16

        def _segment_softmax(scores, seg_ids, num_segments):
            m = jax.ops.segment_max(scores, seg_ids, num_segments=num_segments)
            e = jnp.exp(scores - m[seg_ids])
            denom = jax.ops.segment_sum(e, seg_ids, num_segments=num_segments)
            return e / (denom[seg_ids] + EPS)
        key = jax.random.key(seed)
        ks = jax.random.split(key, 11)
        scale = 0.1
        return {'entity_embed': jax.random.normal(ks[0], (N_ENTITIES, DIM), jnp.float32), 'relation_embed': jax.random.normal(ks[1], (N_RELATIONS, DIM), jnp.float32), 'W_h': jax.random.normal(ks[2], (DIM, HEADS * DIM), jnp.float32) * scale, 'W_t': jax.random.normal(ks[3], (DIM, HEADS * DIM), jnp.float32) * scale, 'W_r': jax.random.normal(ks[4], (DIM, HEADS * DIM), jnp.float32) * scale, 'att_h': jax.random.normal(ks[5], (HEADS, DIM), jnp.float32) * scale, 'att_t': jax.random.normal(ks[6], (HEADS, DIM), jnp.float32) * scale, 'att_r': jax.random.normal(ks[7], (HEADS, DIM), jnp.float32) * scale, 'W_o': jax.random.normal(ks[8], (HEADS * DIM, DIM), jnp.float32) * scale, 'edge_index': jax.random.randint(ks[9], (2, N_EDGES), 0, N_ENTITIES, jnp.int64), 'edge_type': jax.random.randint(ks[10], (N_EDGES,), 0, N_RELATIONS, jnp.int64)}
    _L0_gnn_all = _L0_gnn_setup()
    _L0_gnn_in = {k: v for k, v in _L0_gnn_all.items() if k in ('relation_embed', 'W_h', 'W_t', 'W_r', 'att_h', 'att_t', 'att_r', 'W_o')}
    del _L0_gnn_all

    def _L1_gnn_setup():
        import jax, jax.numpy as jnp
        import numpy as np
        N = 100000
        E = 12500
        D = 64
        NUM_ROUNDS = 4
        EPS = 1e-05
        key = jax.random.key(seed)
        k0, k1, k2 = jax.random.split(key, 3)
        x = jax.random.normal(k0, (N, D), dtype=jnp.float32)
        edge_index = jax.random.randint(k1, (2, E), 0, N, dtype=jnp.int32)
        W = jax.random.normal(k2, (D, D), dtype=jnp.float32) * (1.0 / np.sqrt(D))
        b = jnp.zeros((D,), dtype=jnp.float32)
        gamma = jnp.ones((D,), dtype=jnp.float32)
        beta = jnp.zeros((D,), dtype=jnp.float32)
        return {'x': x, 'edge_index': edge_index, 'W': W, 'b': b, 'gamma': gamma, 'beta': beta, 'num_rounds': NUM_ROUNDS}
    _L1_gnn_all = _L1_gnn_setup()
    _L1_gnn_in = {k: v for k, v in _L1_gnn_all.items() if k in ('W', 'b', 'gamma', 'beta')}
    del _L1_gnn_all

    def _L2_gnn_setup():
        import jax, jax.numpy as jnp
        import numpy as np
        N_NODES = 100000
        N_EDGES_DIR = 12500
        F_IN = 64
        F_OUT = 64
        K = 3

        def _cheb_forward(x, edge_weight, W, bias, edge_index):
            row, col = (edge_index[0], edge_index[1])
            n = x.shape[0]
            deg = jax.ops.segment_sum(edge_weight, row, num_segments=n)
            safe_deg = jnp.where(deg > 0, deg, 1.0)
            dinv = jnp.where(deg > 0, jax.lax.rsqrt(safe_deg), 0.0)
            w = -dinv[row] * edge_weight * dinv[col]

            def prop(t):
                return jax.ops.segment_sum(w[:, None] * t[col], row, num_segments=n)
            Tx0 = x
            out = Tx0 @ W[0]
            Tx1 = prop(Tx0)
            out = out + Tx1 @ W[1]
            for k in range(2, W.shape[0]):
                Tx2 = 2.0 * prop(Tx1) - Tx0
                out = out + Tx2 @ W[k]
                Tx0, Tx1 = (Tx1, Tx2)
            return out + bias
        key = jax.random.key(seed)
        k1, k2, k3, k4, k5 = jax.random.split(key, 5)
        src = jax.random.randint(k1, (N_EDGES_DIR,), 0, N_NODES)
        dst = jax.random.randint(k2, (N_EDGES_DIR,), 0, N_NODES)
        dst = jnp.where(dst == src, (dst + 1) % N_NODES, dst)
        edge_index = jnp.stack([jnp.concatenate([src, dst]), jnp.concatenate([dst, src])])
        edge_weight = jnp.ones((2 * N_EDGES_DIR,), jnp.float32)
        x = jax.random.normal(k3, (N_NODES, F_IN), jnp.float32)
        W = jax.random.normal(k4, (K, F_IN, F_OUT), jnp.float32) * (1.0 / np.sqrt(F_IN * K))
        bias = jax.random.normal(k5, (F_OUT,), jnp.float32) * 0.01
        return {'x': x, 'edge_index': edge_index, 'edge_weight': edge_weight, 'W': W, 'bias': bias}
    _L2_gnn_all = _L2_gnn_setup()
    _L2_gnn_in = {k: v for k, v in _L2_gnn_all.items() if k in ('W', 'bias')}
    del _L2_gnn_all

    def _L3_gnn_setup():
        import jax, jax.numpy as jnp
        import numpy as np
        N = 100000
        E = 25000
        D = 64
        O = 64
        BN_EPS = 1e-05
        key = jax.random.key(seed)
        ks = jax.random.split(key, 8)
        x = jax.random.normal(ks[0], (N, D), dtype=jnp.float32)
        edge_index = jax.random.randint(ks[1], (2, E), 0, N, dtype=jnp.int64)
        s = 1.0 / np.sqrt(D)
        W_lin = jax.random.uniform(ks[2], (D, D), jnp.float32, -s, s)
        b_lin = jax.random.uniform(ks[3], (D,), jnp.float32, -s, s)
        eps = jnp.zeros((1,), jnp.float32)
        W1 = jax.random.uniform(ks[4], (D, D), jnp.float32, -s, s)
        gamma = jnp.ones((D,), jnp.float32)
        beta = jnp.zeros((D,), jnp.float32)
        W2 = jax.random.uniform(ks[5], (O, D), jnp.float32, -s, s)
        return {'x': x, 'edge_index': edge_index, 'W_lin': W_lin, 'b_lin': b_lin, 'eps': eps, 'W1': W1, 'gamma': gamma, 'beta': beta, 'W2': W2}
    _L3_gnn_all = _L3_gnn_setup()
    _L3_gnn_in = {k: v for k, v in _L3_gnn_all.items() if k in ('W_lin', 'b_lin', 'eps', 'W1', 'gamma', 'beta', 'W2')}
    del _L3_gnn_all
    return {'x': x, 'src': src, 'dst': dst, 'edge_type_200': edge_type_200, 'edge_weight': edge_weight, 'L0_gnn_relation_embed': _L0_gnn_in['relation_embed'], 'L0_gnn_W_h': _L0_gnn_in['W_h'], 'L0_gnn_W_t': _L0_gnn_in['W_t'], 'L0_gnn_W_r': _L0_gnn_in['W_r'], 'L0_gnn_att_h': _L0_gnn_in['att_h'], 'L0_gnn_att_t': _L0_gnn_in['att_t'], 'L0_gnn_att_r': _L0_gnn_in['att_r'], 'L0_gnn_W_o': _L0_gnn_in['W_o'], 'L1_gnn_W': _L1_gnn_in['W'], 'L1_gnn_b': _L1_gnn_in['b'], 'L1_gnn_gamma': _L1_gnn_in['gamma'], 'L1_gnn_beta': _L1_gnn_in['beta'], 'L2_gnn_W': _L2_gnn_in['W'], 'L2_gnn_bias': _L2_gnn_in['bias'], 'L3_gnn_W_lin': _L3_gnn_in['W_lin'], 'L3_gnn_b_lin': _L3_gnn_in['b_lin'], 'L3_gnn_eps': _L3_gnn_in['eps'], 'L3_gnn_W1': _L3_gnn_in['W1'], 'L3_gnn_gamma': _L3_gnn_in['gamma'], 'L3_gnn_beta': _L3_gnn_in['beta'], 'L3_gnn_W2': _L3_gnn_in['W2']}

def reference(x, src, dst, edge_type_200, edge_weight, L0_gnn_relation_embed, L0_gnn_W_h, L0_gnn_W_t, L0_gnn_W_r, L0_gnn_att_h, L0_gnn_att_t, L0_gnn_att_r, L0_gnn_W_o, L1_gnn_W, L1_gnn_b, L1_gnn_gamma, L1_gnn_beta, L2_gnn_W, L2_gnn_bias, L3_gnn_W_lin, L3_gnn_b_lin, L3_gnn_eps, L3_gnn_W1, L3_gnn_gamma, L3_gnn_beta, L3_gnn_W2):
    import jax
    import jax.numpy as jnp

    def _L0_gnn_ref(entity_embed, relation_embed, W_h, W_t, W_r, att_h, att_t, att_r, W_o, edge_index, edge_type):
        import jax, jax.numpy as jnp
        import numpy as np
        N_ENTITIES = 100000
        N_EDGES = 500000
        N_RELATIONS = 200
        DIM = 64
        HEADS = 4
        POW_ITER = 5
        ALPHA = 0.1
        LEAKY_SLOPE = 0.01
        EPS = 1e-16

        def _segment_softmax(scores, seg_ids, num_segments):
            m = jax.ops.segment_max(scores, seg_ids, num_segments=num_segments)
            e = jnp.exp(scores - m[seg_ids])
            denom = jax.ops.segment_sum(e, seg_ids, num_segments=num_segments)
            return e / (denom[seg_ids] + EPS)
        head_ids, tail_ids = (edge_index[0], edge_index[1])
        Wh = (entity_embed[head_ids] @ W_h).reshape(-1, HEADS, DIM)
        Wt = (entity_embed[tail_ids] @ W_t).reshape(-1, HEADS, DIM)
        Wr = (relation_embed[edge_type] @ W_r).reshape(-1, HEADS, DIM)
        s_h = jnp.sum(jnp.tanh(Wh) * att_h[None], axis=-1)
        s_t = jnp.sum(jnp.tanh(Wt) * att_t[None], axis=-1)
        s_r = jnp.sum(jnp.tanh(Wr) * att_r[None], axis=-1)
        scores = jax.nn.leaky_relu(s_h + s_t + s_r, negative_slope=LEAKY_SLOPE)
        att = _segment_softmax(scores, head_ids, N_ENTITIES)
        A = (1.0 - ALPHA) * att
        Z0 = entity_embed[:, None, :]
        Z_init = jnp.broadcast_to(Z0, (N_ENTITIES, HEADS, DIM))

        def step(Z, _):
            msgs = A[:, :, None] * Z[tail_ids]
            Z_new = jax.ops.segment_sum(msgs, head_ids, num_segments=N_ENTITIES) + ALPHA * Z0
            return (Z_new, None)
        Z, _ = jax.lax.scan(step, Z_init, None, length=POW_ITER)
        out = Z.reshape(N_ENTITIES, HEADS * DIM) @ W_o
        return out

    def _L1_gnn_ref(x, edge_index, W, b, gamma, beta, num_rounds):
        import jax, jax.numpy as jnp
        import numpy as np
        N = 100000
        E = 12500
        D = 64
        NUM_ROUNDS = 4
        EPS = 1e-05
        n = x.shape[0]
        loops = jnp.arange(n, dtype=edge_index.dtype)
        src = jnp.concatenate([edge_index[0], loops])
        dst = jnp.concatenate([edge_index[1], loops])
        deg = jax.ops.segment_sum(jnp.ones_like(dst, dtype=x.dtype), dst, num_segments=n)
        dis = jnp.where(deg > 0, jax.lax.rsqrt(deg), 0.0)
        norm = dis[src] * dis[dst]
        for _ in range(num_rounds):
            h = x @ W
            msgs = h[src] * norm[:, None]
            agg = jax.ops.segment_sum(msgs, dst, num_segments=n) + b
            mu = agg.mean(axis=-1, keepdims=True)
            var = agg.var(axis=-1, keepdims=True)
            x = (agg - mu) * jax.lax.rsqrt(var + EPS) * gamma + beta
        return x

    def _L2_gnn_ref(x, edge_index, edge_weight, W, bias):
        import jax, jax.numpy as jnp
        import numpy as np
        N_NODES = 100000
        N_EDGES_DIR = 12500
        F_IN = 64
        F_OUT = 64
        K = 3

        def _cheb_forward(x, edge_weight, W, bias, edge_index):
            row, col = (edge_index[0], edge_index[1])
            n = x.shape[0]
            deg = jax.ops.segment_sum(edge_weight, row, num_segments=n)
            safe_deg = jnp.where(deg > 0, deg, 1.0)
            dinv = jnp.where(deg > 0, jax.lax.rsqrt(safe_deg), 0.0)
            w = -dinv[row] * edge_weight * dinv[col]

            def prop(t):
                return jax.ops.segment_sum(w[:, None] * t[col], row, num_segments=n)
            Tx0 = x
            out = Tx0 @ W[0]
            Tx1 = prop(Tx0)
            out = out + Tx1 @ W[1]
            for k in range(2, W.shape[0]):
                Tx2 = 2.0 * prop(Tx1) - Tx0
                out = out + Tx2 @ W[k]
                Tx0, Tx1 = (Tx1, Tx2)
            return out + bias
        return _cheb_forward(x, edge_weight, W, bias, edge_index)

    def _L3_gnn_ref(x, edge_index, W_lin, b_lin, eps, W1, gamma, beta, W2):
        import jax, jax.numpy as jnp
        import numpy as np
        N = 100000
        E = 25000
        D = 64
        O = 64
        BN_EPS = 1e-05
        dst, src = (edge_index[0], edge_index[1])
        h = x @ W_lin.T + b_lin
        message = jax.nn.relu(h[src])
        aggregate = jax.ops.segment_sum(message, dst, num_segments=x.shape[0])
        z = x * (1.0 + eps) + aggregate
        z1 = z @ W1.T
        mean = jnp.mean(z1, axis=0)
        var = jnp.mean((z1 - mean) ** 2, axis=0)
        zn = (z1 - mean) * jax.lax.rsqrt(var + BN_EPS) * gamma + beta
        out = jax.nn.relu(zn) @ W2.T
        return out
    edge_index = jnp.stack([src, dst])
    x = _layernorm(x + _L0_gnn_ref(x, L0_gnn_relation_embed, L0_gnn_W_h, L0_gnn_W_t, L0_gnn_W_r, L0_gnn_att_h, L0_gnn_att_t, L0_gnn_att_r, L0_gnn_W_o, edge_index, edge_type_200), axis=-1)
    x = _layernorm(x + _L1_gnn_ref(x, edge_index, L1_gnn_W, L1_gnn_b, L1_gnn_gamma, L1_gnn_beta, 4), axis=-1)
    x = _layernorm(x + _L2_gnn_ref(x, edge_index, edge_weight, L2_gnn_W, L2_gnn_bias), axis=-1)
    x = _layernorm(x + _L3_gnn_ref(x, edge_index, L3_gnn_W_lin, L3_gnn_b_lin, L3_gnn_eps, L3_gnn_W1, L3_gnn_gamma, L3_gnn_beta, L3_gnn_W2), axis=-1)
    return x

_drawn_inputs = setup_inputs


def setup_inputs(seed=0):
    import zlib

    import numpy as np

    out = dict(_drawn_inputs(seed))
    spreads = {'L1_gnn_b': (0.0, 0.1),
     'L1_gnn_gamma': (1.0, 0.2),
     'L1_gnn_beta': (0.0, 0.1),
     'L3_gnn_gamma': (1.0, 0.2),
     'L3_gnn_beta': (0.0, 0.272)}
    factors = {'L0_gnn_relation_embed': 3.984,
     'L0_gnn_W_h': 6.226,
     'L0_gnn_W_t': 3.755,
     'L0_gnn_W_r': 3.719,
     'L0_gnn_att_h': 6.692,
     'L0_gnn_att_t': 3.852,
     'L0_gnn_att_r': 3.701,
     'L2_gnn_bias': 8.0,
     'L3_gnn_b_lin': 4.049}
    for name, (base, spread) in spreads.items():
        noise = np.random.default_rng([zlib.crc32(name.encode()), seed]).standard_normal(out[name].shape)
        drawn = base * np.exp(spread * noise) if base else spread * noise
        out[name] = jnp.asarray(drawn.astype(out[name].dtype))
    for name, factor in factors.items():
        out[name] = (out[name] * factor).astype(out[name].dtype)
    return out
```

```python
from contextlib import ExitStack, contextmanager

import concourse.bass as bass
from concourse import mybir

P = 128
N = 100000
E = 50000
D = 64
H = 4
R = 200
BLK = 256
NBLK = 392
NP = BLK * NBLK
J = NP // P
TILES = 392
EP = TILES * P
CT = 7
CH = CT * P
PAIRS = TILES // (2 * CT)
Q = 98
BIG = float(1 << 20)
NONE = float(EP)

ALU = mybir.AluOpType
ACT = mybir.ActivationFunctionType
AX = mybir.AxisListType
F32 = mybir.dt.float32
F16 = mybir.dt.float16
BF16 = mybir.dt.bfloat16
I32 = mybir.dt.int32


class Chain:

    def __init__(self, eng, sem, base=0):
        self.eng, self.sem, self.base, self.n = eng, sem, base, 0

    def link(self, ins):
        self.n += 1
        ins.then_inc(self.sem, 1)
        self.eng.wait_ge(self.sem, self.base + self.n)


def repeat(eng, steps):
    def run(body):
        body(0)
        with eng.Fori(1, steps) as i:
            body(i)
    return run


def skewed(eng, steps, most):
    back = -(-most // 2)

    def run(body):
        def pair(i):
            for u in range(2):
                def ago(n):
                    turn = i + (u - n) // 2 if (u - n) // 2 else i
                    out = isinstance(turn, int) and not 0 <= turn < steps
                    return () if out else ((turn, (u - n) % 2),)
                body(ago)
        for i in range(back + 1):
            pair(i)
        with eng.Fori(back + 1, steps) as i:
            pair(i)
        for i in range(steps, steps + back):
            pair(i)
    return run


def wait(eng, sem, value):
    if not (isinstance(value, int) and value <= 0):
        eng.wait_ge(sem, value)


SPENT = []


@contextmanager
def semaphore(nc, name):
    handle = nc.alloc_semaphore(name=name)
    yield handle
    SPENT.append(handle)


def recycle(nc):
    nc.clear_and_free_semaphores(SPENT)
    SPENT.clear()
    nc.all_engine_barrier()


class Tensors:
    pass


def tensors(nc, ctx):
    t = Tensors()

    def sb(name, shape, dt=F32):
        return ctx.enter_context(nc.sbuf_tensor(name, shape, dt))

    def dram(name, shape, dt=F32):
        return nc.dram_tensor(name, shape, dt).ap()

    t.iota = sb("iota", [P, NBLK], F16)
    t.ident = sb("ident", [P, P])
    t.before = sb("before", [P, P], F16)
    t.notbefore = sb("notbefore", [P, P], F16)
    t.beforef = sb("beforef", [P, P])
    t.beforea = sb("beforea", [P, 2, BLK])
    t.ones = sb("ones", [P, P])
    t.base_lo = sb("base_lo", [P, 2, BLK])
    t.base_hi = sb("base_hi", [P, 2, NBLK])
    t.by_lo_s = dram("by_lo_s", [EP, 4])
    t.by_lo_t = dram("by_lo_t", [EP, 2])
    t.sorted_s = dram("sorted_s", [EP, 4])
    t.sorted_t = dram("sorted_t", [EP, 2])
    t.last_of_node = dram("last_of_node", [NP, 1], I32)
    t.in_degree = dram("in_degree", [NP, 1])
    return t


def constants(nc, t):
    with ExitStack() as ctx:
        diff = ctx.enter_context(nc.sbuf_tensor("diff", [P, BLK], I32))
        row = ctx.enter_context(nc.sbuf_tensor("row", [P, NBLK], I32))
        made = ctx.enter_context(semaphore(nc, "iotas_made"))
        block = ctx.enter_context(nc.Block())

        @block.gpsimd
        def _(pool):
            nc.gpsimd.iota(diff[:], [[1, BLK]], base=0, channel_multiplier=-1).then_inc(made, 1)
            nc.gpsimd.iota(row[:], [[1, NBLK]], base=0, channel_multiplier=0).then_inc(made, 1)

        @block.vector
        def _(dve):
            dve.wait_ge(made, 2)
            nc.vector.tensor_copy(t.iota[:], row[:])
            nc.vector.memset(t.ones[:], 1.0)
            nc.vector.tensor_scalar(t.ident[:], diff[:, 0:P], 0.0, None, ALU.is_equal)
            nc.vector.tensor_scalar(t.before[:], diff[:, 0:P], 0.0, None, ALU.is_gt)
            nc.vector.tensor_scalar(t.notbefore[:], diff[:, 0:P], 0.0, None, ALU.is_le)
            nc.vector.tensor_scalar(t.beforef[:], diff[:, 0:P], 0.0, None, ALU.is_gt)
            nc.vector.tensor_scalar(t.beforea[:, 0, :], diff[:], 0.0, None, ALU.is_gt)
            nc.vector.tensor_scalar(t.beforea[:, 1, :], diff[:], float(P), None, ALU.is_gt)


def digits(dve, link, key_i, lo, hi, tmp):
    link(dve.tensor_scalar(tmp, key_i, BLK - 1, None, ALU.bitwise_and))
    link(dve.tensor_copy(lo, tmp))
    link(dve.tensor_scalar(tmp, key_i, 8, None, ALU.logical_shift_right))
    link(dve.tensor_copy(hi, tmp))


def histogram(nc, t, lo, hi):
    with ExitStack() as ctx:
        def sb(name, shape, dt=F32):
            return ctx.enter_context(nc.sbuf_tensor(name, shape, dt))

        def sem(name):
            return ctx.enter_context(semaphore(nc, name))

        oh = sb("onehots", [P, 2, 2, BLK + NBLK], F16)
        zeros = sb("hist_zeros", [P, NBLK], F16)
        cnt = sb("counts", [P, 2, 2, NBLK])
        rows = sb("row_sums", [P, 4])
        rowsb = sb("row_sums_b", [P, 4, P])
        incl = sb("inclusive", [P, NBLK])
        node = sb("node_rows", [P, 2, 2, NBLK])
        flag = sb("node_flags", [P, 2, NBLK])
        turned = sb("turned", [Q, 2, 4, BLK])
        turned_i = sb("turned_i", [Q, 4, BLK], I32)
        ps = ctx.enter_context(nc.psum_tensor("hist_ps", [P, 8, 512], F32))
        ready = sem("onehots_ready")
        used = sem("onehots_used")
        zero = sem("hist_zero")
        chain = sem("hist_chain")
        pe = sem("hist_pe")
        stored = sem("hist_stored")
        block = ctx.enter_context(nc.Block())

        @block.vector
        def _(dve):
            nc.vector.memset(zeros[:], 0.0).then_inc(zero, 1)
            @repeat(dve, TILES // 2)
            def _(i):
                for u in range(2):
                    dve.wait_ge(used, i * 2 + u + 1)
                    for k in range(2):
                        nc.vector.tensor_scalar(oh[:, u, k, 0:BLK], t.iota[:, 0:BLK],
                                                lo[:, k, bass.ds(i * 2 + u, 1)], None, ALU.is_equal)
                        last = nc.vector.tensor_scalar(oh[:, u, k, BLK:], t.iota[:],
                                                       hi[:, k, bass.ds(i * 2 + u, 1)], None, ALU.is_equal)
                    last.then_inc(ready, 1)
            dve.wait_ge(used, TILES + 2)
            c = Chain(dve, chain)
            for k in range(2):
                c.link(nc.vector.tensor_copy(cnt[:, k, :, :], ps[:, 2 * k:2 * k + 2, 0:NBLK]))
                c.link(nc.vector.tensor_reduce(rows[:, 2 * k:2 * k + 2], cnt[:, k, :, :], AX.X, ALU.add))
                for m in range(2):
                    c.link(nc.vector.tensor_scalar(rowsb[:, 2 * k + m, :], t.ones[:],
                                                   rows[:, 2 * k + m:2 * k + m + 1], None, ALU.mult))
            for k in range(2):
                dve.wait_ge(pe, 2 * k + 1)
                c.link(nc.vector.tensor_copy(t.base_lo[:, k, :], ps[:, 4, 0:BLK]))
                c.link(nc.vector.tensor_tensor_scan(incl[:], t.ones[:, 0:1].to_broadcast([P, NBLK]), ps[:, 5, 0:NBLK],
                                                    0.0, ALU.mult, ALU.add))
                c.link(nc.vector.tensor_tensor(t.base_hi[:, k, :], incl[:], ps[:, 5, 0:NBLK], ALU.subtract))
                if k == 0:
                    dve.wait_ge(pe, 2)
                    for m in range(2):
                        c.link(nc.vector.tensor_tensor(node[:, 0, m, :], ps[:, 6 + m, 0:NBLK], t.base_hi[:, 0, :], ALU.add))
                        c.link(nc.vector.tensor_scalar(flag[:, m, :], cnt[:, 0, m, :], 0.0, None, ALU.is_gt))
                        c.link(nc.vector.tensor_tensor(node[:, 0, m, :], node[:, 0, m, :], cnt[:, 0, m, :], ALU.add))
                        c.link(nc.vector.scalar_tensor_tensor(node[:, 0, m, :], node[:, 0, m, :], -1.0 - NONE,
                                                              flag[:, m, :], ALU.add, ALU.mult))
                        c.link(nc.vector.tensor_scalar(node[:, 0, m, :], node[:, 0, m, :], NONE, None, ALU.add))
            for k in range(2):
                for g in range(4):
                    dve.wait_ge(pe, 3 + 4 * k + g + 1)
                    c.link(nc.vector.tensor_copy(turned[:, k, g, :], ps[0:Q, 4 + g, 0:BLK]))
            c.link(nc.vector.tensor_copy(turned_i[:], turned[:, 0, :, :]))

        @block.tensor
        def _(pe_):
            pe_.wait_ge(zero, 1)
            for k in range(2):
                for m in range(2):
                    ins = nc.tensor.matmul(ps[:, 2 * k + m, 0:NBLK], zeros[:, 0:P], zeros[:],
                                           start=True, stop=False, skip_group_check=True)
                ins.then_inc(used, 1)
            @repeat(pe_, TILES // 2)
            def _(i):
                for u in range(2):
                    pe_.wait_ge(ready, i * 2 + u + 1)
                    for k in range(2):
                        for m in range(2):
                            ins = nc.tensor.matmul(ps[:, 2 * k + m, 0:NBLK], oh[:, u, k, m * P:(m + 1) * P],
                                                   oh[:, u, k, BLK:], start=False, stop=False, skip_group_check=True)
                    ins.then_inc(used, 1)
            for k in range(2):
                pe_.wait_ge(chain, [8, 11][k])
                for m in range(2):
                    nc.tensor.matmul(ps[:, 4, 0:BLK], rowsb[:, 2 * k + m, :], t.beforea[:, m, :], start=m == 0, stop=m == 1)
                for m in range(2):
                    ins = nc.tensor.matmul(ps[:, 5, 0:NBLK], t.ones[:], cnt[:, k, m, :], start=m == 0, stop=m == 1)
                ins.then_inc(pe, 1)
                if k == 0:
                    nc.tensor.matmul(ps[:, 6, 0:NBLK], t.beforef[:], cnt[:, 0, 0, :], start=True, stop=True)
                    nc.tensor.matmul(ps[:, 7, 0:NBLK], t.ones[:], cnt[:, 0, 0, :], start=True, stop=False)
                    nc.tensor.matmul(ps[:, 7, 0:NBLK], t.beforef[:], cnt[:, 0, 1, :], start=False, stop=True).then_inc(pe, 1)
            for k in range(2):
                for g in range(4):
                    pe_.wait_ge(chain, 24 if k == 0 else 24 + g + 1)
                    for m in range(2):
                        src = node[:, 0, m, :] if k == 0 else cnt[:, 1, m, :]
                        ins = nc.tensor.transpose(ps[0:Q, 4 + g, m * P:(m + 1) * P],
                                                  src[:, g * Q:(g + 1) * Q], t.ident[:])
                    ins.then_inc(pe, 1)

        @block.sync
        def _(sp):
            sp.wait_ge(chain, 33)
            sp.dma_start(t.last_of_node.rearrange("(g q a) o -> q g (a o)", g=4, q=Q), turned_i[:]).then_inc(stored, 16)
            sp.dma_start(t.in_degree.rearrange("(g q a) o -> q g (a o)", g=4, q=Q), turned[:, 1, :, :]).then_inc(stored, 16)
            sp.wait_ge(stored, 32)


def radix_pass(nc, t, name, pay, dig, width, base, dst):
    W = [4, 2]
    with ExitStack() as ctx:
        def sb(n, shape, dt=F32):
            return ctx.enter_context(nc.sbuf_tensor(f"{name}_{n}", shape, dt))

        def sem(n):
            return ctx.enter_context(semaphore(nc, f"{name}_{n}"))

        oh = sb("onehot", [P, 2, 2, width], F16)
        junk = sb("junk", [P, 2, 2, width])
        pos = sb("pos", [P, 2, 2, CT])
        pos_i = sb("pos_i", [P, 2, 2, CT], I32)
        stage = [sb(f"stage{k}", [P, 2, CT, W[k]]) for k in range(2)]
        acc = ctx.enter_context(nc.psum_tensor(f"{name}_acc", [P, 2, 512], F32))
        ready, counted, freed = sem("onehot_ready"), sem("counted"), sem("onehot_free")
        picked, posok = sem("picked"), sem("positions_ready")
        staged, passed = sem("staged"), sem("passed")
        sent = [sem("sent0"), sem("sent1")]
        block = ctx.enter_context(nc.Block())
        B = 2 * CT

        @block.vector
        def _(dve):
            def onehot(i, n):
                dve.wait_ge(freed, i * B + n + 1)
                for k in range(2):
                    ins = nc.vector.tensor_scalar(oh[:, n % 2, k, :], t.iota[:, 0:width],
                                                  dig[:, k, bass.ds(i * B + n, 1)], None, ALU.is_equal)
                ins.then_inc(ready, 1)

            @repeat(dve, PAIRS)
            def _(i):
                onehot(i, 0)
                for u in range(2):
                    wait(dve, sent[u], i * 16 * 2 * CT)
                    for c in range(CT):
                        n = u * CT + c
                        if n + 1 < B:
                            onehot(i, n + 1)
                        dve.wait_ge(counted, i * B + n + 1)
                        for k in range(2):
                            ins = nc.vector.tensor_tensor_reduce(junk[:, n % 2, k, :], oh[:, n % 2, k, :], acc[:, k, 0:width],
                                                                 1.0, 0.0, ALU.mult, ALU.add, pos[:, u, k, c:c + 1])
                        ins.then_inc(picked, 1)
                    dve.wait_ge(picked, i * B + (u + 1) * CT)
                    nc.vector.tensor_copy(pos_i[:, u, :, :], pos[:, u, :, :]).then_inc(posok, 1)

        @block.tensor
        def _(pe):
            for k in range(2):
                nc.tensor.matmul(acc[:, k, 0:width], t.ident[:], base[:, k, :], start=True, stop=False,
                                 skip_group_check=True).then_inc(freed, 1)
            @repeat(pe, PAIRS)
            def _(i):
                for n in range(B):
                    pe.wait_ge(ready, i * B + n + 1)
                    for k in range(2):
                        ins = nc.tensor.matmul(acc[:, k, 0:width], t.before[:], oh[:, n % 2, k, :],
                                               start=False, stop=False, skip_group_check=True)
                    ins.then_inc(counted, 1)
                    pe.wait_ge(picked, i * B + n + 1)
                    for k in range(2):
                        ins = nc.tensor.matmul(acc[:, k, 0:width], t.notbefore[:], oh[:, n % 2, k, :],
                                               start=False, stop=False, skip_group_check=True)
                    ins.then_inc(freed, 1)

        @block.scalar
        def _(act):
            @repeat(act, PAIRS)
            def _(i):
                for u in range(2):
                    wait(act, sent[u], i * 16 * 2 * CT)
                    for k in range(2):
                        ins = nc.scalar.copy(stage[k][:, u, :, :], pay[k][:, bass.ds(i * B + u * CT, CT), 0:W[k]])
                    ins.then_inc(staged, 1)

        @block.gpsimd
        def _(pool):
            @repeat(pool, PAIRS)
            def _(i):
                for u in range(2):
                    pool.wait_ge(posok, i * 2 + u + 1)
                    pool.wait_ge(staged, i * 2 + u + 1)
                    pool.sem_inc(passed, 1)
                    for c in range(CT):
                        for k in range(2):
                            pool.indirect_dma_start(
                                out=dst[k], out_offset=bass.IndirectOffsetOnAxis(pos_i[:, u, k, c:c + 1], 0),
                                in_=stage[k][:, u, c, :], in_offset=None).then_inc(sent[u], 16)
            for u in range(2):
                pool.wait_ge(sent[u], PAIRS * 16 * 2 * CT)


def sort_edges(nc, t, src, dst, etype, weight):
    with ExitStack() as ctx:
        def sb(name, shape, dt=F32):
            return ctx.enter_context(nc.sbuf_tensor(name, shape, dt))

        lo = sb("digit_lo", [P, 2, TILES])
        hi = sb("digit_hi", [P, 2, TILES])
        pay_s = sb("payload_s", [P, TILES, 4])
        pay_t = sb("payload_t", [P, TILES, 2])
        key = sb("keys_i", [P, 3, TILES], I32)
        w = sb("weights_in", [P, TILES])
        tmp = sb("digit_tmp", [P, TILES], I32)
        with ExitStack() as c2:
            loaded = c2.enter_context(semaphore(nc, "edges_loaded"))
            chain = c2.enter_context(semaphore(nc, "digit_chain"))
            block = c2.enter_context(nc.Block())

            @block.sync
            def _(sp):
                for n, a in enumerate((src, dst, etype)):
                    sp.dma_start(key[:, n, :], a).then_inc(loaded, 16)
                sp.dma_start(w[:], weight).then_inc(loaded, 16)

            @block.vector
            def _(dve):
                dve.wait_ge(loaded, 64)
                c = Chain(dve, chain)
                for k in range(2):
                    digits(nc.vector, c.link, key[:, k, :], lo[:, k, :], hi[:, k, :], tmp[:])
                for n in range(3):
                    nc.vector.tensor_copy(pay_s[:, :, n], key[:, n, :])
                nc.vector.tensor_copy(pay_s[:, :, 3], w[:])
                nc.vector.tensor_copy(pay_t[:, :, 0], key[:, 1, :])
                nc.vector.tensor_copy(pay_t[:, :, 1], key[:, 0, :])

        histogram(nc, t, lo, hi)
        radix_pass(nc, t, "low", [pay_s, pay_t], lo, BLK, t.base_lo, [t.by_lo_s, t.by_lo_t])
        with ExitStack() as c2:
            loaded = c2.enter_context(semaphore(nc, "by_lo_loaded"))
            chain = c2.enter_context(semaphore(nc, "digit2_chain"))
            block = c2.enter_context(nc.Block())

            @block.sync
            def _(sp):
                sp.dma_start(pay_s[:], t.by_lo_s.rearrange("(j p) w -> p j w", p=P)).then_inc(loaded, 16)
                sp.dma_start(pay_t[:], t.by_lo_t.rearrange("(j p) w -> p j w", p=P)).then_inc(loaded, 16)

            @block.vector
            def _(dve):
                dve.wait_ge(loaded, 32)
                c = Chain(dve, chain)
                for k, pay in enumerate((pay_s, pay_t)):
                    c.link(nc.vector.tensor_copy(key[:, k, :], pay[:, :, 0]))
                    c.link(nc.vector.tensor_scalar(tmp[:], key[:, k, :], 8, None, ALU.logical_shift_right))
                    c.link(nc.vector.tensor_copy(hi[:, k, :], tmp[:]))

        radix_pass(nc, t, "high", [pay_s, pay_t], hi, NBLK, t.base_hi, [t.sorted_s, t.sorted_t])


def add_tensors(nc, ctx, t):
    def sb(name, shape, dt=F32):
        return ctx.enter_context(nc.sbuf_tensor(name, shape, dt))

    def dram(name, shape, dt=F32):
        return nc.dram_tensor(name, shape, dt).ap()

    more = TILES + 2 * CT
    t.s_col = sb("s_col", [P, more], I32)
    t.t_col = sb("t_col", [P, more], I32)
    t.t_row_s = sb("t_row_s", [P, more], I32)
    t.next_col = sb("next_col", [P, more], I32)
    t.put_s = sb("put_s", [P, more], I32)
    t.put_t = sb("put_t", [P, more], I32)
    t.w_col = sb("w_col", [P, TILES])
    t.negdinv_col = sb("negdinv_col", [P, TILES])
    t.negdinv2_col = sb("negdinv2_col", [P, TILES])
    t.deg_col = sb("deg_col", [P, TILES])
    t.att_col = sb("att_col", [P, TILES, H])
    t.key_s = sb("key_s", [P, TILES])
    t.key_t = sb("key_t", [P, TILES])
    t.same_s = sb("same_s", [P, TILES])
    t.last_s = sb("last_s", [P, TILES])
    t.span_s = sb("span_s", [Q, 4, TILES])
    t.span_t = sb("span_t", [Q, 4, TILES])
    t.fix_edge = sb("fix_edge", [Q, 4], I32)
    t.fix_node_s = sb("fix_node_s", [Q, 4], I32)
    t.fix_node_t = sb("fix_node_t", [Q, 4], I32)
    t.row_s = dram("row_s", [10, EP])
    t.row_t = dram("row_t", [3, EP])
    t.firsts = dram("firsts", [2, TILES + 8])
    t.eq_s = dram("eq_s", [TILES // CT, P, CH])
    t.eq_t = dram("eq_t", [TILES // CT, P, CH])
    t.x_dst = dram("x_dst", [TILES // CT, P, CT * D])
    t.scores = dram("scores", [H, EP])
    t.edges_a = dram("edges_a", [EP + P, H * D])
    t.edges_b = dram("edges_b", [EP + P, H * D])
    t.sum0 = dram("sum0", [NP + 512, D + 1])
    t.sum_s = dram("sum_s", [NP + 512, D])
    t.sum_t = dram("sum_t", [NP + 512, D])
    t.lasts = dram("lasts", [TILES, D + 1])
    t.cheb_msg = dram("cheb_msg", [TILES // CT, P, CT * D])
    t.cheb_rows = dram("cheb_rows", [EP + P, D])


def clear_tables(nc, t):
    with ExitStack() as ctx:
        z = ctx.enter_context(nc.sbuf_tensor("zeros", [P, 4096], F32))
        made = ctx.enter_context(semaphore(nc, "zeros_made"))
        wrote = ctx.enter_context(semaphore(nc, "zeros_written"))
        block = ctx.enter_context(nc.Block())

        @block.vector
        def _(dve):
            nc.vector.memset(z[:], 0.0).then_inc(made, 1)

        @block.sync
        def _(sp):
            sp.wait_ge(made, 1)
            n = 0
            for tab in (t.sum0, t.sum_s, t.sum_t):
                w = tab.shape[1]
                flat = tab.rearrange("(p r) w -> p (r w)", p=P)
                total = flat.shape[1]
                for a in range(0, total, 4096):
                    b = min(total, a + 4096)
                    sp.dma_start(flat[:, a:b], z[:, 0:b - a]).then_inc(wrote, 16)
                    n += 1
            for tab in (t.edges_a, t.edges_b, t.cheb_rows):
                sp.dma_start(tab[EP:EP + P, :], z[:, 0:tab.shape[1]]).then_inc(wrote, 16)
                n += 1
            sp.wait_ge(wrote, 16 * n)


def segment_scan(nc, t, name, factor, adds, outs, reverse, biggest=False):
    C = len(adds)
    floor = -1e30 if biggest else 0.0
    op0, op1 = (ALU.add, ALU.max) if biggest else (ALU.mult, ALU.add)

    def way(ap):
        return ap[:, ::-1] if reverse else ap

    end = 0 if reverse else TILES - 1
    with ExitStack() as ctx:
        ends = ctx.enter_context(nc.sbuf_tensor(f"{name}_ends", [P, 2, C], F32))
        across = ctx.enter_context(nc.sbuf_tensor(f"{name}_across", [C, 4, P], F32))
        into = ctx.enter_context(nc.sbuf_tensor(f"{name}_into", [P, C], F32))
        whole = ctx.enter_context(nc.sbuf_tensor(f"{name}_whole", [P, 1], F32))
        ps = ctx.enter_context(nc.psum_tensor(f"{name}_ps", [P, 3, 512], F32))
        chain = ctx.enter_context(semaphore(nc, f"{name}_chain"))
        turned = ctx.enter_context(semaphore(nc, f"{name}_turned"))
        block = ctx.enter_context(nc.Block())

        @block.vector
        def _(dve):
            c = Chain(dve, chain)
            c.link(nc.vector.tensor_reduce(whole[:], factor, AX.X, ALU.min))
            c.link(nc.vector.tensor_scalar(ends[:, 1, :], t.ones[:, 0:C], whole[:], None, ALU.mult))
            for k in range(C):
                c.link(nc.vector.tensor_tensor_scan(way(outs[k]), way(factor), way(adds[k]), floor, op0, op1))
                c.link(nc.vector.tensor_copy(ends[:, 0, k:k + 1], outs[k][:, end:end + 1]))
            dve.wait_ge(turned, 1)
            c.link(nc.vector.tensor_copy(across[:, 0:2, :], ps[0:C, 0:2, 0:P]))
            c.link(nc.vector.tensor_tensor_scan(way(across[:, 2, :]), way(across[:, 1, :]), way(across[:, 0, :]),
                                                floor, op0, op1))
            c.link(nc.vector.memset(across[:, 3, :], floor))
            if reverse:
                c.link(nc.vector.tensor_copy(across[:, 3, 0:P - 1], across[:, 2, 1:P]))
            else:
                c.link(nc.vector.tensor_copy(across[:, 3, 1:P], across[:, 2, 0:P - 1]))
            dve.wait_ge(turned, 2)
            c.link(nc.vector.tensor_copy(into[:], ps[:, 2, 0:C]))
            for k in range(C):
                c.link(nc.vector.tensor_tensor_scan(way(outs[k]), way(factor), way(adds[k]), into[:, k:k + 1],
                                                    op0, op1))

        @block.tensor
        def _(pe):
            pe.wait_ge(chain, 2 + 2 * C)
            nc.tensor.transpose(ps[0:C, 0, 0:P], ends[:, 0, :], t.ident[:])
            nc.tensor.transpose(ps[0:C, 1, 0:P], ends[:, 1, :], t.ident[:]).then_inc(turned, 1)
            pe.wait_ge(chain, 2 + 2 * C + 4)
            nc.tensor.transpose(ps[:, 2, 0:C], across[:, 3, :], t.ident[0:C, 0:C]).then_inc(turned, 1)


def to_tiles(nc, t, name, rows, outs):
    F = len(rows)
    with ExitStack() as ctx:
        flat = ctx.enter_context(nc.sbuf_tensor(f"{name}_flat", [Q, F, 4, P], F32))
        ps = ctx.enter_context(nc.psum_tensor(f"{name}_ps", [P, 2, 512], F32))
        loaded = ctx.enter_context(semaphore(nc, f"{name}_loaded"))
        turned = ctx.enter_context(semaphore(nc, f"{name}_turned"))
        read = ctx.enter_context(semaphore(nc, f"{name}_read"))
        block = ctx.enter_context(nc.Block())

        @block.sync
        def _(sp):
            for f in range(F):
                sp.dma_start(flat[:, f], rows[f].rearrange("(c q p) -> q c p", c=4, q=Q)).then_inc(loaded, 16)

        @block.tensor
        def _(pe):
            pe.wait_ge(loaded, 16 * F)
            for f in range(F):
                if f >= 2:
                    pe.wait_ge(read, f - 1)
                for c in range(4):
                    ins = nc.tensor.transpose(ps[:, f % 2, c * Q:(c + 1) * Q], flat[:, f, c, :], t.ident[0:Q, 0:Q])
                ins.then_inc(turned, 1)

        @block.vector
        def _(dve):
            for f in range(F):
                dve.wait_ge(turned, f + 1)
                nc.vector.tensor_copy(outs[f], ps[:, f % 2, 0:TILES]).then_inc(read, 1)


def edge_fields(nc, t):
    with ExitStack() as ctx:
        def sb(name, shape, dt=F32):
            return ctx.enter_context(nc.sbuf_tensor(name, shape, dt))

        pay_s = sb("sorted_rows_s", [P, TILES, 4])
        pay_t = sb("sorted_rows_t", [P, TILES, 2])
        keys = sb("keys_with_ends", [P, 2, TILES + 2])
        tmp = sb("field_tmp", [P, 2, TILES])
        last_t = sb("last_t", [P, TILES])
        fields = sb("fields", [P, 6, TILES])
        fields_t = sb("fields_t", [P, 2, TILES])
        deg = sb("deg_scan", [P, 3, TILES])
        pick = sb("deg_pick", [P, 2, TILES])
        sums = [t.sorted_s, t.sorted_t]
        with ExitStack() as c2:
            loaded = c2.enter_context(semaphore(nc, "rows_loaded"))
            ends = c2.enter_context(semaphore(nc, "key_ends_set"))
            chain = c2.enter_context(semaphore(nc, "field_chain"))
            stored = c2.enter_context(semaphore(nc, "fields_stored"))
            block = c2.enter_context(nc.Block())

            @block.sync
            def _(sp):
                sp.dma_start(pay_s[:], t.sorted_s.rearrange("(p j) w -> p j w", p=P)).then_inc(loaded, 16)
                sp.dma_start(pay_t[:], t.sorted_t.rearrange("(p j) w -> p j w", p=P)).then_inc(loaded, 16)
                sp.wait_ge(ends, 1)
                for k in range(2):
                    rows = sums[k].rearrange("(p j) w -> p j w", p=P)
                    sp.dma_start(keys[1:P, k, 0:1], rows[0:P - 1, TILES - 1, 0:1], allow_slow_non_contiguous=True).then_inc(loaded, 16)
                    sp.dma_start(keys[0:P - 1, k, TILES + 1:TILES + 2], rows[1:P, 0, 0:1], allow_slow_non_contiguous=True).then_inc(loaded, 16)
                sp.wait_ge(chain, 18)
                for f in range(5):
                    sp.dma_start(t.row_s[f].rearrange("(p j) -> p j", p=P), fields[:, f, :]).then_inc(stored, 16)
                for f in range(2):
                    sp.dma_start(t.row_t[f].rearrange("(p j) -> p j", p=P), fields_t[:, f, :]).then_inc(stored, 16)
                sp.dma_start(t.row_t[2].rearrange("(p j) -> p j", p=P), fields[:, 5, :]).then_inc(stored, 16)
                sp.wait_ge(stored, 16 * 8)

            @block.vector
            def _(dve):
                nc.vector.memset(keys[:], -1.0).then_inc(ends, 1)
                dve.wait_ge(ends, 1)
                dve.wait_ge(loaded, 96)
                c = Chain(dve, chain)
                for k, pay in enumerate((pay_s, pay_t)):
                    c.link(nc.vector.tensor_copy(keys[:, k, 1:TILES + 1], pay[:, :, 0]))
                c.link(nc.vector.tensor_tensor(t.same_s[:], keys[:, 0, 1:TILES + 1], keys[:, 0, 0:TILES], ALU.is_equal))
                for k, last in enumerate((t.last_s, last_t)):
                    c.link(nc.vector.tensor_tensor(last[:], keys[:, k, 1:TILES + 1], keys[:, k, 2:TILES + 2], ALU.not_equal))
                    c.link(nc.vector.tensor_scalar(tmp[:, 0, :], last[:], -BIG, BIG, ALU.mult, ALU.add))
                    c.link(nc.vector.tensor_scalar(tmp[:, 1, :], keys[:, k, 1:TILES + 1], float(N), BIG, ALU.is_ge, ALU.mult))
                    c.link(nc.vector.tensor_tensor(tmp[:, 0, :], tmp[:, 0, :], tmp[:, 1, :], ALU.add))
                    c.link(nc.vector.tensor_tensor(fields[:, 4 + k, :], tmp[:, 0, :], keys[:, k, 1:TILES + 1], ALU.add))
                for f, src in enumerate((0, 1, 3, 2)):
                    ins = nc.vector.tensor_copy(fields[:, f, :], pay_s[:, :, src])
                c.link(ins)
                c.link(nc.vector.tensor_copy(fields_t[:, 0, :], pay_t[:, :, 0]))
                c.link(nc.vector.tensor_copy(fields_t[:, 1, :], pay_t[:, :, 1]))
                c.link(nc.vector.tensor_copy(deg[:, 0, :], pay_s[:, :, 3]))
                c.link(nc.vector.tensor_scalar(pick[:, 0, :], t.last_s[:], -1.0, 1.0, ALU.mult, ALU.add))

        segment_scan(nc, t, "deg_up", t.same_s[:], [deg[:, 0, :]], [deg[:, 1, :]], reverse=False)
        last_only(nc, "deg", t, [deg[:, 1, :]], [pick[:, 1, :]])
        segment_scan(nc, t, "deg_down", pick[:, 0, :], [pick[:, 1, :]], [deg[:, 2, :]], reverse=True)
        with ExitStack() as c2:
            stored = c2.enter_context(semaphore(nc, "deg_stored"))
            block = c2.enter_context(nc.Block())

            @block.sync
            def _(sp):
                sp.dma_start(t.row_s[5].rearrange("(p j) -> p j", p=P), deg[:, 2, :]).then_inc(stored, 16)
                sp.wait_ge(stored, 16)
    to_tiles(nc, t, "cols_s", [t.row_s[0], t.row_s[0], t.row_s[1], t.row_s[2], t.row_s[4], t.row_s[5]],
             [t.s_col[:, 0:TILES], t.key_s[:], t.t_col[:, 0:TILES], t.w_col[:], t.put_s[:, 0:TILES], t.deg_col[:]])
    to_tiles(nc, t, "cols_t", [t.row_t[0], t.row_t[1], t.row_t[2]],
             [t.key_t[:], t.t_row_s[:, 0:TILES], t.put_t[:, 0:TILES]])
    with ExitStack() as ctx:
        tmp = ctx.enter_context(nc.sbuf_tensor("dinv_tmp", [P, 2, TILES], F32))
        chain = ctx.enter_context(semaphore(nc, "dinv_chain"))
        root = ctx.enter_context(semaphore(nc, "dinv_root"))
        block = ctx.enter_context(nc.Block())

        @block.vector
        def _(dve):
            c = Chain(dve, chain)
            for a in (t.s_col, t.t_col, t.t_row_s, t.put_s, t.put_t, t.next_col):
                nc.vector.memset(a[:, TILES:], 0)
            inverse_root(c, nc, dve, t.deg_col[:], tmp[:, 0, :], tmp[:, 1, :], root)
            c.link(nc.vector.tensor_scalar(t.negdinv_col[:], tmp[:, 0, :], -1.0, None, ALU.mult))
            c.link(nc.vector.scalar_tensor_tensor(t.negdinv2_col[:], tmp[:, 0, :], -1.0, tmp[:, 0, :], ALU.mult, ALU.mult))

        @block.scalar
        def _(act):
            act.wait_ge(chain, 3)
            nc.scalar.activation(tmp[:, 0, :], tmp[:, 0, :], ACT.Sqrt).then_inc(root, 1)


def inverse_root(c, nc, dve, deg, out, has, root):
    c.link(nc.vector.tensor_scalar(has, deg, 0.0, None, ALU.is_gt))
    c.link(nc.vector.tensor_tensor(out, deg, has, ALU.mult))
    c.link(nc.vector.scalar_tensor_tensor(out, out, 1.0, has, ALU.add, ALU.subtract))
    dve.wait_ge(root, 1)
    c.link(nc.vector.reciprocal(out, out))
    c.link(nc.vector.tensor_tensor(out, out, has, ALU.mult))


def last_only(nc, name, t, ins, outs):
    with ExitStack() as ctx:
        block = ctx.enter_context(nc.Block())

        @block.vector
        def _(dve):
            for a, b in zip(ins, outs):
                nc.vector.tensor_tensor(b, a, t.last_s[:], ALU.mult)


def spans(nc, t, k, row, span, fix_edge, fix_node):
    n = f"span{k}_"
    with ExitStack() as ctx:
        def sb(name, shape, dt=F32):
            return ctx.enter_context(nc.sbuf_tensor(n + name, shape, dt))

        def sem(name):
            return ctx.enter_context(semaphore(nc, n + name))

        keys = sb("keys", [Q, 4, P])
        first = sb("first", [Q, 4])
        nxt = sb("next", [Q, 4])
        frow = sb("frow", [Q, TILES])
        order = sb("order", [Q, TILES], I32)
        orderf = sb("orderf", [Q, TILES])
        tile_i = sb("tile_i", [Q, 4], I32)
        tile = sb("tile", [Q, 4])
        eq = sb("eq", [Q, 4, P])
        cnt = sb("cnt", [Q, 4])
        tmp = sb("tmp", [Q, 6, 4])
        minus = sb("minus", [1, 8])
        loaded, chain, made, stored, again = sem("loaded"), sem("chain"), sem("made"), sem("stored"), sem("again")
        block = ctx.enter_context(nc.Block())

        @block.gpsimd
        def _(pool):
            nc.gpsimd.iota(order[:], [[1, TILES]], base=0, channel_multiplier=-1).then_inc(made, 1)
            nc.gpsimd.iota(tile_i[:], [[Q, 4]], base=0, channel_multiplier=1).then_inc(made, 1)

        @block.sync
        def _(sp):
            sp.dma_start(keys[:], row.rearrange("(c q p) -> q c p", c=4, q=Q)).then_inc(loaded, 16)
            sp.wait_ge(chain, 2)
            sp.dma_start(t.firsts[k, 0:TILES].rearrange("(c q) -> q c", c=4), first[:], allow_slow_non_contiguous=True).then_inc(stored, 16)
            sp.dma_start(t.firsts[k:k + 1, TILES:TILES + 8], minus[:]).then_inc(stored, 16)
            sp.wait_ge(stored, 32)
            sp.dma_start(nxt[:], t.firsts[k, 1:TILES + 1].rearrange("(c q) -> q c", c=4), allow_slow_non_contiguous=True).then_inc(again, 16)
            sp.dma_start(frow[:], t.firsts[k:k + 1, 0:TILES].partition_broadcast(Q)).then_inc(again, 16)

        @block.vector
        def _(dve):
            c = Chain(dve, chain)
            c.link(nc.vector.memset(minus[:], -1.0))
            dve.wait_ge(loaded, 16)
            c.link(nc.vector.tensor_copy(first[:], keys[:, :, 0]))
            dve.wait_ge(made, 2)
            c.link(nc.vector.tensor_copy(orderf[:], order[:]))
            c.link(nc.vector.tensor_copy(tile[:], tile_i[:]))
            c.link(nc.vector.tensor_tensor(eq[:], keys[:], first[:].unsqueeze(2).to_broadcast([Q, 4, P]), ALU.is_equal))
            c.link(nc.vector.tensor_reduce(cnt[:], eq[:], AX.X, ALU.add))
            c.link(nc.vector.scalar_tensor_tensor(tmp[:, 0, :], tile[:], float(P), cnt[:], ALU.mult, ALU.add))
            c.link(nc.vector.tensor_scalar(tmp[:, 0, :], tmp[:, 0, :], -1.0, None, ALU.add))
            if fix_edge is not None:
                c.link(nc.vector.tensor_copy(fix_edge, tmp[:, 0, :]))
            dve.wait_ge(again, 32)
            c.link(nc.vector.tensor_tensor(tmp[:, 1, :], first[:], nxt[:], ALU.is_equal))
            c.link(nc.vector.tensor_scalar(tmp[:, 2, :], cnt[:], float(P), None, ALU.is_equal))
            c.link(nc.vector.tensor_tensor(tmp[:, 1, :], tmp[:, 1, :], tmp[:, 2, :], ALU.mult))
            c.link(nc.vector.tensor_scalar(tmp[:, 2, :], first[:], float(N), None, ALU.is_ge))
            c.link(nc.vector.tensor_tensor(tmp[:, 1, :], tmp[:, 1, :], tmp[:, 2, :], ALU.max))
            c.link(nc.vector.scalar_tensor_tensor(tmp[:, 3, :], tile[:], float(NP), first[:], ALU.add, ALU.subtract))
            c.link(nc.vector.tensor_tensor(tmp[:, 3, :], tmp[:, 3, :], tmp[:, 1, :], ALU.mult))
            c.link(nc.vector.tensor_tensor(tmp[:, 3, :], tmp[:, 3, :], first[:], ALU.add))
            c.link(nc.vector.tensor_copy(fix_node, tmp[:, 3, :]))
            for g in range(4):
                c.link(nc.vector.tensor_scalar(span[:, g, :], orderf[:], float(g * Q), None, ALU.is_gt))
                c.link(nc.vector.scalar_tensor_tensor(span[:, g, :], frow[:], keys[:, g, P - 1:P], span[:, g, :],
                                                      ALU.is_equal, ALU.mult))


def equal_tables(nc, t):
    with ExitStack() as ctx:
        rows = ctx.enter_context(nc.sbuf_tensor("eq_rows", [P, 2, CT, P], F32))
        eq = ctx.enter_context(nc.sbuf_tensor("eq_made", [P, 2, CT, P], F32))
        loaded = [ctx.enter_context(semaphore(nc, f"eq_loaded{u}")) for u in range(2)]
        made = [ctx.enter_context(semaphore(nc, f"eq_ready{u}")) for u in range(2)]
        stored = [ctx.enter_context(semaphore(nc, f"eq_stored{u}")) for u in range(2)]
        sp_passed = ctx.enter_context(semaphore(nc, "eq_sp_passed"))
        block = ctx.enter_context(nc.Block())
        both = ((t.row_s[0:1, :], t.key_s, t.eq_s, 0), (t.row_t[0:1, :], t.key_t, t.eq_t, PAIRS))

        @block.sync
        def _(sp):
            for row, col, out, done in both:
                @repeat(sp, PAIRS)
                def _(i):
                    for u in range(2):
                        wait(sp, made[u], i + done)
                        sp.sem_inc(sp_passed, 1)
                        sp.dma_start(rows[:, u], row[:, bass.ds((i * 2 + u) * CH, CH)].partition_broadcast(P)
                                     .rearrange("q o (c p) -> q (o c) p", c=CT)).then_inc(loaded[u], 16)

        @block.vector
        def _(dve):
            for row, col, out, done in both:
                @repeat(dve, PAIRS)
                def _(i):
                    for u in range(2):
                        dve.wait_ge(loaded[u], (i + done + 1) * 16)
                        wait(dve, stored[u], (i + done) * 16)
                        nc.vector.tensor_tensor(eq[:, u], rows[:, u],
                                                col[:, bass.ds((i * 2 + u) * CT, CT)].unsqueeze(2).to_broadcast([P, CT, P]),
                                                ALU.is_equal).then_inc(made[u], 1)

        @block.scalar
        def _(act):
            for row, col, out, done in both:
                @repeat(act, PAIRS)
                def _(i):
                    for u in range(2):
                        act.wait_ge(made[u], i + done + 1)
                        act.dma_start(out[bass.ds(i * 2 + u, 1)].rearrange("o p c -> p (o c)"),
                                      eq[:, u].rearrange("p c e -> p (c e)")).then_inc(stored[u], 16)
            for u in range(2):
                act.wait_ge(stored[u], 2 * PAIRS * 16)


def follow(nc, t):
    with ExitStack() as ctx:
        idx = ctx.enter_context(nc.sbuf_tensor("follow_idx", [P, 2, CT], I32))
        got = ctx.enter_context(nc.sbuf_tensor("follow_got", [P, 2, CT], I32))
        ready = [ctx.enter_context(semaphore(nc, f"follow_idx_ready{u}")) for u in range(2)]
        gathered = [ctx.enter_context(semaphore(nc, f"followed{u}")) for u in range(2)]
        kept = [ctx.enter_context(semaphore(nc, f"follow_kept{u}")) for u in range(2)]
        passed = ctx.enter_context(semaphore(nc, "follow_passed"))
        block = ctx.enter_context(nc.Block())

        @block.vector
        def _(dve):
            for u in range(2):
                nc.vector.tensor_copy(idx[:, u], t.t_col[:, u * CT:(u + 1) * CT]).then_inc(ready[u], 1)
            @repeat(dve, PAIRS)
            def _(i):
                for u in range(2):
                    dve.wait_ge(gathered[u], (i + 1) * 16 * CT)
                    nc.vector.tensor_copy(t.next_col[:, bass.ds((i * 2 + u) * CT, CT)], got[:, u]).then_inc(kept[u], 1)
                    nc.vector.tensor_copy(idx[:, u], t.t_col[:, bass.ds((i * 2 + 2 + u) * CT, CT)]).then_inc(ready[u], 1)

        @block.gpsimd
        def _(pool):
            @repeat(pool, PAIRS)
            def _(i):
                for u in range(2):
                    pool.wait_ge(ready[u], i + 1)
                    wait(pool, kept[u], i)
                    pool.sem_inc(passed, 1)
                    for c in range(CT):
                        pool.indirect_dma_start(out=got[:, u, c:c + 1], out_offset=None, in_=t.last_of_node,
                                                in_offset=bass.IndirectOffsetOnAxis(idx[:, u, c:c + 1], 0)
                                                ).then_inc(gathered[u], 16)


def weights(nc, ctx, t, w):
    def sb(name, shape, dt=F32):
        return ctx.enter_context(nc.sbuf_tensor(name, shape, dt))

    t.b_lin = w["L3_gnn_b_lin"]
    t.w_ht = sb("w_ht", [P, H * D])
    t.w_r = sb("w_r", [D, H * D])
    t.att = sb("att", [P, 3, 2, H])
    t.rel_score = sb("rel_score", [R // 2, 2, H])
    t.wo_c = sb("wo_c", [P, 2, D])
    t.dense0 = sb("dense0", [P, P])
    t.dense1 = sb("dense1", [P, P])
    t.dense2 = sb("dense2", [P, P])
    t.cheb_c = sb("cheb_c", [P, D])
    t.lin = sb("lin", [D, D])
    t.dense3 = sb("dense3", [P, P])
    t.out3 = sb("out3", [P, P])
    t.center2 = sb("center2", [P, P])
    t.rows = sb("rows", [1, 4, 2 * D])
    t.gamma1 = sb("gamma1", [P, D])
    t.beta1 = sb("beta1", [P, D])
    t.gb3 = sb("gb3", [P, 2])
    t.eps1 = sb("eps1", [P, 1])
    with ExitStack() as c2:
        def tmp(name, shape):
            return c2.enter_context(nc.sbuf_tensor(name, shape, F32))

        def sem(name):
            return c2.enter_context(semaphore(nc, name))

        stack = tmp("w_stack", [P, 8, D])
        wo = tmp("wo_raw", [P, 2, D])
        wo4 = tmp("wo_heads", [P, H, D])
        rel = tmp("rel", [R // 2, 2, D])
        relt = tmp("relt", [D, R])
        th = tmp("rel_tanh", [P, 2, R])
        mean = tmp("w_mean", [P, 16])
        brow = tmp("b_raw", [1, 4, 2 * D])
        ps = c2.enter_context(nc.psum_tensor("w_ps", [P, 4, 512], F32))
        cleared, loaded, chain, pe_done, act_done = sem("w_cleared"), sem("w_loaded"), sem("w_chain"), sem("w_pe"), sem("w_act")
        block = c2.enter_context(nc.Block())

        loads = [(t.w_ht[0:D, :], w["L0_gnn_W_h"]), (t.w_ht[D:P, :], w["L0_gnn_W_t"]), (t.w_r[:], w["L0_gnn_W_r"]),
                 (wo[:], w["L0_gnn_W_o"].rearrange("(c p) d -> p c d", p=P)),
                 (rel[:], w["L0_gnn_relation_embed"].rearrange("(c p) d -> p c d", c=2)),
                 (t.lin[:], w["L3_gnn_W_lin_T"]),
                 (t.gamma1[:], w["L1_gnn_gamma"].partition_broadcast(P)), (t.beta1[:], w["L1_gnn_beta"].partition_broadcast(P)),
                 (t.eps1[:], w["L3_gnn_eps"].partition_broadcast(P)),
                 (t.cheb_c[0:D, :], w["L2_gnn_W"][1]), (t.cheb_c[D:P, :], w["L2_gnn_W"][2])]
        for h in (0, 1):
            half = slice(h * D, (h + 1) * D)
            loads.append((wo4[half], w["L0_gnn_W_o"].rearrange("(h k) d -> k h d", h=H)))
            for n, a in enumerate((w["L1_gnn_W"], w["L2_gnn_W"][0], w["L2_gnn_W"][2], w["L3_gnn_W1_T"], w["L3_gnn_W2_T"])):
                loads.append((stack[half, n, :], a))
            for n, a in enumerate((w["L1_gnn_b"], w["L2_gnn_bias"], w["L3_gnn_b_lin"])):
                loads.append((brow[0:1, n, half], a))
            for n, a in enumerate((w["L3_gnn_gamma"], w["L3_gnn_beta"])):
                loads.append((t.gb3[half, n:n + 1], a.rearrange("o d -> d o")))
            for n, a in enumerate((w["L0_gnn_att_h"], w["L0_gnn_att_t"], w["L0_gnn_att_r"])):
                for m in range(2):
                    hh = 2 * m + h
                    loads.append((t.att[half, n, m, hh:hh + 1], a[hh:hh + 1, :].rearrange("o d -> d o")))

        @block.sync
        def _(sp):
            sp.wait_ge(cleared, 1)
            for dst, src in loads:
                sp.dma_start(dst, src, allow_slow_non_contiguous=True).then_inc(loaded, 16)

        @block.vector
        def _(dve):
            for a in (t.dense0, t.dense1, t.dense2, t.dense3, t.out3, t.center2, t.rows):
                nc.vector.memset(a[:], 0.0)
            nc.vector.memset(t.att[:], 0.0).then_inc(cleared, 1)
            dve.wait_ge(cleared, 1)
            dve.wait_ge(loaded, 16 * len(loads))
            c = Chain(dve, chain)
            c.link(nc.vector.tensor_scalar(t.eps1[:], t.eps1[:], 1.0, None, ALU.add))
            eye = stack[:, 5, :]
            c.link(nc.vector.tensor_copy(eye[0:D], t.ident[0:D, 0:D]))
            c.link(nc.vector.tensor_copy(eye[D:P], t.ident[D:P, D:P]))
            c.link(nc.vector.tensor_tensor(wo4[:, 0:2], wo4[:, 0:2], wo4[:, 2:4], ALU.add))
            c.link(nc.vector.tensor_tensor(wo4[:, 0], wo4[:, 0], wo4[:, 1], ALU.add))
            c.link(nc.vector.scalar_tensor_tensor(stack[:, 6, :], wo4[:, 0], 0.1, eye, ALU.mult, ALU.add))
            c.link(nc.vector.tensor_tensor(stack[:, 7, :], stack[:, 1, :], stack[:, 2, :], ALU.subtract))
            c.link(nc.vector.tensor_tensor(stack[:, 7, :], stack[:, 7, :], eye, ALU.add))

            def centred(dst, src, parts=P):
                n = c.n % 16
                c.link(nc.vector.tensor_reduce(mean[0:parts, n:n + 1], src, AX.X, ALU.add))
                c.link(nc.vector.tensor_scalar(mean[0:parts, n:n + 1], mean[0:parts, n:n + 1], 1.0 / D, None, ALU.mult))
                for a, b, p in dst:
                    c.link(nc.vector.tensor_scalar(a, b, mean[p, n:n + 1], None, ALU.subtract))

            up, down = slice(0, D), slice(D, P)

            def diagonal(big, s):
                return [(big[up, 0:D], stack[up, s, :], up), (big[down, D:P], stack[down, s, :], down)]

            centred(diagonal(t.dense0, 6), stack[:, 6, :])
            centred(diagonal(t.dense1, 0), stack[:, 0, :])
            centred(diagonal(t.dense2, 7), stack[:, 7, :])
            centred(diagonal(t.out3, 4), stack[:, 4, :])
            centred(diagonal(t.center2, 5), eye)
            c.link(nc.vector.tensor_copy(t.dense3[up, 0:D], stack[up, 3, :]))
            c.link(nc.vector.tensor_copy(t.dense3[down, D:P], stack[down, 3, :]))
            for m in range(2):
                centred([(t.wo_c[:, m, :], wo[:, m, :], slice(0, P))], wo[:, m, :])
            centred([(t.cheb_c[:], t.cheb_c[:], slice(0, P))], t.cheb_c[:])
            for n in range(2):
                for h in (0, 1):
                    centred([(t.rows[0:1, n, h * D:(h + 1) * D], brow[0:1, n, h * D:(h + 1) * D], slice(0, 1))],
                            brow[0:1, n, h * D:(h + 1) * D], 1)
            c.link(nc.vector.tensor_copy(t.rows[0:1, 2, :], brow[0:1, 2, :]))
            dve.wait_ge(pe_done, 1)
            nc.vector.tensor_copy(relt[:], ps[0:D, 0, 0:R]).then_inc(pe_done, 1)
            dve.wait_ge(pe_done, 4)
            for m in range(2):
                ins = nc.vector.tensor_copy(t.rel_score[:, m, :], ps[0:R // 2, 3, m * H:(m + 1) * H])

        @block.tensor
        def _(pe):
            pe.wait_ge(loaded, 16 * len(loads))
            for m in range(2):
                ins = nc.tensor.transpose(ps[0:D, 0, m * 100:(m + 1) * 100], rel[:, m, :], t.ident[0:R // 2, 0:R // 2])
            ins.then_inc(pe_done, 1)
            pe.wait_ge(pe_done, 2)
            for m in range(2):
                ins = nc.tensor.matmul(ps[:, 1 + m, 0:R], t.w_r[:, m * P:(m + 1) * P], relt[:], start=True, stop=True)
            ins.then_inc(pe_done, 1)
            pe.wait_ge(act_done, 1)
            for r in range(2):
                for m in range(2):
                    ins = nc.tensor.matmul(ps[0:R // 2, 3, r * H:(r + 1) * H], th[:, m, r * 100:(r + 1) * 100],
                                           t.att[:, 2, m, :], start=m == 0, stop=m == 1, skip_group_check=True)
            ins.then_inc(pe_done, 1)

        @block.scalar
        def _(act):
            act.wait_ge(pe_done, 3)
            for m in range(2):
                ins = nc.scalar.activation(th[:, m, :], ps[:, 1 + m, 0:R], ACT.Tanh)
            ins.then_inc(act_done, 1)


def edge_scores(nc, t, x):
    with ExitStack() as ctx:
        def sb(name, shape, dt=F32):
            return ctx.enter_context(nc.sbuf_tensor("sc_" + name, shape, dt))

        def sem(name):
            return ctx.enter_context(semaphore(nc, "sc_" + name))

        def sems(name):
            return [sem(name + str(u)) for u in range(2)]

        idx = sb("idx", [P, 2, 2, CT], I32)
        got = sb("got", [P, 2, CT, 2, D])
        xt = sb("xt", [P, 2, CH])
        th = sb("tanh", [P, 2, CH])
        types = sb("types", [R // 2, 2, CH])
        relid = sb("relid", [R // 2, 2])
        relid_i = sb("relid_i", [R // 2, 2], I32)
        oh = sb("relhot", [R // 2, 2, 2, CH])
        raw = sb("raw", [H, 2, CH])
        leaky = sb("leaky", [H, 2, CH])
        psx = ctx.enter_context(nc.psum_tensor("sc_psx", [P, 2, 512], F32))
        psz = ctx.enter_context(nc.psum_tensor("sc_psz", [P, 2, 2, 512], F32))
        pss = ctx.enter_context(nc.psum_tensor("sc_pss", [P, 2, 512], F32))
        idx_ready, gathered, turned, xt_ready = sems("idx_ready"), sems("gathered"), sems("turned"), sems("xt_ready")
        z_ready, tanh_ready, tanh_used = sems("z_ready"), sems("tanh_ready"), sems("tanh_used")
        types_in, hot, summed, raw_ready = sems("types_in"), sems("hot"), sems("summed"), sems("raw_ready")
        leaky_ready, stored, kept, passed = sems("leaky_ready"), sems("stored"), sems("kept"), sem("passed")
        ids, sp_passed = sem("ids"), sem("sp_passed")
        block = ctx.enter_context(nc.Block())
        parts = ((0, 512), (512, CH))

        @block.gpsimd
        def _(pool):
            nc.gpsimd.iota(relid_i[:], [[R // 2, 2]], base=0, channel_multiplier=1).then_inc(ids, 1)
            @repeat(pool, PAIRS)
            def _(i):
                for u in range(2):
                    pool.wait_ge(idx_ready[u], i + 1)
                    wait(pool, turned[u], i)
                    wait(pool, kept[u], i * 16)
                    pool.sem_inc(passed, 1)
                    for c in range(CT):
                        for g in range(2):
                            pool.indirect_dma_start(out=got[:, u, c, g, :], out_offset=None, in_=x,
                                                    in_offset=bass.IndirectOffsetOnAxis(idx[:, u, g, c:c + 1], 0)
                                                    ).then_inc(gathered[u], 16)

        @block.sync
        def _(sp):
            @repeat(sp, PAIRS)
            def _(i):
                for u in range(2):
                    wait(sp, hot[u], i)
                    sp.sem_inc(sp_passed, 1)
                    sp.dma_start(types[:, u, :], t.row_s[3:4, bass.ds((i * 2 + u) * CH, CH)].partition_broadcast(R // 2)
                                 .rearrange("q o e -> q (o e)")).then_inc(types_in[u], 16)
                for u in range(2):
                    sp.wait_ge(gathered[u], (i + 1) * 32 * CT)
                    sp.sem_inc(sp_passed, 1)
                    sp.dma_start(t.x_dst[bass.ds(i * 2 + u, 1)].rearrange("o p (c d) -> p (o c) d", c=CT),
                                 got[:, u, :, 1, :]).then_inc(kept[u], 16)
                    sp.wait_ge(leaky_ready[u], i + 1)
                    sp.sem_inc(sp_passed, 1)
                    sp.dma_start(t.scores[:, bass.ds((i * 2 + u) * CH, CH)], leaky[:, u, :]).then_inc(stored[u], 16)
            for u in range(2):
                sp.wait_ge(stored[u], PAIRS * 16)
                sp.wait_ge(kept[u], PAIRS * 16)

        @block.scalar
        def _(act):
            def indices(u, at):
                nc.scalar.copy(idx[:, u, 0, :], t.s_col[:, at])
                nc.scalar.copy(idx[:, u, 1, :], t.t_col[:, at]).then_inc(idx_ready[u], 1)

            for u in range(2):
                indices(u, slice(u * CT, (u + 1) * CT))
            @repeat(act, PAIRS)
            def _(i):
                for u in range(2):
                    act.wait_ge(gathered[u], (i + 1) * 32 * CT)
                    indices(u, bass.ds((i * 2 + 2 + u) * CT, CT))
                    for q in range(4):
                        z, n = q % 2, (i * 2 + u) * 2 + q // 2
                        act.wait_ge(z_ready[z], n + 1)
                        act.wait_ge(tanh_used[z], n)
                        for b, (lo, hi) in enumerate(parts):
                            ins = nc.scalar.activation(th[:, z, lo:hi], psz[:, z, b, 0:hi - lo], ACT.Tanh)
                        ins.then_inc(tanh_ready[z], 1)
                    act.wait_ge(summed[u], i + 1)
                    wait(act, leaky_ready[u], i)
                    for b, (lo, hi) in enumerate(parts):
                        ins = nc.scalar.copy(raw[:, u, lo:hi], pss[0:H, b, 0:hi - lo])
                    ins.then_inc(raw_ready[u], 1)

        @block.vector
        def _(dve):
            dve.wait_ge(ids, 1)
            nc.vector.tensor_copy(relid[:], relid_i[:]).then_inc(ids, 1)
            dve.wait_ge(ids, 2)
            @repeat(dve, PAIRS)
            def _(i):
                for u in range(2):
                    dve.wait_ge(turned[u], i + 1)
                    wait(dve, summed[u], i)
                    for b, (lo, hi) in enumerate(parts):
                        ins = nc.vector.tensor_copy(xt[:, u, lo:hi], psx[:, b, 0:hi - lo])
                    ins.then_inc(xt_ready[u], 1)
                    dve.wait_ge(types_in[u], (i + 1) * 16)
                    for r in range(2):
                        ins = nc.vector.tensor_scalar(oh[:, u, r, :], types[:, u, :], relid[:, r:r + 1], None, ALU.is_equal)
                    ins.then_inc(hot[u], 1)
                    dve.wait_ge(raw_ready[u], i + 1)
                    wait(dve, stored[u], i * 16)
                    nc.vector.scalar_tensor_tensor(leaky[:, u, :], raw[:, u, :], 0.01, raw[:, u, :],
                                                   ALU.mult, ALU.max).then_inc(leaky_ready[u], 1)

        @block.tensor
        def _(pe):
            @repeat(pe, PAIRS)
            def _(i):
                for u in range(2):
                    pe.wait_ge(gathered[u], (i + 1) * 32 * CT)
                    wait(pe, xt_ready[1 - u], i + u)
                    for c in range(CT):
                        ins = nc.tensor.transpose(psx[:, c // 4, c % 4 * P:(c % 4 + 1) * P],
                                                  got[:, u, c].rearrange("p g d -> p (g d)"), t.ident[:])
                    ins.then_inc(turned[u], 1)
                    pe.wait_ge(xt_ready[u], i + 1)

                    def project(q):
                        g, m, z = q // 2, q % 2, q % 2
                        half = slice(g * D, (g + 1) * D)
                        wait(pe, tanh_ready[z], (i * 2 + u) * 2 + q // 2)
                        for b, (lo, hi) in enumerate(parts):
                            ins = nc.tensor.matmul(psz[:, z, b, 0:hi - lo], t.w_ht[half, m * P:(m + 1) * P],
                                                   xt[half, u, lo:hi], start=True, stop=True)
                        ins.then_inc(z_ready[z], 1)

                    def score(q):
                        g, m, z = q // 2, q % 2, q % 2
                        pe.wait_ge(tanh_ready[z], (i * 2 + u) * 2 + q // 2 + 1)
                        if q == 0:
                            wait(pe, raw_ready[1 - u], i + u)
                        for b, (lo, hi) in enumerate(parts):
                            ins = nc.tensor.matmul(pss[0:H, b, 0:hi - lo], t.att[:, g, m, :], th[:, z, lo:hi],
                                                   start=q == 0, stop=False, skip_group_check=True)
                        ins.then_inc(tanh_used[z], 1)

                    project(0)
                    project(1)
                    score(0)
                    project(2)
                    score(1)
                    project(3)
                    score(2)
                    score(3)
                    pe.wait_ge(hot[u], i + 1)
                    for b, (lo, hi) in enumerate(parts):
                        for r in range(2):
                            ins = nc.tensor.matmul(pss[0:H, b, 0:hi - lo], t.rel_score[:, r, :], oh[:, u, r, lo:hi],
                                                   start=False, stop=r == 1, skip_group_check=True)
                    ins.then_inc(summed[u], 1)


def edge_softmax(nc, t):
    with ExitStack() as ctx:
        def sb(name, shape, dt=F32):
            return ctx.enter_context(nc.sbuf_tensor("sm_" + name, shape, dt))

        s = sb("scores", [P, H, TILES])
        up = sb("up", [P, H, TILES])
        pick = sb("pick", [P, H, TILES])
        tot = sb("total", [P, H, TILES])
        e = sb("exp", [P, H, TILES])
        goes_on = sb("goes_on", [P, TILES])
        penalty = sb("penalty", [P, TILES])

        def each(a):
            return [a[:, h, :] for h in range(H)]

        last = t.last_s[:].unsqueeze(1).to_broadcast([P, H, TILES])
        with ExitStack() as c2:
            loaded = c2.enter_context(semaphore(nc, "sm_loaded"))
            block = c2.enter_context(nc.Block())

            @block.sync
            def _(sp):
                sp.dma_start(s[:], t.scores.rearrange("h (p j) -> p h j", p=P)).then_inc(loaded, 16)
                sp.wait_ge(loaded, 16)

            @block.vector
            def _(dve):
                nc.vector.tensor_scalar(goes_on[:], t.last_s[:], -1.0, 1.0, ALU.mult, ALU.add)
                nc.vector.tensor_scalar(penalty[:], t.same_s[:], -1.0, 1e30, ALU.add, ALU.mult)
        segment_scan(nc, t, "max_up", penalty[:], each(s), each(up), reverse=False, biggest=True)
        with nc.Block() as block:
            @block.vector
            def _(dve):
                nc.vector.tensor_tensor(pick[:], up[:], last, ALU.mult)
        segment_scan(nc, t, "max_down", goes_on[:], each(pick), each(tot), reverse=True)
        with ExitStack() as c2:
            ready = c2.enter_context(semaphore(nc, "sm_ready"))
            block = c2.enter_context(nc.Block())

            @block.vector
            def _(dve):
                nc.vector.tensor_tensor(s[:], s[:], tot[:], ALU.subtract).then_inc(ready, 1)

            @block.scalar
            def _(act):
                act.wait_ge(ready, 1)
                nc.scalar.activation(e[:], s[:], ACT.Exp)
        segment_scan(nc, t, "sum_up", t.same_s[:], each(e), each(up), reverse=False)
        with nc.Block() as block:
            @block.vector
            def _(dve):
                nc.vector.tensor_tensor(pick[:], up[:], last, ALU.mult)
        segment_scan(nc, t, "sum_down", goes_on[:], each(pick), each(tot), reverse=True)
        with ExitStack() as c2:
            chain = c2.enter_context(semaphore(nc, "sm_chain"))
            stored = c2.enter_context(semaphore(nc, "sm_stored"))
            block = c2.enter_context(nc.Block())

            @block.vector
            def _(dve):
                c = Chain(dve, chain)
                c.link(nc.vector.tensor_scalar(tot[:], tot[:], 1e-16, None, ALU.add))
                c.link(nc.vector.reciprocal(tot[:], tot[:]))
                c.link(nc.vector.scalar_tensor_tensor(tot[:], e[:], 0.9, tot[:], ALU.mult, ALU.mult))

            @block.sync
            def _(sp):
                sp.wait_ge(chain, 3)
                sp.dma_start(t.row_s[6:10].rearrange("h (p j) -> p h j", p=P), tot[:]).then_inc(stored, 16)
                sp.wait_ge(stored, 16)
    to_tiles(nc, t, "att_cols", [t.row_s[6 + h] for h in range(H)], [t.att_col[:, :, h] for h in range(H)])


def edge_pass(nc, t, name, kind, eq, table=None, idx=None, put=None, target=None):
    heads = kind in ("heads", "heads_out")
    W = H * D if heads else D
    G = table.shape[1] if table is not None else 0
    O = target.shape[1]
    turned = kind in ("heads_out", "cheb2")
    C = {"heads_out": 2, "cheb2": 1}.get(kind, 0)
    M = C * P if turned else W
    nodes = put is not None
    side = t.x_dst if heads else t.cheb_msg if kind == "cheb2" else None
    own_msg = kind != "plain"
    wide = kind == "heads"
    with ExitStack() as ctx:
        def sb(n, shape, dt=F32):
            return ctx.enter_context(nc.sbuf_tensor(f"{name}_{n}", shape, dt))

        def sem(n):
            return ctx.enter_context(semaphore(nc, f"{name}_{n}"))

        def sems(n):
            return [sem(n + str(u)) for u in range(2)]

        def psum(n, shape):
            return ctx.enter_context(nc.psum_tensor(f"{name}_{n}", shape, F32))

        eqs = sb("eq", [P, 2, CT, P])
        out = sb("out", [P, 2, CT, O])
        msg = sb("msg", [P, 2, CT, M]) if own_msg else None
        if table is not None:
            gidx = sb("gather_idx", [P, 2, CT], I32)
            got = sb("got", [P, 2, CT, G])
        if nodes:
            pidx = sb("put_idx", [P, 2, CT], I32)
        if side is not None:
            sides = sb("side", [P, 2, CT, D])
        if turned:
            rt = sb("rt", [P, C, CH])
            ps_rt = psum("ps_rt", [P, C, 2, 512])
        if kind == "gin":
            gt = sb("gt", [D + 1, 2, CH])
            lin = sb("lin", [D + 1, D])
            ps_gt = psum("ps_gt", [P, 2, 512])
            ps_lin = psum("ps_lin", [P, 512])
        ps_o = psum("ps_out", [P, 2, 4 if wide else 1, 512])

        idx_ready, gathered, msg_ready = sems("idx_ready"), sems("gathered"), sems("msg_ready")
        eq_in, side_in, summed, out_ready = sems("eq_in"), sems("side_in"), sems("summed"), sems("out_ready")
        stored, lasts_stored, msg_kept = sems("stored"), sems("lasts_stored"), sems("msg_kept")
        put_ready, added = sems("put_ready"), sem("added")
        rt_done, rt_read, gt_done, gt_read, lin_done = sem("rt_done"), sem("rt_read"), sem("gt_done"), sem("gt_read"), sem("lin_done")
        pool_passed, sp_passed, pe_passed, setup = sem("pool_passed"), sem("sp_passed"), sem("pe_passed"), sem("setup")
        block = ctx.enter_context(nc.Block())
        rows_of = {u: [out[:, u, c, :] for c in range(CT)] for u in range(2)}
        used = summed if not turned else rt_done
        parts = ((0, 512), (512, CH))

        def used_up(i, u):
            return (rt_done, i * 2 + u) if turned else (summed[u], i)

        @block.gpsimd
        def _(pool):
            def gather(i, u):
                pool.wait_ge(idx_ready[u], i + 1)
                if own_msg:
                    wait(pool, msg_ready[u] if kind != "gin" else lin_done, i if kind != "gin" else i * 2 + u)
                else:
                    wait(pool, summed[u], i)
                pool.sem_inc(pool_passed, 1)
                for c in range(CT):
                    pool.indirect_dma_start(out=got[:, u, c, :], out_offset=None, in_=table,
                                            in_offset=bass.IndirectOffsetOnAxis(gidx[:, u, c:c + 1], 0)
                                            ).then_inc(gathered[u], 16)

            def scatter(i, u):
                pool.wait_ge(put_ready[u], i + 1)
                pool.wait_ge(out_ready[u], i + 1)
                pool.sem_inc(pool_passed, 1)
                for c in range(CT):
                    pool.indirect_dma_start(out=target, out_offset=bass.IndirectOffsetOnAxis(pidx[:, u, c:c + 1], 0),
                                            in_=rows_of[u][c], in_offset=None, bounds_check=NP - 1,
                                            oob_is_err=False).then_inc(stored[u], 16)

            def step(i, more):
                gather(i, 1)
                if nodes:
                    scatter(i, 0)
                if more:
                    gather(i + 1, 0)
                if nodes:
                    scatter(i, 1)

            if table is not None:
                gather(0, 0)

                @repeat(pool, PAIRS - 1)
                def _(i):
                    step(i, True)
                step(PAIRS - 1, False)
            if nodes:
                for u in range(2):
                    pool.wait_ge(stored[u], PAIRS * 16 * CT)

        @block.sync
        def _(sp):
            @repeat(sp, PAIRS)
            def _(i):
                for u in range(2):
                    at = bass.ds(i * 2 + u, 1)
                    wait(sp, *used_up(i, u))
                    sp.sem_inc(sp_passed, 1)
                    sp.dma_start(eqs[:, u].rearrange("p c e -> p (c e)"), eq[at].rearrange("o p e -> p (o e)")).then_inc(eq_in[u], 16)
                    if side is not None:
                        wait(sp, msg_ready[u], i)
                        sp.sem_inc(sp_passed, 1)
                        sp.dma_start(sides[:, u].rearrange("p c d -> p (c d)"), side[at].rearrange("o p e -> p (o e)")).then_inc(side_in[u], 16)

        def out_waits(eng, i, u):
            wait(eng, stored[u], i * 16 * (CT if nodes else 1))
            if nodes:
                wait(eng, lasts_stored[u], i * 16)

        @block.vector
        def _(dve):
            if kind == "gin":
                nc.vector.memset(gt[:], 1.0)
                nc.vector.tensor_copy(lin[0:D, :], t.lin[:]).then_inc(setup, 1)
                dve.wait_ge(setup, 17)
            @repeat(dve, PAIRS)
            def _(i):
                for u in range(2):
                    at = bass.ds((i * 2 + u) * CT, CT)
                    if table is not None:
                        dve.wait_ge(gathered[u], (i + 1) * 16 * CT)
                    if side is not None:
                        dve.wait_ge(side_in[u], (i + 1) * 16)
                    if own_msg and kind != "gin":
                        wait(dve, *used_up(i, u))
                    if heads:
                        def four(a):
                            return a.unsqueeze(2).to_broadcast([P, CT, H, D])

                        att = t.att_col[:, at, :].unsqueeze(3).to_broadcast([P, CT, H, D])
                        m = msg[:, u].rearrange("p c (h d) -> p c h d", h=H)
                        if table is None:
                            nc.vector.tensor_tensor(m, four(sides[:, u]), att, ALU.mult).then_inc(msg_ready[u], 1)
                        else:
                            g = got[:, u].rearrange("p c (h d) -> p c h d", h=H)
                            nc.vector.tensor_scalar(sides[:, u], sides[:, u], 0.1, None, ALU.mult).then_inc(added, 1)
                            dve.wait_ge(added, (i * 2 + u) * 2 + 1)
                            nc.vector.tensor_tensor(g, four(sides[:, u]), g, ALU.add).then_inc(added, 1)
                            wait(dve, added, (i * 2 + u) * 2 + 2)
                            nc.vector.tensor_tensor(m, g, att, ALU.mult).then_inc(msg_ready[u], 1)
                    if kind == "cheb1":
                        wait(dve, msg_kept[u], i * 16)
                        nc.vector.tensor_tensor(msg[:, u], got[:, u], t.w_col[:, at].unsqueeze(2).to_broadcast([P, CT, D]),
                                                ALU.mult).then_inc(msg_ready[u], 1)
                    if kind == "cheb2":
                        nc.vector.tensor_copy(msg[:, u, :, 0:D], sides[:, u])
                        nc.vector.scalar_tensor_tensor(msg[:, u, :, D:P], got[:, u], 2.0,
                                                       t.w_col[:, at].unsqueeze(2).to_broadcast([P, CT, D]),
                                                       ALU.mult, ALU.mult).then_inc(msg_ready[u], 1)
                    if kind == "gin":
                        dve.wait_ge(gt_done, i * 2 + u + 1)
                        wait(dve, lin_done, i * 2)
                        for b, (lo, hi) in enumerate(parts):
                            ins = nc.vector.tensor_copy(gt[0:D, u, lo:hi], ps_gt[0:D, b, 0:hi - lo])
                        ins.then_inc(gt_read, 1)
                    if not wide:
                        dve.wait_ge(summed[u], i + 1)
                        out_waits(dve, i, u)
                        sums = ps_o[:, u, 0, 0:CT * D].rearrange("p (c d) -> p c d", c=CT)
                        if kind in ("cheb1", "cheb2"):
                            col = t.negdinv2_col if kind == "cheb1" else t.negdinv_col
                            nc.vector.tensor_tensor(out[:, u, :, 0:D], sums, col[:, at].unsqueeze(2).to_broadcast([P, CT, D]),
                                                    ALU.mult).then_inc(out_ready[u], 1)
                        else:
                            if O > D:
                                nc.vector.tensor_copy(out[:, u, :, D], t.deg_col[:, at])
                            nc.vector.tensor_copy(out[:, u, :, 0:D], sums).then_inc(out_ready[u], 1)

        @block.scalar
        def _(act):
            if kind == "gin":
                act.dma_start(lin[D:D + 1, :], t.b_lin).then_inc(setup, 16)
            if table is not None:
                for u in range(2):
                    nc.scalar.copy(gidx[:, u], idx[:, u * CT:(u + 1) * CT]).then_inc(idx_ready[u], 1)
            @repeat(act, PAIRS)
            def _(i):
                for u in range(2):
                    at = bass.ds((i * 2 + u) * CT, CT)
                    if table is not None:
                        act.wait_ge(gathered[u], (i + 1) * 16 * CT)
                        nc.scalar.copy(gidx[:, u], idx[:, bass.ds((i * 2 + 2 + u) * CT, CT)]).then_inc(idx_ready[u], 1)
                    if nodes:
                        wait(act, stored[u], i * 16 * CT)
                        nc.scalar.copy(pidx[:, u], put[:, at]).then_inc(put_ready[u], 1)
                    if kind == "cheb1":
                        act.wait_ge(msg_ready[u], i + 1)
                        act.dma_start(t.cheb_msg[bass.ds(i * 2 + u, 1)].rearrange("o p e -> p (o e)"),
                                      msg[:, u].rearrange("p c d -> p (c d)")).then_inc(msg_kept[u], 16)
                    if kind == "gin":
                        act.wait_ge(lin_done, i * 2 + u + 1)
                        wait(act, summed[u], i)
                        nc.scalar.activation(msg[:, u].rearrange("p c d -> p (c d)"), ps_lin[:, 0:CT * D],
                                             ACT.Relu).then_inc(msg_ready[u], 1)
                    if turned:
                        act.wait_ge(rt_done, i * 2 + u + 1)
                        wait(act, summed[1 - u], i + u)
                        for m in range(C):
                            for b, (lo, hi) in enumerate(parts):
                                ins = nc.scalar.copy(rt[:, m, lo:hi], ps_rt[:, m, b, 0:hi - lo])
                        ins.then_inc(rt_read, 1)
                    if wide:
                        act.wait_ge(summed[u], i + 1)
                        out_waits(act, i, u)
                        nc.scalar.copy(out[:, u].rearrange("p c w -> p (c w)"),
                                       ps_o[:, u].rearrange("p b w -> p (b w)")[:, 0:CT * W]).then_inc(out_ready[u], 1)
                    act.wait_ge(out_ready[u], i + 1)
                    if nodes:
                        act.dma_start(t.lasts[at, :].rearrange("(o c) w -> o c w", o=1)[:, :, 0:D], out[P - 1:P, u, :, 0:D]).then_inc(lasts_stored[u], 16)
                    else:
                        act.dma_start(target[bass.ds((i * 2 + u) * CH, CH), :].rearrange("(c p) w -> p c w", p=P),
                                      out[:, u]).then_inc(stored[u], 16)
            for u in range(2):
                if nodes:
                    act.wait_ge(lasts_stored[u], PAIRS * 16)
                else:
                    act.wait_ge(stored[u], PAIRS * 16)
                if kind == "cheb1":
                    act.wait_ge(msg_kept[u], PAIRS * 16)

        @block.tensor
        def _(pe):
            if kind == "gin":
                pe.wait_ge(setup, 17)
            @repeat(pe, PAIRS)
            def _(i):
                for u in range(2):
                    if kind == "gin":
                        pe.wait_ge(gathered[u], (i + 1) * 16 * CT)
                        wait(pe, gt_read, i * 2 + u)
                        pe.sem_inc(pe_passed, 1)
                        for c in range(CT):
                            ins = nc.tensor.transpose(ps_gt[0:D, c // 4, c % 4 * P:(c % 4 + 1) * P], got[:, u, c, :], t.ident[:])
                        ins.then_inc(gt_done, 1)
                        pe.wait_ge(gt_read, i * 2 + u + 1)
                        wait(pe, msg_ready[1 - u], i + u)
                        for c in range(CT):
                            ins = nc.tensor.matmul(ps_lin[:, c * D:(c + 1) * D], gt[:, u, c * P:(c + 1) * P], lin[:],
                                                   start=True, stop=True)
                        ins.then_inc(lin_done, 1)
                    if own_msg:
                        pe.wait_ge(msg_ready[u], i + 1)
                    else:
                        pe.wait_ge(gathered[u], (i + 1) * 16 * CT)
                    pe.wait_ge(eq_in[u], (i + 1) * 16)
                    src = msg if own_msg else got
                    if turned:
                        wait(pe, rt_read, i * 2 + u)
                        for m in range(C):
                            for c in range(CT):
                                ins = nc.tensor.matmul(ps_rt[:, m, c // 4, c % 4 * P:(c % 4 + 1) * P],
                                                       src[:, u, c, m * P:(m + 1) * P], eqs[:, u, c, :], start=True, stop=True)
                        ins.then_inc(rt_done, 1)
                        pe.wait_ge(rt_read, i * 2 + u + 1)
                        wait(pe, out_ready[u], i)
                        wts = t.wo_c if kind == "heads_out" else None
                        for c in range(CT):
                            for m in range(C):
                                rhs = t.wo_c[:, m, :] if kind == "heads_out" else t.cheb_c[:]
                                ins = nc.tensor.matmul(ps_o[:, u, 0, c * D:(c + 1) * D], rt[:, m, c * P:(c + 1) * P], rhs,
                                                       start=m == 0, stop=m == C - 1, skip_group_check=True)
                        ins.then_inc(summed[u], 1)
                    else:
                        wait(pe, out_ready[u], i)
                        flat = ps_o[:, u].rearrange("p b w -> p (b w)")
                        for c in range(CT):
                            ins = nc.tensor.matmul(flat[:, c * W:(c + 1) * W], eqs[:, u, c, :], src[:, u, c, :], start=True, stop=True)
                        ins.then_inc(summed[u], 1)


def carry_spans(nc, t, name, span, lasts, width, target, rows):
    W = target.shape[1]
    with ExitStack() as ctx:
        ends = ctx.enter_context(nc.sbuf_tensor(f"{name}_ends", [Q, 4, width], F32))
        add = ctx.enter_context(nc.sbuf_tensor(f"{name}_add", [Q, 4, W], F32))
        ps = ctx.enter_context(nc.psum_tensor(f"{name}_ps", [P, 4, 512], F32))
        loaded = ctx.enter_context(semaphore(nc, f"{name}_loaded"))
        summed = ctx.enter_context(semaphore(nc, f"{name}_summed"))
        ready = ctx.enter_context(semaphore(nc, f"{name}_ready"))
        added = ctx.enter_context(semaphore(nc, f"{name}_added"))
        block = ctx.enter_context(nc.Block())

        @block.sync
        def _(sp):
            sp.dma_start(ends[:], lasts).then_inc(loaded, 16)

        @block.tensor
        def _(pe):
            pe.wait_ge(loaded, 16)
            for g in range(4):
                for e in range(g + 1):
                    ins = nc.tensor.matmul(ps[0:Q, g, 0:width], span[:, e, g * Q:(g + 1) * Q], ends[:, e, :],
                                           start=e == 0, stop=e == g)
                ins.then_inc(summed, 1)

        @block.vector
        def _(dve):
            if W > width:
                nc.vector.memset(add[:, :, width:], 0.0)
            for g in range(4):
                dve.wait_ge(summed, g + 1)
                nc.vector.tensor_copy(add[:, g, 0:width], ps[0:Q, g, 0:width]).then_inc(ready, 1)

        @block.gpsimd
        def _(pool):
            for g in range(4):
                pool.wait_ge(ready, g + 1)
                pool.indirect_dma_start(out=target, out_offset=bass.IndirectOffsetOnAxis(rows[:, g:g + 1], 0),
                                        in_=add[:, g, :], in_offset=None, compute_op=ALU.add).then_inc(added, 16)
            pool.wait_ge(added, 64)


def attention(nc, t):
    recycle(nc)
    tables = (t.edges_a, t.edges_b)

    def tile_ends(tab):
        return tab[0:EP, :].rearrange("(c q p) w -> p q c w", c=4, q=Q)[P - 1]

    edge_pass(nc, t, "hop0", "heads", t.eq_s, target=tables[0])
    carry_spans(nc, t, "carry0", t.span_s, tile_ends(tables[0]), H * D, tables[0], t.fix_edge)
    for k in range(1, 4):
        recycle(nc)
        a, b = tables[(k - 1) % 2], tables[k % 2]
        edge_pass(nc, t, f"hop{k}", "heads", t.eq_s, table=a, idx=t.next_col, target=b)
        carry_spans(nc, t, f"carry{k}", t.span_s, tile_ends(b), H * D, b, t.fix_edge)
    recycle(nc)
    edge_pass(nc, t, "hop4", "heads_out", t.eq_s, table=tables[1], idx=t.next_col, put=t.put_s, target=t.sum0)
    carry_spans(nc, t, "carry4", t.span_s, node_ends(t), D, t.sum0, t.fix_node_s)


def node_ends(t):
    return t.lasts.rearrange("(c q) w -> q c w", c=4)[:, :, 0:D]


T = 14
TD = T * D
STEPS = J // (2 * T)
EPS = 1e-5


def chunk(table, i, u, width=D):
    return table[0:NP, :].rearrange("(p j) w -> p j w", p=P)[:, bass.ds((i * 2 + u) * T, T), 0:width]


def per_node(col):
    return col.unsqueeze(2).to_broadcast([P, T, D])


def per_feature(row):
    return row.unsqueeze(1).to_broadcast([P, T, D])


def dense_pass(nc, t, name, kind, src, add, weight, outs, bias=None, x1=None):
    gathered_in = kind in ("round", "join")
    with ExitStack() as ctx:
        def sb(n, shape, dt=F32):
            return ctx.enter_context(nc.sbuf_tensor(f"{name}_{n}", shape, dt))

        def sems(n):
            return [ctx.enter_context(semaphore(nc, f"{name}_{n}{u}")) for u in range(2)]

        A = add.shape[1]
        in0 = sb("in0", [P, 2, T, D])
        in1 = sb("in1", [P, 2, T, A])
        g = sb("g", [P, 2, T, D]) if gathered_in else in0
        gt = sb("gt", [P, 2, TD])
        v = sb("v", [P, 2, T, D])
        sq = sb("sq", [P, 2, T, D])
        stat = sb("stat", [P, 2, 4, T])
        y = sb("y", [P, 2, T, D]) if kind != "round" else None
        second = sb("second", [P, 2, T, D]) if kind != "cheb" else None
        if bias is not None:
            brow, split, rest = sb("brow", [3, TD], BF16), sb("split", [3, 3, P], BF16), sb("rest", [3, 3, P])
            ones = sb("ones", [3, P], BF16)
            bias_chain = ctx.enter_context(semaphore(nc, f"{name}_bias_chain"))
        ps_t = ctx.enter_context(nc.psum_tensor(f"{name}_ps_t", [P, 2, 1024], F32))
        ps_v = ctx.enter_context(nc.psum_tensor(f"{name}_ps_v", [P, 2, 1024], F32))
        in0_ok, in1_ok, added, g_ready = sems("in0_ok"), sems("in1_ok"), sems("added"), sems("g_ready")
        turned, gt_ready, product = sems("turned"), sems("gt_ready"), sems("product")
        v_ready, sq_ready, summed, var_ready = sems("v_ready"), sems("sq_ready"), sems("summed"), sems("var_ready")
        root_ready, inv_ready, masked = sems("root_ready"), sems("inv_ready"), sems("masked")
        scaled, shifted, y_ready, second_ready = sems("scaled"), sems("shifted"), sems("y_ready"), sems("second_ready")
        y_stored, second_stored = sems("y_stored"), sems("second_stored")
        if kind == "join":
            in2 = sb("in2", [P, 2, T, D])
            r = sb("r", [P, 2, T, D])
            rsq = sb("rsq", [P, 2, T, D])
            rstat = sb("rstat", [P, 2, 6, T])
            in2_ok, r_added, r_total, r_mean, r_ready = (sems("in2_ok"), sems("r_added"), sems("r_total"), sems("r_mean"),
                                                         sems("r_ready"))
            rsq_ready, r_summed, r_var, r_root, r_inv = (sems("rsq_ready"), sems("r_summed"), sems("r_var"), sems("r_root"),
                                                         sems("r_inv"))
        bias_turned, bias_ok = (ctx.enter_context(semaphore(nc, f"{name}_{n}")) for n in ("bias_turned", "bias_ok"))
        sp_passed = ctx.enter_context(semaphore(nc, f"{name}_sp_passed"))
        block = ctx.enter_context(nc.Block())
        TURN, PROD, NORM, SHIFT, JOIN = (2, 3, 4, 5, 6) if gathered_in else (1, 2, 3, 4, None)
        deep = {"first": 5, "cheb": 5, "round": 7, "join": 9}[kind]

        @block.sync
        def _(sp):
            @skewed(sp, STEPS, deep)
            def _(ago):
                for i, u in ago(0):
                    if gathered_in:
                        wait(sp, added[u], i)
                    else:
                        wait(sp, turned[u], i)
                    sp.sem_inc(sp_passed, 1)
                    sp.dma_start(in0[:, u], chunk(src, i, u)).then_inc(in0_ok[u], 16)
                    if not gathered_in:
                        wait(sp, v_ready[u], i)
                        sp.sem_inc(sp_passed, 1)
                    sp.dma_start(in1[:, u], chunk(add, i, u, A)).then_inc(in1_ok[u], 16)
                if kind == "join":
                    for i, u in ago(SHIFT):
                        wait(sp, r_added[u], i)
                        sp.sem_inc(sp_passed, 1)
                        sp.dma_start(in2[:, u], chunk(x1, i, u)).then_inc(in2_ok[u], 16)
                for i, u in ago(deep):
                    if kind != "round":
                        sp.wait_ge(y_ready[u], i + 1)
                        sp.sem_inc(sp_passed, 1)
                        sp.dma_start(chunk(outs[0], i, u), y[:, u]).then_inc(y_stored[u], 16)
                    if kind != "cheb":
                        sp.wait_ge(second_ready[u], i + 1)
                        sp.sem_inc(sp_passed, 1)
                        sp.dma_start(chunk(outs[-1], i, u), second[:, u]).then_inc(second_stored[u], 16)
            for u in range(2):
                if kind != "round":
                    sp.wait_ge(y_stored[u], STEPS * 16)
                if kind != "cheb":
                    sp.wait_ge(second_stored[u], STEPS * 16)

        @block.gpsimd
        def _(pool):
            if kind == "cheb":
                return

            @skewed(pool, STEPS, SHIFT if kind != "join" else JOIN + 1)
            def _(ago):
                if kind != "round":
                    for i, u in ago(SHIFT if kind == "first" else JOIN + 1):
                        pool.wait_ge(y_ready[u], i + 1)
                        wait(pool, second_stored[u], i * 16)
                        col = (t.dis if kind == "first" else t.dinv)[:, bass.ds((i * 2 + u) * T, T)]
                        nc.gpsimd.tensor_tensor(second[:, u], y[:, u], per_node(col), ALU.mult).then_inc(second_ready[u], 1)
                if gathered_in:
                    for i, u in ago(SHIFT):
                        pool.wait_ge(scaled[u], i + 1)
                        nc.gpsimd.tensor_tensor(v[:, u], v[:, u], per_feature(t.beta1[:]), ALU.add).then_inc(shifted[u], 1)
                    for i, u in ago(0):
                        pool.wait_ge(in0_ok[u], (i + 1) * 16)
                        pool.wait_ge(in1_ok[u], (i + 1) * 16)
                        wait(pool, turned[u], i)
                        nc.gpsimd.tensor_tensor(g[:, u], in0[:, u], in1[:, u], ALU.add).then_inc(added[u], 1)

        @block.vector
        def _(dve):
            if bias is not None:
                c = Chain(dve, bias_chain)
                c.link(nc.vector.memset(ones[:], 1.0))
                dve.wait_ge(bias_turned, 1)
                c.link(nc.vector.tensor_copy(rest[:, 0, :], ps_t[0:3, 0, 0:P]))
                for k in range(3):
                    c.link(nc.vector.tensor_copy(split[:, k, :], rest[:, k, :]))
                    if k < 2:
                        c.link(nc.vector.tensor_tensor(rest[:, k + 1, :], rest[:, k, :], split[:, k, :], ALU.subtract))
                c.link(nc.vector.tensor_scalar(rest[:, 0, :], split[:, 0, :], t.ident[0:3, 0:1], None, ALU.mult))
                for k in (1, 2):
                    c.link(nc.vector.scalar_tensor_tensor(rest[:, k, :], split[:, k, :], t.ident[0:3, k:k + 1],
                                                          rest[:, k - 1, :], ALU.mult, ALU.add))
                for n in range(T // 2):
                    ins = nc.vector.tensor_copy(brow[:, n * P:(n + 1) * P], rest[:, 2, :])
                ins.then_inc(bias_ok, 1)

            @skewed(dve, STEPS, {"first": NORM, "cheb": NORM, "round": SHIFT, "join": JOIN}[kind])
            def _(ago):
                for i, u in ago(NORM):
                    dve.wait_ge(sq_ready[u], i + 1)
                    nc.vector.tensor_reduce(stat[:, u, 0, :], sq[:, u], AX.X, ALU.add).then_inc(summed[u], 1)
                    dve.wait_ge(summed[u], i + 1)
                    nc.vector.tensor_scalar(stat[:, u, 1, :], stat[:, u, 0, :], 1.0 / D, EPS, ALU.mult, ALU.add).then_inc(var_ready[u], 1)
                if kind == "join":
                    for i, u in ago(JOIN):
                        dve.wait_ge(rsq_ready[u], i + 1)
                        nc.vector.tensor_reduce(rstat[:, u, 0, :], rsq[:, u], AX.X, ALU.add).then_inc(r_summed[u], 1)
                        dve.wait_ge(r_summed[u], i + 1)
                        nc.vector.tensor_scalar(rstat[:, u, 1, :], rstat[:, u, 0, :], 1.0 / D, EPS, ALU.mult, ALU.add).then_inc(r_var[u], 1)
                if gathered_in:
                    for i, u in ago(1):
                        dve.wait_ge(added[u], i + 1)
                        nc.vector.tensor_tensor(g[:, u], g[:, u], per_node(t.dis[:, bass.ds((i * 2 + u) * T, T)]),
                                                ALU.mult).then_inc(g_ready[u], 1)
                else:
                    for i, u in ago(PROD):
                        dve.wait_ge(product[u], i + 1)
                        dve.wait_ge(in1_ok[u], (i + 1) * 16)
                        wait(dve, sq_ready[u], i)
                        if kind == "first":
                            nc.vector.tensor_copy(t.deg[:, bass.ds((i * 2 + u) * T, T)], in1[:, u, :, D])
                        nc.vector.tensor_tensor(v[:, u], ps_v[:, u, 0:TD].rearrange("p (t d) -> p t d", t=T),
                                                in1[:, u, :, 0:D], ALU.add).then_inc(v_ready[u], 1)
                for i, u in ago(NORM):
                    dve.wait_ge(root_ready[u], i + 1)
                    nc.vector.reciprocal(stat[:, u, 3, :], stat[:, u, 2, :]).then_inc(inv_ready[u], 1)
                    dve.wait_ge(inv_ready[u], i + 1)
                    if kind == "cheb":
                        nc.vector.tensor_tensor(stat[:, u, 3, :], stat[:, u, 3, :], t.real[:, bass.ds((i * 2 + u) * T, T)],
                                                ALU.mult).then_inc(masked[u], 1)
                        dve.wait_ge(masked[u], i + 1)
                    if gathered_in:
                        nc.vector.tensor_tensor(v[:, u], ps_v[:, u, 0:TD].rearrange("p (t d) -> p t d", t=T),
                                                per_node(stat[:, u, 3, :]), ALU.mult).then_inc(v_ready[u], 1)
                        dve.wait_ge(v_ready[u], i + 1)
                        nc.vector.tensor_tensor(v[:, u], v[:, u], per_feature(t.gamma1[:]), ALU.mult).then_inc(scaled[u], 1)
                    else:
                        wait(dve, y_stored[u], i * 16)
                        if kind == "first":
                            wait(dve, second_ready[u], i)
                        nc.vector.tensor_tensor(y[:, u], v[:, u], per_node(stat[:, u, 3, :]), ALU.mult).then_inc(y_ready[u], 1)
                if kind == "round":
                    for i, u in ago(SHIFT):
                        dve.wait_ge(shifted[u], i + 1)
                        wait(dve, second_stored[u], i * 16)
                        nc.vector.tensor_tensor(second[:, u], v[:, u], per_node(t.dis[:, bass.ds((i * 2 + u) * T, T)]),
                                                ALU.mult).then_inc(second_ready[u], 1)
                if kind == "join":
                    for i, u in ago(JOIN):
                        dve.wait_ge(r_root[u], i + 1)
                        nc.vector.reciprocal(rstat[:, u, 3, :], rstat[:, u, 2, :]).then_inc(r_inv[u], 1)
                        dve.wait_ge(r_inv[u], i + 1)
                        wait(dve, y_stored[u], i * 16)
                        wait(dve, second_ready[u], i)
                        nc.vector.tensor_tensor(y[:, u], r[:, u], per_node(rstat[:, u, 3, :]), ALU.mult).then_inc(y_ready[u], 1)
                    for i, u in ago(SHIFT):
                        dve.wait_ge(shifted[u], i + 1)
                        dve.wait_ge(in2_ok[u], (i + 1) * 16)
                        nc.vector.tensor_tensor(r[:, u], v[:, u], in2[:, u], ALU.add).then_inc(r_added[u], 1)
                        dve.wait_ge(r_added[u], i + 1)
                        nc.vector.tensor_reduce(rstat[:, u, 4, :], r[:, u], AX.X, ALU.add).then_inc(r_total[u], 1)
                        dve.wait_ge(r_total[u], i + 1)
                        nc.vector.tensor_scalar(rstat[:, u, 5, :], rstat[:, u, 4, :], 1.0 / D, None, ALU.mult).then_inc(r_mean[u], 1)
                        dve.wait_ge(r_mean[u], i + 1)
                        nc.vector.tensor_tensor(r[:, u], r[:, u], per_node(rstat[:, u, 5, :]), ALU.subtract).then_inc(r_ready[u], 1)

        @block.tensor
        def _(pe):
            if bias is not None:
                nc.tensor.matmul(ps_t[0:3, 0, 0:P], t.ones[0:1, 0:3], t.rows[0:1, bias, :], start=True,
                                 stop=True).then_inc(bias_turned, 1)
                pe.wait_ge(bias_ok, 1)

            @skewed(pe, STEPS, PROD)
            def _(ago):
                for i, u in ago(TURN):
                    if gathered_in:
                        pe.wait_ge(g_ready[u], i + 1)
                    else:
                        pe.wait_ge(in0_ok[u], (i + 1) * 16)
                    wait(pe, gt_ready[u], i)
                    for n in range(T // 2):
                        ins = nc.tensor.transpose(ps_t[:, u, n * P:(n + 1) * P],
                                                  g[:, u, 2 * n:2 * n + 2, :].rearrange("p t d -> p (t d)"), t.ident[:])
                    ins.then_inc(turned[u], 1)
                for i, u in ago(PROD):
                    pe.wait_ge(gt_ready[u], i + 1)
                    wait(pe, v_ready[u], i)
                    if bias is not None:
                        for lo, hi in ((0, 512), (512, TD)):
                            nc.tensor.matmul(ps_v[:, u, lo:hi], ones[:], brow[:, lo:hi], start=True, stop=False,
                                             skip_group_check=True)
                    for n in range(T // 2):
                        ins = nc.tensor.matmul(ps_v[:, u, n * P:(n + 1) * P], gt[:, u, n * P:(n + 1) * P], weight[:],
                                               start=bias is None, stop=True, skip_group_check=True)
                    ins.then_inc(product[u], 1)

        @block.scalar
        def _(act):
            @skewed(act, STEPS, JOIN if kind == "join" else NORM)
            def _(ago):
                for i, u in ago(NORM):
                    act.wait_ge(var_ready[u], i + 1)
                    nc.scalar.activation(stat[:, u, 2, :], stat[:, u, 1, :], ACT.Sqrt).then_inc(root_ready[u], 1)
                if kind == "join":
                    for i, u in ago(JOIN):
                        act.wait_ge(r_var[u], i + 1)
                        nc.scalar.activation(rstat[:, u, 2, :], rstat[:, u, 1, :], ACT.Sqrt).then_inc(r_root[u], 1)
                for i, u in ago(TURN):
                    act.wait_ge(turned[u], i + 1)
                    wait(act, product[u], i)
                    nc.scalar.copy(gt[:, u], ps_t[:, u, 0:TD]).then_inc(gt_ready[u], 1)
                for i, u in ago(PROD):
                    if gathered_in:
                        act.wait_ge(product[u], i + 1)
                        squared = ps_v[:, u, 0:TD]
                    else:
                        act.wait_ge(v_ready[u], i + 1)
                        squared = v[:, u].rearrange("p t d -> p (t d)")
                    wait(act, summed[u], i)
                    nc.scalar.activation(sq[:, u].rearrange("p t d -> p (t d)"), squared, ACT.Square).then_inc(sq_ready[u], 1)
                if kind == "join":
                    for i, u in ago(SHIFT):
                        act.wait_ge(r_ready[u], i + 1)
                        wait(act, r_summed[u], i)
                        nc.scalar.activation(rsq[:, u], r[:, u], ACT.Square).then_inc(rsq_ready[u], 1)


def node_degrees(nc, t, ctx, part):
    with ExitStack() as c2:
        n = f"deg{part}_"
        tmp = c2.enter_context(nc.sbuf_tensor(n + "tmp", [P, 2, J], F32))
        loaded = c2.enter_context(semaphore(nc, n + "loaded"))
        chain = c2.enter_context(semaphore(nc, n + "chain"))
        root = c2.enter_context(semaphore(nc, n + "root"))
        block = c2.enter_context(nc.Block())
        if part == 0:
            index = c2.enter_context(nc.sbuf_tensor(n + "index", [P, J], I32))

            @block.gpsimd
            def _(pool):
                nc.gpsimd.iota(index[:], [[1, J]], base=0, channel_multiplier=J).then_inc(root, 1)

            @block.sync
            def _(sp):
                sp.dma_start(tmp[:, 0, :], t.in_degree.rearrange("(p j) o -> p (j o)", p=P)).then_inc(loaded, 16)

            @block.vector
            def _(dve):
                c = Chain(dve, chain)
                dve.wait_ge(root, 1)
                dve.wait_ge(loaded, 16)
                c.link(nc.vector.tensor_scalar(t.real[:], index[:], float(N), None, ALU.is_lt))
                c.link(nc.vector.tensor_scalar(tmp[:, 0, :], tmp[:, 0, :], 1.0, None, ALU.add))
                dve.wait_ge(root, 2)
                nc.vector.reciprocal(t.dis[:], tmp[:, 1, :])

            @block.scalar
            def _(act):
                act.wait_ge(chain, 2)
                nc.scalar.activation(tmp[:, 1, :], tmp[:, 0, :], ACT.Sqrt).then_inc(root, 1)
        else:
            @block.vector
            def _(dve):
                inverse_root(Chain(dve, chain), nc, dve, t.deg[:], t.dinv[:], tmp[:, 0, :], root)

            @block.scalar
            def _(act):
                act.wait_ge(chain, 3)
                nc.scalar.activation(t.dinv[:], t.dinv[:], ACT.Sqrt).then_inc(root, 1)


def gin_first(nc, t, x3, add, z1t):
    with ExitStack() as ctx:
        def sb(n, shape, dt=F32):
            return ctx.enter_context(nc.sbuf_tensor(f"bn_{n}", shape, dt))

        def sem(n):
            return ctx.enter_context(semaphore(nc, f"bn_{n}"))

        def sems(n):
            return [sem(n + str(u)) for u in range(2)]

        in0, in1, g = sb("in0", [P, 2, T, D]), sb("in1", [P, 2, T, D]), sb("g", [P, 2, T, D])
        gt, z, junk = sb("gt", [P, 2, TD]), sb("z", [P, 2, TD]), sb("junk", [P, 2, TD])
        sums = sb("sums", [P, 2, 2 * STEPS])
        total, tot2, fold, tmp = sb("total", [P, 2]), sb("total2", [P, 2]), sb("fold", [P, P]), sb("tmp", [P, 4])
        ps_t = ctx.enter_context(nc.psum_tensor("bn_ps_t", [P, 2, 1024], F32))
        ps_z = ctx.enter_context(nc.psum_tensor("bn_ps_z", [P, 2, 1024], F32))
        loaded, g_ready, turned, gt_ready, product = sems("loaded"), sems("g_ready"), sems("turned"), sems("gt_ready"), sems("product")
        z_ready, squared, stored, sp_passed, chain, folded, root = sems("z_ready"), sems("squared"), sems("stored"), sem("sp_passed"), sem("chain"), sem("folded"), sem("root")
        block = ctx.enter_context(nc.Block())

        @block.sync
        def _(sp):
            @repeat(sp, STEPS)
            def _(i):
                for u in range(2):
                    wait(sp, g_ready[u], i)
                    sp.sem_inc(sp_passed, 1)
                    sp.dma_start(in0[:, u], chunk(x3, i, u)).then_inc(loaded[u], 16)
                    sp.dma_start(in1[:, u], chunk(add, i, u)).then_inc(loaded[u], 16)

        @block.vector
        def _(dve):
            @repeat(dve, STEPS)
            def _(i):
                for u in range(2):
                    dve.wait_ge(loaded[u], (i + 1) * 32)
                    wait(dve, turned[u], i)
                    nc.vector.scalar_tensor_tensor(g[:, u], in0[:, u], t.eps1[:], in1[:, u], ALU.mult, ALU.add).then_inc(g_ready[u], 1)
            c = Chain(dve, chain)
            for u in range(2):
                dve.wait_ge(squared[u], STEPS)
            for h in range(2):
                half = slice(h * D, (h + 1) * D)
                for k in range(2):
                    nc.vector.tensor_copy(fold[half, k * D:(k + 1) * D], t.ident[half, half])
            c.link(nc.vector.tensor_reduce(total[:], sums[:], AX.X, ALU.add))
            dve.wait_ge(folded, 1)
            c.link(nc.vector.tensor_scalar(tot2[:], ps_t[:, 0, 0:2], 1.0 / N, None, ALU.mult))
            c.link(nc.vector.tensor_tensor(tmp[:, 0:1], tot2[:, 0:1], tot2[:, 0:1], ALU.mult))
            c.link(nc.vector.scalar_tensor_tensor(tmp[:, 1:2], tot2[:, 1:2], EPS, tmp[:, 0:1], ALU.add, ALU.subtract))
            dve.wait_ge(root, 1)
            c.link(nc.vector.reciprocal(tmp[:, 3:4], tmp[:, 2:3]))
            c.link(nc.vector.tensor_tensor(t.bn[:, 0:1], t.gb3[:, 0:1], tmp[:, 3:4], ALU.mult))
            c.link(nc.vector.tensor_tensor(tmp[:, 0:1], tot2[:, 0:1], t.bn[:, 0:1], ALU.mult))
            c.link(nc.vector.tensor_tensor(t.bn[:, 1:2], t.gb3[:, 1:2], tmp[:, 0:1], ALU.subtract))

        @block.tensor
        def _(pe):
            @repeat(pe, STEPS)
            def _(i):
                for u in range(2):
                    pe.wait_ge(g_ready[u], i + 1)
                    wait(pe, gt_ready[u], i)
                    for n in range(T // 2):
                        ins = nc.tensor.transpose(ps_t[:, u, n * P:(n + 1) * P],
                                                  g[:, u, 2 * n:2 * n + 2, :].rearrange("p t d -> p (t d)"), t.ident[:])
                    ins.then_inc(turned[u], 1)
                for u in range(2):
                    pe.wait_ge(gt_ready[u], i + 1)
                    wait(pe, squared[u], i)
                    for lo, hi in ((0, 512), (512, TD)):
                        ins = nc.tensor.matmul(ps_z[:, u, lo:hi], t.dense3[:], gt[:, u, lo:hi], start=True, stop=True)
                    ins.then_inc(product[u], 1)
            pe.wait_ge(chain, 1)
            nc.tensor.matmul(ps_t[:, 0, 0:2], fold[:], total[:], start=True, stop=True).then_inc(folded, 1)

        @block.scalar
        def _(act):
            @repeat(act, STEPS)
            def _(i):
                for u in range(2):
                    act.wait_ge(turned[u], i + 1)
                    wait(act, product[u], i)
                    nc.scalar.copy(gt[:, u], ps_t[:, u, 0:TD]).then_inc(gt_ready[u], 1)
                for u in range(2):
                    c = bass.ds(i * 2 + u, 1)
                    act.wait_ge(product[u], i + 1)
                    wait(act, stored[u], i * 16)
                    nc.scalar.activation(z[:, u], ps_z[:, u, 0:TD], ACT.Identity, accum_out=sums[:, 0, c]).then_inc(z_ready[u], 1)
                    wait(act, squared[u], i)
                    nc.scalar.activation(junk[:, u], ps_z[:, u, 0:TD], ACT.Square, accum_out=sums[:, 1, c]).then_inc(squared[u], 1)
                    act.wait_ge(z_ready[u], i + 1)
                    act.dma_start(z1t[c].rearrange("o p e -> p (o e)"), z[:, u]).then_inc(stored[u], 16)
            for u in range(2):
                act.wait_ge(stored[u], STEPS * 16)
            act.wait_ge(chain, 4)
            nc.scalar.activation(tmp[:, 2:3], tmp[:, 1:2], ACT.Sqrt).then_inc(root, 1)


def gin_last(nc, t, x3, z1t, out):
    with ExitStack() as ctx:
        def sb(n, shape, dt=F32):
            return ctx.enter_context(nc.sbuf_tensor(f"last_{n}", shape, dt))

        def sem(n):
            return ctx.enter_context(semaphore(nc, f"last_{n}"))

        def sems(n):
            return [sem(n + str(u)) for u in range(2)]

        in0, v, sq = sb("in0", [P, 2, T, D]), sb("v", [P, 2, T, D]), sb("sq", [P, 2, T, D])
        z, r, stat = sb("z", [P, 2, TD]), sb("r", [P, 2, TD]), sb("stat", [P, 2, 4, T])
        ps_v = ctx.enter_context(nc.psum_tensor("last_ps_v", [P, 2, 1024], F32))
        z_ok, x_ok, r_ready, product, v_ready = sems("z_ok"), sems("x_ok"), sems("r_ready"), sems("product"), sems("v_ready")
        sq_ready, var_ready, root_ready, chain, y_ready, stored = sems("sq_ready"), sems("var_ready"), sems("root_ready"), sems("chain"), sems("y_ready"), sems("stored")
        sp_passed = sem("sp_passed")
        block = ctx.enter_context(nc.Block())

        @block.sync
        def _(sp):
            @repeat(sp, STEPS)
            def _(i):
                for u in range(2):
                    wait(sp, r_ready[u], i)
                    sp.sem_inc(sp_passed, 1)
                    sp.dma_start(z[:, u], z1t[bass.ds(i * 2 + u, 1)].rearrange("o p e -> p (o e)")).then_inc(z_ok[u], 16)
                    wait(sp, v_ready[u], i)
                    sp.sem_inc(sp_passed, 1)
                    sp.dma_start(in0[:, u], chunk(x3, i, u)).then_inc(x_ok[u], 16)

        @block.scalar
        def _(act):
            @repeat(act, STEPS)
            def _(i):
                for u in range(2):
                    act.wait_ge(z_ok[u], (i + 1) * 16)
                    wait(act, product[u], i)
                    nc.scalar.activation(r[:, u], z[:, u], ACT.Relu, scale=t.bn[:, 0:1], bias=t.bn[:, 1:2]).then_inc(r_ready[u], 1)
                for u in range(2):
                    act.wait_ge(v_ready[u], i + 1)
                    nc.scalar.activation(sq[:, u], v[:, u], ACT.Square).then_inc(sq_ready[u], 1)
                for u in range(2):
                    act.wait_ge(var_ready[u], i + 1)
                    nc.scalar.activation(stat[:, u, 2, :], stat[:, u, 1, :], ACT.Sqrt).then_inc(root_ready[u], 1)
                for u in range(2):
                    act.wait_ge(y_ready[u], i + 1)
                    act.dma_start(chunk(out, i, u), v[:, u]).then_inc(stored[u], 16)
            for u in range(2):
                act.wait_ge(stored[u], STEPS * 16)

        @block.tensor
        def _(pe):
            @repeat(pe, STEPS)
            def _(i):
                for u in range(2):
                    pe.wait_ge(r_ready[u], i + 1)
                    wait(pe, v_ready[u], i)
                    for n in range(T // 2):
                        ins = nc.tensor.matmul(ps_v[:, u, n * P:(n + 1) * P], r[:, u, n * P:(n + 1) * P], t.out3[:], start=True, stop=True)
                    ins.then_inc(product[u], 1)

        @block.vector
        def _(dve):
            @repeat(dve, STEPS)
            def _(i):
                for u in range(2):
                    dve.wait_ge(product[u], i + 1)
                    dve.wait_ge(x_ok[u], (i + 1) * 16)
                    wait(dve, stored[u], i * 16)
                    nc.vector.tensor_tensor(v[:, u], ps_v[:, u, 0:TD].rearrange("p (t d) -> p t d", t=T), in0[:, u], ALU.add).then_inc(v_ready[u], 1)
                for u in range(2):
                    dve.wait_ge(sq_ready[u], i + 1)
                    nc.vector.tensor_reduce(stat[:, u, 0, :], sq[:, u], AX.X, ALU.add).then_inc(chain[u], 1)
                    dve.wait_ge(chain[u], i * 2 + 1)
                    nc.vector.tensor_scalar(stat[:, u, 1, :], stat[:, u, 0, :], 1.0 / D, EPS, ALU.mult, ALU.add).then_inc(var_ready[u], 1)
                for u in range(2):
                    dve.wait_ge(root_ready[u], i + 1)
                    nc.vector.reciprocal(stat[:, u, 3, :], stat[:, u, 2, :]).then_inc(chain[u], 1)
                    wait(dve, chain[u], i * 2 + 2)
                    nc.vector.tensor_tensor(v[:, u], v[:, u], per_node(stat[:, u, 3, :]), ALU.mult).then_inc(y_ready[u], 1)


def node_tensors(nc, ctx, t):
    def sb(name, shape, dt=F32):
        return ctx.enter_context(nc.sbuf_tensor(name, shape, dt))

    def dram(name, shape, dt=F32):
        return nc.dram_tensor(name, shape, dt).ap()

    t.dis = sb("dis", [P, J])
    t.deg = sb("deg", [P, J])
    t.dinv = sb("dinv", [P, J])
    t.real = sb("real", [P, J])
    t.bn = sb("bn", [P, 2])
    t.x1 = dram("x1", [NP, D])
    t.xt = dram("xt", [NP, D])
    t.x2 = dram("x2", [NP, D])
    t.xs = dram("xs", [NP, D])
    t.x3 = dram("x3", [NP, D])
    t.z1t = dram("z1t", [2 * STEPS, P, TD])


def four_layers(nc, w, out):
    SPENT.clear()
    with ExitStack() as ctx:
        t = tensors(nc, ctx)
        add_tensors(nc, ctx, t)
        node_tensors(nc, ctx, t)
        constants(nc, t)
        sort_edges(nc, t, w["src"], w["dst"], w["etype"], w["weight"])
        clear_tables(nc, t)
        edge_fields(nc, t)
        spans(nc, t, 0, t.row_s[0], t.span_s, t.fix_edge[:], t.fix_node_s[:])
        spans(nc, t, 1, t.row_t[0], t.span_t, None, t.fix_node_t[:])
        equal_tables(nc, t)
        follow(nc, t)
        weights(nc, ctx, t, w)
        edge_scores(nc, t, w["x"])
        edge_softmax(nc, t)
        attention(nc, t)
        recycle(nc)
        node_degrees(nc, t, ctx, 0)
        dense_pass(nc, t, "first", "first", w["x"], t.sum0, t.dense0, [t.x1, t.xt])
        node_degrees(nc, t, ctx, 1)
        for k in range(4):
            recycle(nc)
            edge_pass(nc, t, f"gcn{k}", "plain", t.eq_t, table=t.xt, idx=t.t_row_s, put=t.put_t, target=t.sum_t)
            carry_spans(nc, t, f"gcn_carry{k}", t.span_t, node_ends(t), D, t.sum_t, t.fix_node_t)
            if k < 3:
                dense_pass(nc, t, f"round{k}", "round", t.xt, t.sum_t, t.dense1, [t.xt], bias=0)
            else:
                dense_pass(nc, t, "join", "join", t.xt, t.sum_t, t.dense1, [t.x2, t.xs], bias=0, x1=t.x1)
        recycle(nc)
        edge_pass(nc, t, "cheb1", "cheb1", t.eq_s, table=t.xs, idx=t.t_col, target=t.cheb_rows)
        ends = t.cheb_rows[0:EP, :].rearrange("(c q p) w -> p q c w", c=4, q=Q)[P - 1]
        carry_spans(nc, t, "cheb_carry1", t.span_s, ends, D, t.cheb_rows, t.fix_edge)
        edge_pass(nc, t, "cheb2", "cheb2", t.eq_s, table=t.cheb_rows, idx=t.next_col, put=t.put_s, target=t.sum_s)
        carry_spans(nc, t, "cheb_carry2", t.span_s, node_ends(t), D, t.sum_s, t.fix_node_s)
        recycle(nc)
        dense_pass(nc, t, "chebd", "cheb", t.x2, t.sum_s, t.dense2, [t.x3], bias=1)
        edge_pass(nc, t, "gin", "gin", t.eq_s, table=t.x3, idx=t.t_col, put=t.put_s, target=t.sum_s)
        carry_spans(nc, t, "gin_carry", t.span_s, node_ends(t), D, t.sum_s, t.fix_node_s)
        recycle(nc)
        gin_first(nc, t, t.x3, t.sum_s, t.z1t)
        gin_last(nc, t, t.x3, t.z1t, out)


def kernel(**inputs):
    import numpy as np
    import concourse.bacc as bacc
    from concourse.bass_utils import run_bass_kernel_spmd

    a = {k: np.asarray(v) for k, v in inputs.items()}

    def tile_major(v, pad):
        out = np.full(EP, pad, v.dtype)
        out[:E] = v
        return np.ascontiguousarray(out.reshape(TILES, P).T)

    x = np.zeros((NP, D), a["x"].dtype)
    x[:N] = a["x"]
    arrays = {"x": x, "src": tile_major(a["src"], N), "dst": tile_major(a["dst"], N),
              "etype": tile_major(a["edge_type_200"], 0), "weight": tile_major(a["edge_weight"], 0)}
    for k, v in a.items():
        if k.startswith("L"):
            if k in ("L3_gnn_W_lin", "L3_gnn_W1", "L3_gnn_W2"):
                arrays[k + "_T"] = np.ascontiguousarray(v.T)
            else:
                arrays[k] = np.ascontiguousarray(v.reshape(1, -1) if v.ndim == 1 else v)
    nc = bacc.Bacc("TRN2", target_bir_lowering=False, num_devices=1)
    w = {}
    for name, v in arrays.items():
        w[name] = nc.dram_tensor(f"in_{name}", v.shape, mybir.dt.from_np(v.dtype), kind="ExternalInput").ap()
    out = nc.dram_tensor("out", [NP, D], F32, kind="ExternalOutput").ap()
    four_layers(nc, w, out)
    r = run_bass_kernel_spmd(nc, [{f"in_{name}": v for name, v in arrays.items()}], core_ids=[0])
    return r.results[0]["out"][:N]
```

```python
from contextlib import ExitStack, contextmanager

import concourse.bass as bass
from concourse import mybir

P = 128
N = 100000
E = 50000
D = 64
H = 4
R = 200
BLK = 256
NBLK = 392
NP = BLK * NBLK
J = NP // P
TILES = 392
EP = TILES * P
CT = 7
CH = CT * P
PAIRS = TILES // (2 * CT)
Q = 98
BIG = float(1 << 20)
NONE = float(EP)

ALU = mybir.AluOpType
ACT = mybir.ActivationFunctionType
AX = mybir.AxisListType
F32 = mybir.dt.float32
F16 = mybir.dt.float16
BF16 = mybir.dt.bfloat16
I32 = mybir.dt.int32


class Chain:

    def __init__(self, eng, sem, base=0):
        self.eng, self.sem, self.base, self.n = eng, sem, base, 0

    def link(self, ins):
        self.n += 1
        ins.then_inc(self.sem, 1)
        self.eng.wait_ge(self.sem, self.base + self.n)


def repeat(eng, steps):
    def run(body):
        body(0)
        with eng.Fori(1, steps) as i:
            body(i)
    return run


def skewed(eng, steps, most):
    back = -(-most // 2)

    def run(body):
        def pair(i):
            for u in range(2):
                def ago(n):
                    turn = i + (u - n) // 2 if (u - n) // 2 else i
                    out = isinstance(turn, int) and not 0 <= turn < steps
                    return () if out else ((turn, (u - n) % 2),)
                body(ago)
        for i in range(back + 1):
            pair(i)
        with eng.Fori(back + 1, steps) as i:
            pair(i)
        for i in range(steps, steps + back):
            pair(i)
    return run


def wait(eng, sem, value):
    if not (isinstance(value, int) and value <= 0):
        eng.wait_ge(sem, value)


SPENT = []


@contextmanager
def semaphore(nc, name):
    handle = nc.alloc_semaphore(name=name)
    yield handle
    SPENT.append(handle)


def recycle(nc):
    nc.clear_and_free_semaphores(SPENT)
    SPENT.clear()
    nc.all_engine_barrier()


class Tensors:
    pass


def tensors(nc, ctx):
    t = Tensors()

    def sb(name, shape, dt=F32):
        return ctx.enter_context(nc.sbuf_tensor(name, shape, dt))

    def dram(name, shape, dt=F32):
        return nc.dram_tensor(name, shape, dt).ap()

    t.iota = sb("iota", [P, NBLK], F16)
    t.ident = sb("ident", [P, P])
    t.before = sb("before", [P, P], F16)
    t.notbefore = sb("notbefore", [P, P], F16)
    t.beforef = sb("beforef", [P, P])
    t.beforea = sb("beforea", [P, 2, BLK])
    t.ones = sb("ones", [P, P])
    t.base_lo = sb("base_lo", [P, 2, BLK])
    t.base_hi = sb("base_hi", [P, 2, NBLK])
    t.by_lo_s = dram("by_lo_s", [EP, 4])
    t.by_lo_t = dram("by_lo_t", [EP, 2])
    t.sorted_s = dram("sorted_s", [EP, 4])
    t.sorted_t = dram("sorted_t", [EP, 2])
    t.last_of_node = dram("last_of_node", [NP, 1], I32)
    t.in_degree = dram("in_degree", [NP, 1])
    return t


def constants(nc, t):
    with ExitStack() as ctx:
        diff = ctx.enter_context(nc.sbuf_tensor("diff", [P, BLK], I32))
        row = ctx.enter_context(nc.sbuf_tensor("row", [P, NBLK], I32))
        made = ctx.enter_context(semaphore(nc, "iotas_made"))
        block = ctx.enter_context(nc.Block())

        @block.gpsimd
        def _(pool):
            nc.gpsimd.iota(diff[:], [[1, BLK]], base=0, channel_multiplier=-1).then_inc(made, 1)
            nc.gpsimd.iota(row[:], [[1, NBLK]], base=0, channel_multiplier=0).then_inc(made, 1)

        @block.vector
        def _(dve):
            dve.wait_ge(made, 2)
            nc.vector.tensor_copy(t.iota[:], row[:])
            nc.vector.memset(t.ones[:], 1.0)
            nc.vector.tensor_scalar(t.ident[:], diff[:, 0:P], 0.0, None, ALU.is_equal)
            nc.vector.tensor_scalar(t.before[:], diff[:, 0:P], 0.0, None, ALU.is_gt)
            nc.vector.tensor_scalar(t.notbefore[:], diff[:, 0:P], 0.0, None, ALU.is_le)
            nc.vector.tensor_scalar(t.beforef[:], diff[:, 0:P], 0.0, None, ALU.is_gt)
            nc.vector.tensor_scalar(t.beforea[:, 0, :], diff[:], 0.0, None, ALU.is_gt)
            nc.vector.tensor_scalar(t.beforea[:, 1, :], diff[:], float(P), None, ALU.is_gt)


def digits(dve, link, key_i, lo, hi, tmp):
    link(dve.tensor_scalar(tmp, key_i, BLK - 1, None, ALU.bitwise_and))
    link(dve.tensor_copy(lo, tmp))
    link(dve.tensor_scalar(tmp, key_i, 8, None, ALU.logical_shift_right))
    link(dve.tensor_copy(hi, tmp))


def histogram(nc, t, lo, hi):
    with ExitStack() as ctx:
        def sb(name, shape, dt=F32):
            return ctx.enter_context(nc.sbuf_tensor(name, shape, dt))

        def sem(name):
            return ctx.enter_context(semaphore(nc, name))

        SLOTS = 4
        oh = sb("onehots", [P, SLOTS, 2, BLK + NBLK], F16)
        zeros = sb("hist_zeros", [P, NBLK], F16)
        blank = sb("blank", [P, 2048])
        cnt = sb("counts", [P, 2, 2, NBLK])
        rows = sb("row_sums", [P, 4])
        rowsb = sb("row_sums_b", [P, 4, P])
        incl = sb("inclusive", [P, NBLK])
        node = sb("node_rows", [P, 2, 2, NBLK])
        flag = sb("node_flags", [P, 2, NBLK])
        turned = sb("turned", [Q, 2, 4, BLK])
        turned_i = sb("turned_i", [Q, 4, BLK], I32)
        ps = ctx.enter_context(nc.psum_tensor("hist_ps", [P, 8, 512], F32))
        ready = sem("onehots_ready")
        used = sem("onehots_used")
        zero = sem("hist_zero")
        chain = sem("hist_chain")
        pe = sem("hist_pe")
        stored = sem("hist_stored")
        blank_made, cleared = sem("blank_made"), sem("tables_cleared")
        block = ctx.enter_context(nc.Block())

        @block.scalar
        def _(act):
            act.wait_ge(blank_made, 1)
            n = 0
            for tab in (t.sum0, t.sum_s, t.sum_t):
                flat = tab.rearrange("(p r) w -> p (r w)", p=P)
                for a in range(0, flat.shape[1], blank.shape[1]):
                    b = min(flat.shape[1], a + blank.shape[1])
                    act.dma_start(flat[:, a:b], blank[:, 0:b - a]).then_inc(cleared, 16)
                    n += 1
            for tab in (t.edges_a, t.edges_b, t.cheb_rows):
                act.dma_start(tab[EP:EP + P, :], blank[:, 0:tab.shape[1]]).then_inc(cleared, 16)
                n += 1
            act.wait_ge(cleared, 16 * n)

        @block.vector
        def _(dve):
            nc.vector.memset(zeros[:], 0.0).then_inc(zero, 1)
            nc.vector.memset(blank[:], 0.0).then_inc(blank_made, 1)
            @repeat(dve, TILES // SLOTS)
            def _(i):
                for u in range(SLOTS):
                    wait(dve, used, i * SLOTS + u + 3 - SLOTS)
                    for k in range(2):
                        nc.vector.tensor_scalar(oh[:, u, k, 0:BLK], t.iota[:, 0:BLK],
                                                lo[:, k, bass.ds(i * SLOTS + u, 1)], None, ALU.is_equal)
                        last = nc.vector.tensor_scalar(oh[:, u, k, BLK:], t.iota[:],
                                                       hi[:, k, bass.ds(i * SLOTS + u, 1)], None, ALU.is_equal)
                    last.then_inc(ready, 1)
            dve.wait_ge(used, TILES + 2)
            c = Chain(dve, chain)
            for k in range(2):
                c.link(nc.vector.tensor_copy(cnt[:, k, :, :], ps[:, 2 * k:2 * k + 2, 0:NBLK]))
                c.link(nc.vector.tensor_reduce(rows[:, 2 * k:2 * k + 2], cnt[:, k, :, :], AX.X, ALU.add))
                for m in range(2):
                    c.link(nc.vector.tensor_scalar(rowsb[:, 2 * k + m, :], t.ones[:],
                                                   rows[:, 2 * k + m:2 * k + m + 1], None, ALU.mult))
            for k in range(2):
                dve.wait_ge(pe, 2 * k + 1)
                c.link(nc.vector.tensor_copy(t.base_lo[:, k, :], ps[:, 4, 0:BLK]))
                c.link(nc.vector.tensor_tensor_scan(incl[:], t.ones[:, 0:1].to_broadcast([P, NBLK]), ps[:, 5, 0:NBLK],
                                                    0.0, ALU.mult, ALU.add))
                c.link(nc.vector.tensor_tensor(t.base_hi[:, k, :], incl[:], ps[:, 5, 0:NBLK], ALU.subtract))
                if k == 0:
                    dve.wait_ge(pe, 2)
                    for m in range(2):
                        c.link(nc.vector.tensor_tensor(node[:, 0, m, :], ps[:, 6 + m, 0:NBLK], t.base_hi[:, 0, :], ALU.add))
                        c.link(nc.vector.tensor_scalar(flag[:, m, :], cnt[:, 0, m, :], 0.0, None, ALU.is_gt))
                        c.link(nc.vector.tensor_tensor(node[:, 0, m, :], node[:, 0, m, :], cnt[:, 0, m, :], ALU.add))
                        c.link(nc.vector.scalar_tensor_tensor(node[:, 0, m, :], node[:, 0, m, :], -1.0 - NONE,
                                                              flag[:, m, :], ALU.add, ALU.mult))
                        c.link(nc.vector.tensor_scalar(node[:, 0, m, :], node[:, 0, m, :], NONE, None, ALU.add))
            for k in range(2):
                for g in range(4):
                    dve.wait_ge(pe, 3 + 4 * k + g + 1)
                    c.link(nc.vector.tensor_copy(turned[:, k, g, :], ps[0:Q, 4 + g, 0:BLK]))
            c.link(nc.vector.tensor_copy(turned_i[:], turned[:, 0, :, :]))

        @block.tensor
        def _(pe_):
            pe_.wait_ge(zero, 1)
            for k in range(2):
                for m in range(2):
                    ins = nc.tensor.matmul(ps[:, 2 * k + m, 0:NBLK], zeros[:, 0:P], zeros[:],
                                           start=True, stop=False, skip_group_check=True)
                ins.then_inc(used, 1)
            @repeat(pe_, TILES // SLOTS)
            def _(i):
                for u in range(SLOTS):
                    pe_.wait_ge(ready, i * SLOTS + u + 1)
                    for k in range(2):
                        for m in range(2):
                            ins = nc.tensor.matmul(ps[:, 2 * k + m, 0:NBLK], oh[:, u, k, m * P:(m + 1) * P],
                                                   oh[:, u, k, BLK:], start=False, stop=False, skip_group_check=True)
                    ins.then_inc(used, 1)
            for k in range(2):
                pe_.wait_ge(chain, [8, 11][k])
                for m in range(2):
                    nc.tensor.matmul(ps[:, 4, 0:BLK], rowsb[:, 2 * k + m, :], t.beforea[:, m, :], start=m == 0, stop=m == 1)
                for m in range(2):
                    ins = nc.tensor.matmul(ps[:, 5, 0:NBLK], t.ones[:], cnt[:, k, m, :], start=m == 0, stop=m == 1)
                ins.then_inc(pe, 1)
                if k == 0:
                    nc.tensor.matmul(ps[:, 6, 0:NBLK], t.beforef[:], cnt[:, 0, 0, :], start=True, stop=True)
                    nc.tensor.matmul(ps[:, 7, 0:NBLK], t.ones[:], cnt[:, 0, 0, :], start=True, stop=False)
                    nc.tensor.matmul(ps[:, 7, 0:NBLK], t.beforef[:], cnt[:, 0, 1, :], start=False, stop=True).then_inc(pe, 1)
            for k in range(2):
                for g in range(4):
                    pe_.wait_ge(chain, 24 if k == 0 else 24 + g + 1)
                    for m in range(2):
                        src = node[:, 0, m, :] if k == 0 else cnt[:, 1, m, :]
                        ins = nc.tensor.transpose(ps[0:Q, 4 + g, m * P:(m + 1) * P],
                                                  src[:, g * Q:(g + 1) * Q], t.ident[:])
                    ins.then_inc(pe, 1)

        @block.sync
        def _(sp):
            sp.wait_ge(chain, 33)
            sp.dma_start(t.last_of_node.rearrange("(g q a) o -> q g (a o)", g=4, q=Q), turned_i[:]).then_inc(stored, 16)
            sp.dma_start(t.in_degree.rearrange("(g q a) o -> q g (a o)", g=4, q=Q), turned[:, 1, :, :]).then_inc(stored, 16)
            sp.wait_ge(stored, 32)


def radix_pass(nc, t, name, pay, dig, width, base, dst):
    W = [4, 2]
    with ExitStack() as ctx:
        def sb(n, shape, dt=F32):
            return ctx.enter_context(nc.sbuf_tensor(f"{name}_{n}", shape, dt))

        def sem(n):
            return ctx.enter_context(semaphore(nc, f"{name}_{n}"))

        oh = sb("onehot", [P, 2, 2, width], F16)
        junk = sb("junk", [P, 2, 2, width])
        pos = sb("pos", [P, 2, 2, CT])
        pos_i = sb("pos_i", [P, 2, 2, CT], I32)
        stage = [sb(f"stage{k}", [P, 2, CT, W[k]]) for k in range(2)]
        acc = ctx.enter_context(nc.psum_tensor(f"{name}_acc", [P, 2, 512], F32))
        ready, counted, freed, picked = ([sem(f"{n}{k}") for k in range(2)] for n in
                                         ("onehot_ready", "counted", "onehot_free", "picked"))
        posok = sem("positions_ready")
        staged, passed = sem("staged"), sem("passed")
        sent = [sem("sent0"), sem("sent1")]
        block = ctx.enter_context(nc.Block())
        B = 2 * CT

        @block.vector
        def _(dve):
            def onehot(i, n, k):
                wait(dve, freed[k], i * B + n)
                nc.vector.tensor_scalar(oh[:, n % 2, k, :], t.iota[:, 0:width], dig[:, k, bass.ds(i * B + n, 1)], None,
                                        ALU.is_equal).then_inc(ready[k], 1)

            @repeat(dve, PAIRS)
            def _(i):
                for k in range(2):
                    onehot(i, 0, k)
                for u in range(2):
                    wait(dve, sent[u], i * 16 * 2 * CT)
                    for c in range(CT):
                        n = u * CT + c
                        for k in range(2):
                            if n + 1 < B:
                                onehot(i, n + 1, k)
                            dve.wait_ge(counted[k], i * B + n + 1)
                            nc.vector.tensor_tensor_reduce(junk[:, n % 2, k, :], oh[:, n % 2, k, :], acc[:, k, 0:width],
                                                           1.0, 0.0, ALU.mult, ALU.add,
                                                           pos[:, u, k, c:c + 1]).then_inc(picked[k], 1)
                    for k in range(2):
                        dve.wait_ge(picked[k], i * B + (u + 1) * CT)
                    nc.vector.tensor_copy(pos_i[:, u, :, :], pos[:, u, :, :]).then_inc(posok, 1)

        @block.tensor
        def _(pe):
            for k in range(2):
                nc.tensor.matmul(acc[:, k, 0:width], t.ident[:], base[:, k, :], start=True, stop=False,
                                 skip_group_check=True).then_inc(freed[k], 1)

            @repeat(pe, PAIRS)
            def _(i):
                for n in range(B):
                    for k in range(2):
                        if n > 0 or not isinstance(i, int):
                            pe.wait_ge(picked[k], i * B + n)
                            nc.tensor.matmul(acc[:, k, 0:width], t.notbefore[:], oh[:, (n - 1) % 2, k, :],
                                             start=False, stop=False, skip_group_check=True).then_inc(freed[k], 1)
                        pe.wait_ge(ready[k], i * B + n + 1)
                        nc.tensor.matmul(acc[:, k, 0:width], t.before[:], oh[:, n % 2, k, :],
                                         start=False, stop=False, skip_group_check=True).then_inc(counted[k], 1)

        @block.scalar
        def _(act):
            @repeat(act, PAIRS)
            def _(i):
                for u in range(2):
                    wait(act, sent[u], i * 16 * 2 * CT)
                    for k in range(2):
                        ins = nc.scalar.copy(stage[k][:, u, :, :], pay[k][:, bass.ds(i * B + u * CT, CT), 0:W[k]])
                    ins.then_inc(staged, 1)

        @block.gpsimd
        def _(pool):
            @repeat(pool, PAIRS)
            def _(i):
                for u in range(2):
                    pool.wait_ge(posok, i * 2 + u + 1)
                    pool.wait_ge(staged, i * 2 + u + 1)
                    pool.sem_inc(passed, 1)
                    for c in range(CT):
                        for k in range(2):
                            pool.indirect_dma_start(
                                out=dst[k], out_offset=bass.IndirectOffsetOnAxis(pos_i[:, u, k, c:c + 1], 0),
                                in_=stage[k][:, u, c, :], in_offset=None).then_inc(sent[u], 16)
            for u in range(2):
                pool.wait_ge(sent[u], PAIRS * 16 * 2 * CT)


def sort_edges(nc, t, src, dst, etype, weight):
    with ExitStack() as ctx:
        def sb(name, shape, dt=F32):
            return ctx.enter_context(nc.sbuf_tensor(name, shape, dt))

        lo = sb("digit_lo", [P, 2, TILES])
        hi = sb("digit_hi", [P, 2, TILES])
        pay_s = sb("payload_s", [P, TILES, 4])
        pay_t = sb("payload_t", [P, TILES, 2])
        key = sb("keys_i", [P, 3, TILES], I32)
        w = sb("weights_in", [P, TILES])
        tmp = sb("digit_tmp", [P, TILES], I32)
        with ExitStack() as c2:
            loaded = c2.enter_context(semaphore(nc, "edges_loaded"))
            chain = c2.enter_context(semaphore(nc, "digit_chain"))
            block = c2.enter_context(nc.Block())

            @block.sync
            def _(sp):
                for n, a in enumerate((src, dst, etype)):
                    sp.dma_start(key[:, n, :], a).then_inc(loaded, 16)
                sp.dma_start(w[:], weight).then_inc(loaded, 16)

            @block.vector
            def _(dve):
                dve.wait_ge(loaded, 64)
                c = Chain(dve, chain)
                for k in range(2):
                    digits(nc.vector, c.link, key[:, k, :], lo[:, k, :], hi[:, k, :], tmp[:])
                for n in range(3):
                    nc.vector.tensor_copy(pay_s[:, :, n], key[:, n, :])
                nc.vector.tensor_copy(pay_s[:, :, 3], w[:])
                nc.vector.tensor_copy(pay_t[:, :, 0], key[:, 1, :])
                nc.vector.tensor_copy(pay_t[:, :, 1], key[:, 0, :])

        histogram(nc, t, lo, hi)
        radix_pass(nc, t, "low", [pay_s, pay_t], lo, BLK, t.base_lo, [t.by_lo_s, t.by_lo_t])
        with ExitStack() as c2:
            loaded = c2.enter_context(semaphore(nc, "by_lo_loaded"))
            chain = c2.enter_context(semaphore(nc, "digit2_chain"))
            block = c2.enter_context(nc.Block())

            @block.sync
            def _(sp):
                sp.dma_start(pay_s[:], t.by_lo_s.rearrange("(j p) w -> p j w", p=P)).then_inc(loaded, 16)
                sp.dma_start(pay_t[:], t.by_lo_t.rearrange("(j p) w -> p j w", p=P)).then_inc(loaded, 16)

            @block.vector
            def _(dve):
                dve.wait_ge(loaded, 32)
                c = Chain(dve, chain)
                for k, pay in enumerate((pay_s, pay_t)):
                    c.link(nc.vector.tensor_copy(key[:, k, :], pay[:, :, 0]))
                    c.link(nc.vector.tensor_scalar(tmp[:], key[:, k, :], 8, None, ALU.logical_shift_right))
                    c.link(nc.vector.tensor_copy(hi[:, k, :], tmp[:]))

        radix_pass(nc, t, "high", [pay_s, pay_t], hi, NBLK, t.base_hi, [t.sorted_s, t.sorted_t])


def add_tensors(nc, ctx, t):
    def sb(name, shape, dt=F32):
        return ctx.enter_context(nc.sbuf_tensor(name, shape, dt))

    def dram(name, shape, dt=F32):
        return nc.dram_tensor(name, shape, dt).ap()

    more = TILES + 2 * CT
    t.s_col = sb("s_col", [P, more], I32)
    t.t_col = sb("t_col", [P, more], I32)
    t.t_row_s = sb("t_row_s", [P, more], I32)
    t.next_col = sb("next_col", [P, more], I32)
    t.put_s = sb("put_s", [P, more], I32)
    t.put_t = sb("put_t", [P, more], I32)
    t.w_col = sb("w_col", [P, TILES])
    t.negdinv_col = sb("negdinv_col", [P, TILES])
    t.negdinv2_col = sb("negdinv2_col", [P, TILES])
    t.deg_col = sb("deg_col", [P, TILES])
    t.att_col = sb("att_col", [P, TILES, H])
    t.key_s = sb("key_s", [P, TILES])
    t.key_t = sb("key_t", [P, TILES])
    t.same_s = sb("same_s", [P, TILES])
    t.last_s = sb("last_s", [P, TILES])
    t.span_s = sb("span_s", [Q, 4, TILES])
    t.span_t = sb("span_t", [Q, 4, TILES])
    t.fix_edge = sb("fix_edge", [Q, 4], I32)
    t.fix_node_s = sb("fix_node_s", [Q, 4], I32)
    t.fix_node_t = sb("fix_node_t", [Q, 4], I32)
    t.row_s = dram("row_s", [10, EP])
    t.row_t = dram("row_t", [3, EP])
    t.firsts = dram("firsts", [2, TILES + 8])
    t.eq_s = dram("eq_s", [TILES // CT, P, CH])
    t.eq_t = dram("eq_t", [TILES // CT, P, CH])
    t.x_dst = dram("x_dst", [TILES // CT, P, CT * D])
    t.scores = dram("scores", [H, EP])
    t.edges_a = dram("edges_a", [EP + P, H * D])
    t.edges_b = dram("edges_b", [EP + P, H * D])
    t.sum0 = dram("sum0", [NP + 512, D + 1])
    t.sum_s = dram("sum_s", [NP + 512, D])
    t.sum_t = dram("sum_t", [NP + 512, D])
    t.lasts = dram("lasts", [TILES, D + 1])
    t.cheb_msg = dram("cheb_msg", [TILES // CT, P, CT * D])
    t.cheb_rows = dram("cheb_rows", [EP + P, D])


def segment_scan(nc, t, name, factor, adds, outs, reverse, biggest=False):
    C = len(adds)
    floor = -1e30 if biggest else 0.0
    op0, op1 = (ALU.add, ALU.max) if biggest else (ALU.mult, ALU.add)

    def way(ap):
        return ap[:, ::-1] if reverse else ap

    end = 0 if reverse else TILES - 1
    with ExitStack() as ctx:
        ends = ctx.enter_context(nc.sbuf_tensor(f"{name}_ends", [P, 2, C], F32))
        across = ctx.enter_context(nc.sbuf_tensor(f"{name}_across", [C, 4, P], F32))
        into = ctx.enter_context(nc.sbuf_tensor(f"{name}_into", [P, C], F32))
        whole = ctx.enter_context(nc.sbuf_tensor(f"{name}_whole", [P, 1], F32))
        ps = ctx.enter_context(nc.psum_tensor(f"{name}_ps", [P, 3, 512], F32))
        chain = ctx.enter_context(semaphore(nc, f"{name}_chain"))
        turned = ctx.enter_context(semaphore(nc, f"{name}_turned"))
        block = ctx.enter_context(nc.Block())

        @block.vector
        def _(dve):
            c = Chain(dve, chain)
            c.link(nc.vector.tensor_reduce(whole[:], factor, AX.X, ALU.min))
            c.link(nc.vector.tensor_scalar(ends[:, 1, :], t.ones[:, 0:C], whole[:], None, ALU.mult))
            for k in range(C):
                c.link(nc.vector.tensor_tensor_scan(way(outs[k]), way(factor), way(adds[k]), floor, op0, op1))
                c.link(nc.vector.tensor_copy(ends[:, 0, k:k + 1], outs[k][:, end:end + 1]))
            dve.wait_ge(turned, 1)
            c.link(nc.vector.tensor_copy(across[:, 0:2, :], ps[0:C, 0:2, 0:P]))
            c.link(nc.vector.tensor_tensor_scan(way(across[:, 2, :]), way(across[:, 1, :]), way(across[:, 0, :]),
                                                floor, op0, op1))
            c.link(nc.vector.memset(across[:, 3, :], floor))
            if reverse:
                c.link(nc.vector.tensor_copy(across[:, 3, 0:P - 1], across[:, 2, 1:P]))
            else:
                c.link(nc.vector.tensor_copy(across[:, 3, 1:P], across[:, 2, 0:P - 1]))
            dve.wait_ge(turned, 2)
            c.link(nc.vector.tensor_copy(into[:], ps[:, 2, 0:C]))
            for k in range(C):
                c.link(nc.vector.tensor_tensor_scan(way(outs[k]), way(factor), way(adds[k]), into[:, k:k + 1],
                                                    op0, op1))

        @block.tensor
        def _(pe):
            pe.wait_ge(chain, 2 + 2 * C)
            nc.tensor.transpose(ps[0:C, 0, 0:P], ends[:, 0, :], t.ident[:])
            nc.tensor.transpose(ps[0:C, 1, 0:P], ends[:, 1, :], t.ident[:]).then_inc(turned, 1)
            pe.wait_ge(chain, 2 + 2 * C + 4)
            nc.tensor.transpose(ps[:, 2, 0:C], across[:, 3, :], t.ident[0:C, 0:C]).then_inc(turned, 1)


def to_tiles(nc, t, name, rows, outs):
    F = len(rows)
    with ExitStack() as ctx:
        flat = ctx.enter_context(nc.sbuf_tensor(f"{name}_flat", [Q, F, 4, P], F32))
        ps = ctx.enter_context(nc.psum_tensor(f"{name}_ps", [P, 2, 512], F32))
        loaded = ctx.enter_context(semaphore(nc, f"{name}_loaded"))
        turned = ctx.enter_context(semaphore(nc, f"{name}_turned"))
        read = ctx.enter_context(semaphore(nc, f"{name}_read"))
        block = ctx.enter_context(nc.Block())

        @block.sync
        def _(sp):
            for f in range(F):
                sp.dma_start(flat[:, f], rows[f].rearrange("(c q p) -> q c p", c=4, q=Q)).then_inc(loaded, 16)

        @block.tensor
        def _(pe):
            pe.wait_ge(loaded, 16 * F)
            for f in range(F):
                if f >= 2:
                    pe.wait_ge(read, f - 1)
                for c in range(4):
                    ins = nc.tensor.transpose(ps[:, f % 2, c * Q:(c + 1) * Q], flat[:, f, c, :], t.ident[0:Q, 0:Q])
                ins.then_inc(turned, 1)

        @block.vector
        def _(dve):
            for f in range(F):
                dve.wait_ge(turned, f + 1)
                nc.vector.tensor_copy(outs[f], ps[:, f % 2, 0:TILES]).then_inc(read, 1)


def edge_fields(nc, t):
    with ExitStack() as ctx:
        def sb(name, shape, dt=F32):
            return ctx.enter_context(nc.sbuf_tensor(name, shape, dt))

        pay_s = sb("sorted_rows_s", [P, TILES, 4])
        pay_t = sb("sorted_rows_t", [P, TILES, 2])
        keys = sb("keys_with_ends", [P, 2, TILES + 2])
        tmp = sb("field_tmp", [P, 2, TILES])
        last_t = sb("last_t", [P, TILES])
        fields = sb("fields", [P, 6, TILES])
        fields_t = sb("fields_t", [P, 2, TILES])
        deg = sb("deg_scan", [P, 3, TILES])
        pick = sb("deg_pick", [P, 2, TILES])
        sums = [t.sorted_s, t.sorted_t]
        with ExitStack() as c2:
            loaded = c2.enter_context(semaphore(nc, "rows_loaded"))
            ends = c2.enter_context(semaphore(nc, "key_ends_set"))
            chain = c2.enter_context(semaphore(nc, "field_chain"))
            stored = c2.enter_context(semaphore(nc, "fields_stored"))
            block = c2.enter_context(nc.Block())

            @block.sync
            def _(sp):
                sp.dma_start(pay_s[:], t.sorted_s.rearrange("(p j) w -> p j w", p=P)).then_inc(loaded, 16)
                sp.dma_start(pay_t[:], t.sorted_t.rearrange("(p j) w -> p j w", p=P)).then_inc(loaded, 16)
                sp.wait_ge(ends, 1)
                for k in range(2):
                    rows = sums[k].rearrange("(p j) w -> p j w", p=P)
                    sp.dma_start(keys[1:P, k, 0:1], rows[0:P - 1, TILES - 1, 0:1], allow_slow_non_contiguous=True).then_inc(loaded, 16)
                    sp.dma_start(keys[0:P - 1, k, TILES + 1:TILES + 2], rows[1:P, 0, 0:1], allow_slow_non_contiguous=True).then_inc(loaded, 16)
                sp.wait_ge(chain, 18)
                for f in range(5):
                    sp.dma_start(t.row_s[f].rearrange("(p j) -> p j", p=P), fields[:, f, :]).then_inc(stored, 16)
                for f in range(2):
                    sp.dma_start(t.row_t[f].rearrange("(p j) -> p j", p=P), fields_t[:, f, :]).then_inc(stored, 16)
                sp.dma_start(t.row_t[2].rearrange("(p j) -> p j", p=P), fields[:, 5, :]).then_inc(stored, 16)
                sp.wait_ge(stored, 16 * 8)

            @block.vector
            def _(dve):
                nc.vector.memset(keys[:], -1.0).then_inc(ends, 1)
                dve.wait_ge(ends, 1)
                dve.wait_ge(loaded, 96)
                c = Chain(dve, chain)
                for k, pay in enumerate((pay_s, pay_t)):
                    c.link(nc.vector.tensor_copy(keys[:, k, 1:TILES + 1], pay[:, :, 0]))
                c.link(nc.vector.tensor_tensor(t.same_s[:], keys[:, 0, 1:TILES + 1], keys[:, 0, 0:TILES], ALU.is_equal))
                for k, last in enumerate((t.last_s, last_t)):
                    c.link(nc.vector.tensor_tensor(last[:], keys[:, k, 1:TILES + 1], keys[:, k, 2:TILES + 2], ALU.not_equal))
                    c.link(nc.vector.tensor_scalar(tmp[:, 0, :], last[:], -BIG, BIG, ALU.mult, ALU.add))
                    c.link(nc.vector.tensor_scalar(tmp[:, 1, :], keys[:, k, 1:TILES + 1], float(N), BIG, ALU.is_ge, ALU.mult))
                    c.link(nc.vector.tensor_tensor(tmp[:, 0, :], tmp[:, 0, :], tmp[:, 1, :], ALU.add))
                    c.link(nc.vector.tensor_tensor(fields[:, 4 + k, :], tmp[:, 0, :], keys[:, k, 1:TILES + 1], ALU.add))
                for f, src in enumerate((0, 1, 3, 2)):
                    ins = nc.vector.tensor_copy(fields[:, f, :], pay_s[:, :, src])
                c.link(ins)
                c.link(nc.vector.tensor_copy(fields_t[:, 0, :], pay_t[:, :, 0]))
                c.link(nc.vector.tensor_copy(fields_t[:, 1, :], pay_t[:, :, 1]))
                c.link(nc.vector.tensor_copy(deg[:, 0, :], pay_s[:, :, 3]))
                c.link(nc.vector.tensor_scalar(pick[:, 0, :], t.last_s[:], -1.0, 1.0, ALU.mult, ALU.add))

        segment_scan(nc, t, "deg_up", t.same_s[:], [deg[:, 0, :]], [deg[:, 1, :]], reverse=False)
        last_only(nc, "deg", t, [deg[:, 1, :]], [pick[:, 1, :]])
        segment_scan(nc, t, "deg_down", pick[:, 0, :], [pick[:, 1, :]], [deg[:, 2, :]], reverse=True)
        with ExitStack() as c2:
            stored = c2.enter_context(semaphore(nc, "deg_stored"))
            block = c2.enter_context(nc.Block())

            @block.sync
            def _(sp):
                sp.dma_start(t.row_s[5].rearrange("(p j) -> p j", p=P), deg[:, 2, :]).then_inc(stored, 16)
                sp.wait_ge(stored, 16)
    to_tiles(nc, t, "cols_s", [t.row_s[0], t.row_s[0], t.row_s[1], t.row_s[2], t.row_s[4], t.row_s[5]],
             [t.s_col[:, 0:TILES], t.key_s[:], t.t_col[:, 0:TILES], t.w_col[:], t.put_s[:, 0:TILES], t.deg_col[:]])
    to_tiles(nc, t, "cols_t", [t.row_t[0], t.row_t[1], t.row_t[2]],
             [t.key_t[:], t.t_row_s[:, 0:TILES], t.put_t[:, 0:TILES]])
    with ExitStack() as ctx:
        tmp = ctx.enter_context(nc.sbuf_tensor("dinv_tmp", [P, 2, TILES], F32))
        chain = ctx.enter_context(semaphore(nc, "dinv_chain"))
        root = ctx.enter_context(semaphore(nc, "dinv_root"))
        block = ctx.enter_context(nc.Block())

        @block.vector
        def _(dve):
            c = Chain(dve, chain)
            for a in (t.s_col, t.t_col, t.t_row_s, t.put_s, t.put_t, t.next_col):
                nc.vector.memset(a[:, TILES:], 0)
            inverse_root(c, nc, dve, t.deg_col[:], tmp[:, 0, :], tmp[:, 1, :], root)
            c.link(nc.vector.tensor_scalar(t.negdinv_col[:], tmp[:, 0, :], -1.0, None, ALU.mult))
            c.link(nc.vector.scalar_tensor_tensor(t.negdinv2_col[:], tmp[:, 0, :], -1.0, tmp[:, 0, :], ALU.mult, ALU.mult))

        @block.scalar
        def _(act):
            act.wait_ge(chain, 3)
            nc.scalar.activation(tmp[:, 0, :], tmp[:, 0, :], ACT.Sqrt).then_inc(root, 1)


def inverse_root(c, nc, dve, deg, out, has, root):
    c.link(nc.vector.tensor_scalar(has, deg, 0.0, None, ALU.is_gt))
    c.link(nc.vector.tensor_tensor(out, deg, has, ALU.mult))
    c.link(nc.vector.scalar_tensor_tensor(out, out, 1.0, has, ALU.add, ALU.subtract))
    dve.wait_ge(root, 1)
    c.link(nc.vector.reciprocal(out, out))
    c.link(nc.vector.tensor_tensor(out, out, has, ALU.mult))


def last_only(nc, name, t, ins, outs):
    with ExitStack() as ctx:
        block = ctx.enter_context(nc.Block())

        @block.vector
        def _(dve):
            for a, b in zip(ins, outs):
                nc.vector.tensor_tensor(b, a, t.last_s[:], ALU.mult)


def spans(nc, t, k, row, span, fix_edge, fix_node):
    n = f"span{k}_"
    with ExitStack() as ctx:
        def sb(name, shape, dt=F32):
            return ctx.enter_context(nc.sbuf_tensor(n + name, shape, dt))

        def sem(name):
            return ctx.enter_context(semaphore(nc, n + name))

        keys = sb("keys", [Q, 4, P])
        first = sb("first", [Q, 4])
        nxt = sb("next", [Q, 4])
        frow = sb("frow", [Q, TILES])
        order = sb("order", [Q, TILES], I32)
        orderf = sb("orderf", [Q, TILES])
        tile_i = sb("tile_i", [Q, 4], I32)
        tile = sb("tile", [Q, 4])
        eq = sb("eq", [Q, 4, P])
        cnt = sb("cnt", [Q, 4])
        tmp = sb("tmp", [Q, 6, 4])
        minus = sb("minus", [1, 8])
        loaded, chain, made, stored, again = sem("loaded"), sem("chain"), sem("made"), sem("stored"), sem("again")
        block = ctx.enter_context(nc.Block())

        @block.gpsimd
        def _(pool):
            nc.gpsimd.iota(order[:], [[1, TILES]], base=0, channel_multiplier=-1).then_inc(made, 1)
            nc.gpsimd.iota(tile_i[:], [[Q, 4]], base=0, channel_multiplier=1).then_inc(made, 1)

        @block.sync
        def _(sp):
            sp.dma_start(keys[:], row.rearrange("(c q p) -> q c p", c=4, q=Q)).then_inc(loaded, 16)
            sp.wait_ge(chain, 2)
            sp.dma_start(t.firsts[k, 0:TILES].rearrange("(c q) -> q c", c=4), first[:], allow_slow_non_contiguous=True).then_inc(stored, 16)
            sp.dma_start(t.firsts[k:k + 1, TILES:TILES + 8], minus[:]).then_inc(stored, 16)
            sp.wait_ge(stored, 32)
            sp.dma_start(nxt[:], t.firsts[k, 1:TILES + 1].rearrange("(c q) -> q c", c=4), allow_slow_non_contiguous=True).then_inc(again, 16)
            sp.dma_start(frow[:], t.firsts[k:k + 1, 0:TILES].partition_broadcast(Q)).then_inc(again, 16)

        @block.vector
        def _(dve):
            c = Chain(dve, chain)
            c.link(nc.vector.memset(minus[:], -1.0))
            dve.wait_ge(loaded, 16)
            c.link(nc.vector.tensor_copy(first[:], keys[:, :, 0]))
            dve.wait_ge(made, 2)
            c.link(nc.vector.tensor_copy(orderf[:], order[:]))
            c.link(nc.vector.tensor_copy(tile[:], tile_i[:]))
            c.link(nc.vector.tensor_tensor(eq[:], keys[:], first[:].unsqueeze(2).to_broadcast([Q, 4, P]), ALU.is_equal))
            c.link(nc.vector.tensor_reduce(cnt[:], eq[:], AX.X, ALU.add))
            c.link(nc.vector.scalar_tensor_tensor(tmp[:, 0, :], tile[:], float(P), cnt[:], ALU.mult, ALU.add))
            c.link(nc.vector.tensor_scalar(tmp[:, 0, :], tmp[:, 0, :], -1.0, None, ALU.add))
            if fix_edge is not None:
                c.link(nc.vector.tensor_copy(fix_edge, tmp[:, 0, :]))
            dve.wait_ge(again, 32)
            c.link(nc.vector.tensor_tensor(tmp[:, 1, :], first[:], nxt[:], ALU.is_equal))
            c.link(nc.vector.tensor_scalar(tmp[:, 2, :], cnt[:], float(P), None, ALU.is_equal))
            c.link(nc.vector.tensor_tensor(tmp[:, 1, :], tmp[:, 1, :], tmp[:, 2, :], ALU.mult))
            c.link(nc.vector.tensor_scalar(tmp[:, 2, :], first[:], float(N), None, ALU.is_ge))
            c.link(nc.vector.tensor_tensor(tmp[:, 1, :], tmp[:, 1, :], tmp[:, 2, :], ALU.max))
            c.link(nc.vector.scalar_tensor_tensor(tmp[:, 3, :], tile[:], float(NP), first[:], ALU.add, ALU.subtract))
            c.link(nc.vector.tensor_tensor(tmp[:, 3, :], tmp[:, 3, :], tmp[:, 1, :], ALU.mult))
            c.link(nc.vector.tensor_tensor(tmp[:, 3, :], tmp[:, 3, :], first[:], ALU.add))
            c.link(nc.vector.tensor_copy(fix_node, tmp[:, 3, :]))
            for g in range(4):
                c.link(nc.vector.tensor_scalar(span[:, g, :], orderf[:], float(g * Q), None, ALU.is_gt))
                c.link(nc.vector.scalar_tensor_tensor(span[:, g, :], frow[:], keys[:, g, P - 1:P], span[:, g, :],
                                                      ALU.is_equal, ALU.mult))


def weights(nc, ctx, t, w):
    def sb(name, shape, dt=F32):
        return ctx.enter_context(nc.sbuf_tensor(name, shape, dt))

    t.b_lin = w["L3_gnn_b_lin"]
    t.w_ht = sb("w_ht", [P, H * D])
    t.w_r = sb("w_r", [D, H * D])
    t.att = sb("att", [P, 3, 2, H])
    t.rel_score = sb("rel_score", [R // 2, 2, H])
    t.wo_c = sb("wo_c", [P, 2, D])
    t.dense0 = sb("dense0", [P, P])
    t.dense1 = sb("dense1", [P, P])
    t.dense2 = sb("dense2", [P, P])
    t.cheb_c = sb("cheb_c", [P, D])
    t.lin = sb("lin", [D, D])
    t.dense3 = sb("dense3", [P, P])
    t.out3 = sb("out3", [P, P])
    t.center2 = sb("center2", [P, P])
    t.rows = sb("rows", [1, 4, 2 * D])
    t.gamma1 = sb("gamma1", [P, D])
    t.beta1 = sb("beta1", [P, D])
    t.gb3 = sb("gb3", [P, 2])
    t.eps1 = sb("eps1", [P, 1])
    with ExitStack() as c2:
        def tmp(name, shape):
            return c2.enter_context(nc.sbuf_tensor(name, shape, F32))

        def sem(name):
            return c2.enter_context(semaphore(nc, name))

        stack = tmp("w_stack", [P, 8, D])
        wo = tmp("wo_raw", [P, 2, D])
        wo4 = tmp("wo_heads", [P, H, D])
        rel = tmp("rel", [R // 2, 2, D])
        relt = tmp("relt", [D, R])
        th = tmp("rel_tanh", [P, 2, R])
        mean = tmp("w_mean", [P, 16])
        brow = tmp("b_raw", [1, 4, 2 * D])
        ps = c2.enter_context(nc.psum_tensor("w_ps", [P, 4, 512], F32))
        cleared, loaded, chain, pe_done, act_done = sem("w_cleared"), sem("w_loaded"), sem("w_chain"), sem("w_pe"), sem("w_act")
        block = c2.enter_context(nc.Block())

        loads = [(t.w_ht[0:D, :], w["L0_gnn_W_h"]), (t.w_ht[D:P, :], w["L0_gnn_W_t"]), (t.w_r[:], w["L0_gnn_W_r"]),
                 (wo[:], w["L0_gnn_W_o"].rearrange("(c p) d -> p c d", p=P)),
                 (rel[:], w["L0_gnn_relation_embed"].rearrange("(c p) d -> p c d", c=2)),
                 (t.lin[:], w["L3_gnn_W_lin_T"]),
                 (t.gamma1[:], w["L1_gnn_gamma"].partition_broadcast(P)), (t.beta1[:], w["L1_gnn_beta"].partition_broadcast(P)),
                 (t.eps1[:], w["L3_gnn_eps"].partition_broadcast(P)),
                 (t.cheb_c[0:D, :], w["L2_gnn_W"][1]), (t.cheb_c[D:P, :], w["L2_gnn_W"][2])]
        for h in (0, 1):
            half = slice(h * D, (h + 1) * D)
            loads.append((wo4[half], w["L0_gnn_W_o"].rearrange("(h k) d -> k h d", h=H)))
            for n, a in enumerate((w["L1_gnn_W"], w["L2_gnn_W"][0], w["L2_gnn_W"][2], w["L3_gnn_W1_T"], w["L3_gnn_W2_T"])):
                loads.append((stack[half, n, :], a))
            for n, a in enumerate((w["L1_gnn_b"], w["L2_gnn_bias"], w["L3_gnn_b_lin"])):
                loads.append((brow[0:1, n, half], a))
            for n, a in enumerate((w["L3_gnn_gamma"], w["L3_gnn_beta"])):
                loads.append((t.gb3[half, n:n + 1], a.rearrange("o d -> d o")))
            for n, a in enumerate((w["L0_gnn_att_h"], w["L0_gnn_att_t"], w["L0_gnn_att_r"])):
                for m in range(2):
                    hh = 2 * m + h
                    loads.append((t.att[half, n, m, hh:hh + 1], a[hh:hh + 1, :].rearrange("o d -> d o")))

        @block.sync
        def _(sp):
            sp.wait_ge(cleared, 1)
            for dst, src in loads:
                sp.dma_start(dst, src, allow_slow_non_contiguous=True).then_inc(loaded, 16)

        @block.vector
        def _(dve):
            for a in (t.dense0, t.dense1, t.dense2, t.dense3, t.out3, t.center2, t.rows):
                nc.vector.memset(a[:], 0.0)
            nc.vector.memset(t.att[:], 0.0).then_inc(cleared, 1)
            dve.wait_ge(cleared, 1)
            dve.wait_ge(loaded, 16 * len(loads))
            c = Chain(dve, chain)
            c.link(nc.vector.tensor_scalar(t.eps1[:], t.eps1[:], 1.0, None, ALU.add))
            eye = stack[:, 5, :]
            c.link(nc.vector.tensor_copy(eye[0:D], t.ident[0:D, 0:D]))
            c.link(nc.vector.tensor_copy(eye[D:P], t.ident[D:P, D:P]))
            c.link(nc.vector.tensor_tensor(wo4[:, 0:2], wo4[:, 0:2], wo4[:, 2:4], ALU.add))
            c.link(nc.vector.tensor_tensor(wo4[:, 0], wo4[:, 0], wo4[:, 1], ALU.add))
            c.link(nc.vector.scalar_tensor_tensor(stack[:, 6, :], wo4[:, 0], 0.1, eye, ALU.mult, ALU.add))
            c.link(nc.vector.tensor_tensor(stack[:, 7, :], stack[:, 1, :], stack[:, 2, :], ALU.subtract))
            c.link(nc.vector.tensor_tensor(stack[:, 7, :], stack[:, 7, :], eye, ALU.add))

            def centred(dst, src, parts=P):
                n = c.n % 16
                c.link(nc.vector.tensor_reduce(mean[0:parts, n:n + 1], src, AX.X, ALU.add))
                c.link(nc.vector.tensor_scalar(mean[0:parts, n:n + 1], mean[0:parts, n:n + 1], 1.0 / D, None, ALU.mult))
                for a, b, p in dst:
                    c.link(nc.vector.tensor_scalar(a, b, mean[p, n:n + 1], None, ALU.subtract))

            up, down = slice(0, D), slice(D, P)

            def diagonal(big, s):
                return [(big[up, 0:D], stack[up, s, :], up), (big[down, D:P], stack[down, s, :], down)]

            centred(diagonal(t.dense0, 6), stack[:, 6, :])
            centred(diagonal(t.dense1, 0), stack[:, 0, :])
            centred(diagonal(t.dense2, 7), stack[:, 7, :])
            centred(diagonal(t.out3, 4), stack[:, 4, :])
            centred(diagonal(t.center2, 5), eye)
            c.link(nc.vector.tensor_copy(t.dense3[up, 0:D], stack[up, 3, :]))
            c.link(nc.vector.tensor_copy(t.dense3[down, D:P], stack[down, 3, :]))
            for m in range(2):
                centred([(t.wo_c[:, m, :], wo[:, m, :], slice(0, P))], wo[:, m, :])
            centred([(t.cheb_c[:], t.cheb_c[:], slice(0, P))], t.cheb_c[:])
            for n in range(2):
                for h in (0, 1):
                    centred([(t.rows[0:1, n, h * D:(h + 1) * D], brow[0:1, n, h * D:(h + 1) * D], slice(0, 1))],
                            brow[0:1, n, h * D:(h + 1) * D], 1)
            c.link(nc.vector.tensor_copy(t.rows[0:1, 2, :], brow[0:1, 2, :]))
            dve.wait_ge(pe_done, 1)
            nc.vector.tensor_copy(relt[:], ps[0:D, 0, 0:R]).then_inc(pe_done, 1)
            dve.wait_ge(pe_done, 4)
            for m in range(2):
                ins = nc.vector.tensor_copy(t.rel_score[:, m, :], ps[0:R // 2, 3, m * H:(m + 1) * H])

        @block.tensor
        def _(pe):
            pe.wait_ge(loaded, 16 * len(loads))
            for m in range(2):
                ins = nc.tensor.transpose(ps[0:D, 0, m * 100:(m + 1) * 100], rel[:, m, :], t.ident[0:R // 2, 0:R // 2])
            ins.then_inc(pe_done, 1)
            pe.wait_ge(pe_done, 2)
            for m in range(2):
                ins = nc.tensor.matmul(ps[:, 1 + m, 0:R], t.w_r[:, m * P:(m + 1) * P], relt[:], start=True, stop=True)
            ins.then_inc(pe_done, 1)
            pe.wait_ge(act_done, 1)
            for r in range(2):
                for m in range(2):
                    ins = nc.tensor.matmul(ps[0:R // 2, 3, r * H:(r + 1) * H], th[:, m, r * 100:(r + 1) * 100],
                                           t.att[:, 2, m, :], start=m == 0, stop=m == 1, skip_group_check=True)
            ins.then_inc(pe_done, 1)

        @block.scalar
        def _(act):
            act.wait_ge(pe_done, 3)
            for m in range(2):
                ins = nc.scalar.activation(th[:, m, :], ps[:, 1 + m, 0:R], ACT.Tanh)
            ins.then_inc(act_done, 1)


def edge_scores(nc, t, x):
    with ExitStack() as ctx:
        def sb(name, shape, dt=F32):
            return ctx.enter_context(nc.sbuf_tensor("sc_" + name, shape, dt))

        def sem(name):
            return ctx.enter_context(semaphore(nc, "sc_" + name))

        def sems(name):
            return [sem(name + str(u)) for u in range(2)]

        idx = sb("idx", [P, 2, 2, CT], I32)
        got = sb("got", [P, 2, CT, 2, D])
        last_row = sb("last_row", [P, CT], I32)
        eq_rows, eq = sb("eq_rows", [P, 2, CT, P]), sb("eq", [P, 2, CT, P])
        orders = ((t.row_s[0:1, :], t.key_s, t.eq_s), (t.row_t[0:1, :], t.key_t, t.eq_t))
        xt = sb("xt", [P, 2, CH])
        th = sb("tanh", [P, 2, CH])
        types = sb("types", [R // 2, 2, CH])
        relid = sb("relid", [R // 2, 2])
        relid_i = sb("relid_i", [R // 2, 2], I32)
        oh = sb("relhot", [R // 2, 2, 2, CH])
        raw = sb("raw", [H, 2, CH])
        leaky = sb("leaky", [H, 2, CH])
        psx = ctx.enter_context(nc.psum_tensor("sc_psx", [P, 2, 512], F32))
        psz = ctx.enter_context(nc.psum_tensor("sc_psz", [P, 2, 2, 512], F32))
        pss = ctx.enter_context(nc.psum_tensor("sc_pss", [P, 2, 512], F32))
        idx_ready, gathered, turned, xt_ready = sems("idx_ready"), sems("gathered"), sems("turned"), sems("xt_ready")
        z_ready, tanh_ready, tanh_used = sems("z_ready"), sems("tanh_ready"), sems("tanh_used")
        types_in, hot, summed, raw_ready = sems("types_in"), sems("hot"), sems("summed"), sems("raw_ready")
        leaky_ready, stored, kept, passed = sems("leaky_ready"), sems("stored"), sems("kept"), sem("passed")
        ids, sp_passed = sem("ids"), sem("sp_passed")
        followed, followed_kept = sem("followed"), sem("followed_kept")
        eq_in, eq_made, eq_stored = sems("eq_in"), sems("eq_made"), sems("eq_stored")
        block = ctx.enter_context(nc.Block())
        parts = ((0, 512), (512, CH))

        @block.gpsimd
        def _(pool):
            nc.gpsimd.iota(relid_i[:], [[R // 2, 2]], base=0, channel_multiplier=1).then_inc(ids, 1)
            @repeat(pool, PAIRS)
            def _(i):
                for u in range(2):
                    pool.wait_ge(idx_ready[u], i + 1)
                    if u == 0:
                        wait(pool, followed_kept, i)
                        pool.sem_inc(passed, 1)
                        for c in range(CT):
                            pool.indirect_dma_start(out=last_row[:, c:c + 1], out_offset=None, in_=t.last_of_node,
                                                    in_offset=bass.IndirectOffsetOnAxis(idx[:, u, 1, c:c + 1], 0)
                                                    ).then_inc(followed, 16)
                    wait(pool, turned[u], i)
                    wait(pool, kept[u], i * 16)
                    pool.sem_inc(passed, 1)
                    for c in range(CT):
                        for g in range(2):
                            pool.indirect_dma_start(out=got[:, u, c, g, :], out_offset=None, in_=x,
                                                    in_offset=bass.IndirectOffsetOnAxis(idx[:, u, g, c:c + 1], 0)
                                                    ).then_inc(gathered[u], 16)

        @block.sync
        def _(sp):
            @skewed(sp, PAIRS, 2)
            def _(ago):
                for i, u in ago(0):
                    wait(sp, hot[u], i)
                    sp.sem_inc(sp_passed, 1)
                    sp.dma_start(types[:, u, :], t.row_s[3:4, bass.ds((i * 2 + u) * CH, CH)].partition_broadcast(R // 2)
                                 .rearrange("q o e -> q (o e)")).then_inc(types_in[u], 16)
                    for k, (row, _, _) in enumerate(orders):
                        wait(sp, eq_made[k], i * 2 + u)
                        sp.sem_inc(sp_passed, 1)
                        sp.dma_start(eq_rows[:, k], row[:, bass.ds((i * 2 + u) * CH, CH)].partition_broadcast(P)
                                     .rearrange("q o (c p) -> q (o c) p", c=CT)).then_inc(eq_in[k], 16)
                for i, u in ago(1):
                    for k, (_, _, out) in enumerate(orders):
                        sp.wait_ge(eq_made[k], i * 2 + u + 1)
                        sp.sem_inc(sp_passed, 1)
                        sp.dma_start(out[bass.ds(i * 2 + u, 1)].rearrange("o p c -> p (o c)"),
                                     eq[:, k].rearrange("p c e -> p (c e)")).then_inc(eq_stored[k], 16)
                for i, u in ago(0):
                    sp.wait_ge(gathered[u], (i + 1) * 32 * CT)
                    sp.sem_inc(sp_passed, 1)
                    sp.dma_start(t.x_dst[bass.ds(i * 2 + u, 1)].rearrange("o p (c d) -> p (o c) d", c=CT),
                                 got[:, u, :, 1, :]).then_inc(kept[u], 16)
                for i, u in ago(2):
                    sp.wait_ge(leaky_ready[u], i + 1)
                    sp.sem_inc(sp_passed, 1)
                    sp.dma_start(t.scores[:, bass.ds((i * 2 + u) * CH, CH)], leaky[:, u, :]).then_inc(stored[u], 16)
            for k in range(2):
                sp.wait_ge(eq_stored[k], 2 * PAIRS * 16)
            for u in range(2):
                sp.wait_ge(stored[u], PAIRS * 16)
                sp.wait_ge(kept[u], PAIRS * 16)

        @block.scalar
        def _(act):
            def indices(u, at):
                nc.scalar.copy(idx[:, u, 0, :], t.s_col[:, at])
                nc.scalar.copy(idx[:, u, 1, :], t.t_col[:, at]).then_inc(idx_ready[u], 1)

            for u in range(2):
                indices(u, slice(u * CT, (u + 1) * CT))

            @skewed(act, PAIRS, 1)
            def _(ago):
                for i, u in ago(0):
                    if u == 0:
                        act.wait_ge(followed, (i + 1) * 16 * CT)
                    act.wait_ge(gathered[u], (i + 1) * 32 * CT)
                    indices(u, bass.ds((i * 2 + 2 + u) * CT, CT))
                for i, u in ago(1):
                    for q in range(4):
                        z, n = q % 2, (i * 2 + u) * 2 + q // 2
                        act.wait_ge(z_ready[z], n + 1)
                        wait(act, tanh_used[z], n)
                        for b, (lo, hi) in enumerate(parts):
                            ins = nc.scalar.activation(th[:, z, lo:hi], psz[:, z, b, 0:hi - lo], ACT.Tanh)
                        ins.then_inc(tanh_ready[z], 1)
                    act.wait_ge(summed[u], i + 1)
                    wait(act, leaky_ready[u], i)
                    for b, (lo, hi) in enumerate(parts):
                        ins = nc.scalar.copy(raw[:, u, lo:hi], pss[0:H, b, 0:hi - lo])
                    ins.then_inc(raw_ready[u], 1)

        @block.vector
        def _(dve):
            dve.wait_ge(ids, 1)
            nc.vector.tensor_copy(relid[:], relid_i[:]).then_inc(ids, 1)
            dve.wait_ge(ids, 2)

            @skewed(dve, PAIRS, 1)
            def _(ago):
                for i, u in ago(0):
                    dve.wait_ge(turned[u], i + 1)
                    wait(dve, summed[u], i)
                    for b, (lo, hi) in enumerate(parts):
                        ins = nc.vector.tensor_copy(xt[:, u, lo:hi], psx[:, b, 0:hi - lo])
                    ins.then_inc(xt_ready[u], 1)
                    dve.wait_ge(types_in[u], (i + 1) * 16)
                    for r in range(2):
                        ins = nc.vector.tensor_scalar(oh[:, u, r, :], types[:, u, :], relid[:, r:r + 1], None, ALU.is_equal)
                    ins.then_inc(hot[u], 1)
                    if u == 0:
                        dve.wait_ge(followed, (i + 1) * 16 * CT)
                        nc.vector.tensor_copy(t.next_col[:, bass.ds(i * 2 * CT, CT)], last_row[:]).then_inc(followed_kept, 1)
                    for k, (_, col, _) in enumerate(orders):
                        dve.wait_ge(eq_in[k], (i * 2 + u + 1) * 16)
                        wait(dve, eq_stored[k], (i * 2 + u) * 16)
                        nc.vector.tensor_tensor(eq[:, k], eq_rows[:, k],
                                                col[:, bass.ds((i * 2 + u) * CT, CT)].unsqueeze(2).to_broadcast([P, CT, P]),
                                                ALU.is_equal).then_inc(eq_made[k], 1)
                for i, u in ago(1):
                    dve.wait_ge(raw_ready[u], i + 1)
                    wait(dve, stored[u], i * 16)
                    nc.vector.scalar_tensor_tensor(leaky[:, u, :], raw[:, u, :], 0.01, raw[:, u, :],
                                                   ALU.mult, ALU.max).then_inc(leaky_ready[u], 1)

        @block.tensor
        def _(pe):
            @skewed(pe, PAIRS, 1)
            def _(ago):
                for i, u in ago(0):
                    pe.wait_ge(gathered[u], (i + 1) * 32 * CT)
                    wait(pe, xt_ready[1 - u], i + u)
                    for c in range(CT):
                        ins = nc.tensor.transpose(psx[:, c // 4, c % 4 * P:(c % 4 + 1) * P],
                                                  got[:, u, c].rearrange("p g d -> p (g d)"), t.ident[:])
                    ins.then_inc(turned[u], 1)
                for i, u in ago(1):
                    pe.wait_ge(xt_ready[u], i + 1)

                    def project(q):
                        g, m, z = q // 2, q % 2, q % 2
                        half = slice(g * D, (g + 1) * D)
                        wait(pe, tanh_ready[z], (i * 2 + u) * 2 + q // 2)
                        for b, (lo, hi) in enumerate(parts):
                            ins = nc.tensor.matmul(psz[:, z, b, 0:hi - lo], t.w_ht[half, m * P:(m + 1) * P],
                                                   xt[half, u, lo:hi], start=True, stop=True)
                        ins.then_inc(z_ready[z], 1)

                    def score(q):
                        g, m, z = q // 2, q % 2, q % 2
                        pe.wait_ge(tanh_ready[z], (i * 2 + u) * 2 + q // 2 + 1)
                        if q == 0:
                            wait(pe, raw_ready[1 - u], i + u)
                        for b, (lo, hi) in enumerate(parts):
                            ins = nc.tensor.matmul(pss[0:H, b, 0:hi - lo], t.att[:, g, m, :], th[:, z, lo:hi],
                                                   start=q == 0, stop=False, skip_group_check=True)
                        ins.then_inc(tanh_used[z], 1)

                    project(0)
                    project(1)
                    score(0)
                    project(2)
                    score(1)
                    project(3)
                    score(2)
                    score(3)
                    pe.wait_ge(hot[u], i + 1)
                    for b, (lo, hi) in enumerate(parts):
                        for r in range(2):
                            ins = nc.tensor.matmul(pss[0:H, b, 0:hi - lo], t.rel_score[:, r, :], oh[:, u, r, lo:hi],
                                                   start=False, stop=r == 1, skip_group_check=True)
                    ins.then_inc(summed[u], 1)


def edge_softmax(nc, t):
    with ExitStack() as ctx:
        def sb(name, shape, dt=F32):
            return ctx.enter_context(nc.sbuf_tensor("sm_" + name, shape, dt))

        s = sb("scores", [P, H, TILES])
        up = sb("up", [P, H, TILES])
        pick = sb("pick", [P, H, TILES])
        tot = sb("total", [P, H, TILES])
        e = sb("exp", [P, H, TILES])
        goes_on = sb("goes_on", [P, TILES])
        penalty = sb("penalty", [P, TILES])

        def each(a):
            return [a[:, h, :] for h in range(H)]

        last = t.last_s[:].unsqueeze(1).to_broadcast([P, H, TILES])
        with ExitStack() as c2:
            loaded = c2.enter_context(semaphore(nc, "sm_loaded"))
            block = c2.enter_context(nc.Block())

            @block.sync
            def _(sp):
                sp.dma_start(s[:], t.scores.rearrange("h (p j) -> p h j", p=P)).then_inc(loaded, 16)
                sp.wait_ge(loaded, 16)

            @block.vector
            def _(dve):
                nc.vector.tensor_scalar(goes_on[:], t.last_s[:], -1.0, 1.0, ALU.mult, ALU.add)
                nc.vector.tensor_scalar(penalty[:], t.same_s[:], -1.0, 1e30, ALU.add, ALU.mult)
        segment_scan(nc, t, "max_up", penalty[:], each(s), each(up), reverse=False, biggest=True)
        with nc.Block() as block:
            @block.vector
            def _(dve):
                nc.vector.tensor_tensor(pick[:], up[:], last, ALU.mult)
        segment_scan(nc, t, "max_down", goes_on[:], each(pick), each(tot), reverse=True)
        with ExitStack() as c2:
            ready = c2.enter_context(semaphore(nc, "sm_ready"))
            block = c2.enter_context(nc.Block())

            @block.vector
            def _(dve):
                nc.vector.tensor_tensor(s[:], s[:], tot[:], ALU.subtract).then_inc(ready, 1)

            @block.scalar
            def _(act):
                act.wait_ge(ready, 1)
                nc.scalar.activation(e[:], s[:], ACT.Exp)
        segment_scan(nc, t, "sum_up", t.same_s[:], each(e), each(up), reverse=False)
        with nc.Block() as block:
            @block.vector
            def _(dve):
                nc.vector.tensor_tensor(pick[:], up[:], last, ALU.mult)
        segment_scan(nc, t, "sum_down", goes_on[:], each(pick), each(tot), reverse=True)
        with ExitStack() as c2:
            chain = c2.enter_context(semaphore(nc, "sm_chain"))
            stored = c2.enter_context(semaphore(nc, "sm_stored"))
            block = c2.enter_context(nc.Block())

            @block.vector
            def _(dve):
                c = Chain(dve, chain)
                c.link(nc.vector.tensor_scalar(tot[:], tot[:], 1e-16, None, ALU.add))
                c.link(nc.vector.reciprocal(tot[:], tot[:]))
                c.link(nc.vector.scalar_tensor_tensor(tot[:], e[:], 0.9, tot[:], ALU.mult, ALU.mult))

            @block.sync
            def _(sp):
                sp.wait_ge(chain, 3)
                sp.dma_start(t.row_s[6:10].rearrange("h (p j) -> p h j", p=P), tot[:]).then_inc(stored, 16)
                sp.wait_ge(stored, 16)
    to_tiles(nc, t, "att_cols", [t.row_s[6 + h] for h in range(H)], [t.att_col[:, :, h] for h in range(H)])


def edge_pass(nc, t, name, kind, eq, table=None, idx=None, put=None, target=None):
    heads = kind in ("heads", "heads_out")
    W = H * D if heads else D
    G = table.shape[1] if table is not None else 0
    O = target.shape[1]
    turned = kind in ("heads_out", "cheb2")
    C = {"heads_out": 2, "cheb2": 1}.get(kind, 0)
    M = C * P if turned else W
    nodes = put is not None
    side = t.x_dst if heads else t.cheb_msg if kind == "cheb2" else None
    own_msg = kind != "plain"
    wide = kind == "heads"
    with ExitStack() as ctx:
        def sb(n, shape, dt=F32):
            return ctx.enter_context(nc.sbuf_tensor(f"{name}_{n}", shape, dt))

        def sem(n):
            return ctx.enter_context(semaphore(nc, f"{name}_{n}"))

        def sems(n):
            return [sem(n + str(u)) for u in range(2)]

        def psum(n, shape):
            return ctx.enter_context(nc.psum_tensor(f"{name}_{n}", shape, F32))

        eqs = sb("eq", [P, 2, CT, P])
        out = sb("out", [P, 2, CT, O])
        msg = sb("msg", [P, 2, CT, M]) if own_msg else None
        if table is not None:
            gidx = sb("gather_idx", [P, 2, CT], I32)
            got = sb("got", [P, 2, CT, G])
        follows = table is None
        if follows:
            cut = ((0, CT // 2 + 1), (CT // 2 + 1, CT))
            fidx, last_row = sb("follow_idx", [P, CT], I32), sb("last_row", [P, CT], I32)
            fidx_ready, followed = sems("fidx_ready"), sems("followed")
        if nodes:
            pidx = sb("put_idx", [P, 2, CT], I32)
        if side is not None:
            sides = sb("side", [P, 2, CT, D])
        if turned:
            rt = sb("rt", [P, C, CH])
            ps_rt = psum("ps_rt", [P, C, 2, 512])
        if kind == "gin":
            gt = sb("gt", [D + 1, 2, CH])
            lin = sb("lin", [D + 1, D])
            ps_gt = psum("ps_gt", [P, 2, 512])
            ps_lin = psum("ps_lin", [P, 512])
        ps_o = psum("ps_out", [P, 2, 4 if wide else 1, 512])

        idx_ready, gathered, msg_ready = sems("idx_ready"), sems("gathered"), sems("msg_ready")
        eq_in, side_in, summed, out_ready = sems("eq_in"), sems("side_in"), sems("summed"), sems("out_ready")
        stored, lasts_stored, msg_kept = sems("stored"), sems("lasts_stored"), sems("msg_kept")
        put_ready, added = sems("put_ready"), sem("added")
        rt_done, rt_read, gt_done, gt_read, lin_done = sem("rt_done"), sem("rt_read"), sem("gt_done"), sem("gt_read"), sem("lin_done")
        pool_passed, sp_passed, pe_passed, setup = sem("pool_passed"), sem("sp_passed"), sem("pe_passed"), sem("setup")
        block = ctx.enter_context(nc.Block())
        late = 1 if turned else 0
        rows_of = {u: [out[:, u, c, :] for c in range(CT)] for u in range(2)}
        used = summed if not turned else rt_done
        parts = ((0, 512), (512, CH))

        def used_up(i, u):
            return (rt_done, i * 2 + u) if turned else (summed[u], i)

        @block.gpsimd
        def _(pool):
            def gather(i, u):
                pool.wait_ge(idx_ready[u], i + 1)
                if heads:
                    wait(pool, added, i * 4 + u * 2 - 2)
                elif own_msg:
                    wait(pool, msg_ready[u] if kind != "gin" else lin_done, i if kind != "gin" else i * 2 + u)
                else:
                    wait(pool, summed[u], i)
                pool.sem_inc(pool_passed, 1)
                for c in range(CT):
                    pool.indirect_dma_start(out=got[:, u, c, :], out_offset=None, in_=table,
                                            in_offset=bass.IndirectOffsetOnAxis(gidx[:, u, c:c + 1], 0)
                                            ).then_inc(gathered[u], 16)

            def scatter(i, u):
                pool.wait_ge(put_ready[u], i + 1)
                pool.wait_ge(out_ready[u], i + 1)
                pool.sem_inc(pool_passed, 1)
                for c in range(CT):
                    pool.indirect_dma_start(out=target, out_offset=bass.IndirectOffsetOnAxis(pidx[:, u, c:c + 1], 0),
                                            in_=rows_of[u][c], in_offset=None, bounds_check=NP - 1,
                                            oob_is_err=False).then_inc(stored[u], 16)

            if follows:
                @repeat(pool, PAIRS)
                def _(i):
                    for u, (lo, hi) in enumerate(cut):
                        pool.wait_ge(fidx_ready[u], i + 1)
                        pool.sem_inc(pool_passed, 1)
                        for c in range(lo, hi):
                            pool.indirect_dma_start(out=last_row[:, c:c + 1], out_offset=None, in_=t.last_of_node,
                                                    in_offset=bass.IndirectOffsetOnAxis(fidx[:, c:c + 1], 0)
                                                    ).then_inc(followed[u], 16)

            if table is not None:
                lag = (2 if turned else 1) if nodes else 0

                @skewed(pool, PAIRS, lag)
                def _(ago):
                    for i, u in ago(0):
                        gather(i, u)
                    if nodes:
                        for i, u in ago(lag):
                            scatter(i, u)
            if nodes:
                for u in range(2):
                    pool.wait_ge(stored[u], PAIRS * 16 * CT)

        @block.sync
        def _(sp):
            @repeat(sp, PAIRS)
            def _(i):
                for u in range(2):
                    at = bass.ds(i * 2 + u, 1)
                    if side is not None:
                        wait(sp, msg_ready[u], i)
                        sp.sem_inc(sp_passed, 1)
                        sp.dma_start(sides[:, u].rearrange("p c d -> p (c d)"), side[at].rearrange("o p e -> p (o e)")).then_inc(side_in[u], 16)
                    wait(sp, *used_up(i, u))
                    sp.sem_inc(sp_passed, 1)
                    sp.dma_start(eqs[:, u].rearrange("p c e -> p (c e)"), eq[at].rearrange("o p e -> p (o e)")).then_inc(eq_in[u], 16)

        def out_waits(eng, i, u):
            wait(eng, stored[u], i * 16 * (CT if nodes else 1))
            if nodes:
                wait(eng, lasts_stored[u], i * 16)

        @block.vector
        def _(dve):
            if kind == "gin":
                nc.vector.memset(gt[:], 1.0)
                nc.vector.tensor_copy(lin[0:D, :], t.lin[:]).then_inc(setup, 1)
                dve.wait_ge(setup, 17)
            if follows:
                for u, (lo, hi) in enumerate(cut):
                    nc.vector.tensor_copy(fidx[:, lo:hi], t.t_col[:, CT + lo:CT + hi]).then_inc(fidx_ready[u], 1)

            @skewed(dve, PAIRS, late)
            def _(ago):
                for i, u in ago(0):
                    at = bass.ds((i * 2 + u) * CT, CT)
                    if table is not None:
                        dve.wait_ge(gathered[u], (i + 1) * 16 * CT)
                    if side is not None:
                        dve.wait_ge(side_in[u], (i + 1) * 16)
                    if own_msg and kind != "gin":
                        wait(dve, *used_up(i, u))
                    if heads:
                        def four(a):
                            return a.unsqueeze(2).to_broadcast([P, CT, H, D])

                        att = t.att_col[:, at, :].unsqueeze(3).to_broadcast([P, CT, H, D])
                        m = msg[:, u].rearrange("p c (h d) -> p c h d", h=H)
                        if table is None:
                            nc.vector.tensor_tensor(m, four(sides[:, u]), att, ALU.mult).then_inc(msg_ready[u], 1)
                            lo, hi = cut[u]
                            dve.wait_ge(followed[u], (i + 1) * 16 * (hi - lo))
                            nc.vector.tensor_copy(t.next_col[:, bass.ds((i * 2 + 1) * CT + lo, hi - lo)], last_row[:, lo:hi])
                            nc.vector.tensor_copy(fidx[:, lo:hi], t.t_col[:, bass.ds((i * 2 + 3) * CT + lo, hi - lo)]
                                                  ).then_inc(fidx_ready[u], 1)
                        else:
                            g = got[:, u].rearrange("p c (h d) -> p c h d", h=H)
                            nc.vector.tensor_scalar(sides[:, u], sides[:, u], 0.1, None, ALU.mult).then_inc(added, 1)
                            dve.wait_ge(added, (i * 2 + u) * 2 + 1)
                            nc.vector.tensor_tensor(m, four(sides[:, u]), g, ALU.add).then_inc(added, 1)
                            wait(dve, added, (i * 2 + u) * 2 + 2)
                            nc.vector.tensor_tensor(m, m, att, ALU.mult).then_inc(msg_ready[u], 1)
                    if kind == "cheb1":
                        wait(dve, msg_kept[u], i * 16)
                        nc.vector.tensor_tensor(msg[:, u], got[:, u], t.w_col[:, at].unsqueeze(2).to_broadcast([P, CT, D]),
                                                ALU.mult).then_inc(msg_ready[u], 1)
                    if kind == "cheb2":
                        nc.vector.tensor_copy(msg[:, u, :, 0:D], sides[:, u])
                        nc.vector.scalar_tensor_tensor(msg[:, u, :, D:P], got[:, u], 2.0,
                                                       t.w_col[:, at].unsqueeze(2).to_broadcast([P, CT, D]),
                                                       ALU.mult, ALU.mult).then_inc(msg_ready[u], 1)
                    if kind == "gin":
                        dve.wait_ge(gt_done, i * 2 + u + 1)
                        wait(dve, lin_done, i * 2)
                        for b, (lo, hi) in enumerate(parts):
                            ins = nc.vector.tensor_copy(gt[0:D, u, lo:hi], ps_gt[0:D, b, 0:hi - lo])
                        ins.then_inc(gt_read, 1)
                if not wide:
                    for i, u in ago(late):
                        at = bass.ds((i * 2 + u) * CT, CT)
                        dve.wait_ge(summed[u], i + 1)
                        out_waits(dve, i, u)
                        sums = ps_o[:, u, 0, 0:CT * D].rearrange("p (c d) -> p c d", c=CT)
                        if kind in ("cheb1", "cheb2"):
                            col = t.negdinv2_col if kind == "cheb1" else t.negdinv_col
                            nc.vector.tensor_tensor(out[:, u, :, 0:D], sums, col[:, at].unsqueeze(2).to_broadcast([P, CT, D]),
                                                    ALU.mult).then_inc(out_ready[u], 1)
                        else:
                            if O > D:
                                nc.vector.tensor_copy(out[:, u, :, D], t.deg_col[:, at])
                            nc.vector.tensor_copy(out[:, u, :, 0:D], sums).then_inc(out_ready[u], 1)

        @block.scalar
        def _(act):
            if kind == "gin":
                act.dma_start(lin[D:D + 1, :], t.b_lin).then_inc(setup, 16)
            if table is not None:
                for u in range(2):
                    nc.scalar.copy(gidx[:, u], idx[:, u * CT:(u + 1) * CT]).then_inc(idx_ready[u], 1)
            @repeat(act, PAIRS)
            def _(i):
                for u in range(2):
                    at = bass.ds((i * 2 + u) * CT, CT)
                    if table is not None:
                        act.wait_ge(gathered[u], (i + 1) * 16 * CT)
                        nc.scalar.copy(gidx[:, u], idx[:, bass.ds((i * 2 + 2 + u) * CT, CT)]).then_inc(idx_ready[u], 1)
                    if nodes:
                        wait(act, stored[u], i * 16 * CT)
                        nc.scalar.copy(pidx[:, u], put[:, at]).then_inc(put_ready[u], 1)
                    if kind == "cheb1":
                        act.wait_ge(msg_ready[u], i + 1)
                        act.dma_start(t.cheb_msg[bass.ds(i * 2 + u, 1)].rearrange("o p e -> p (o e)"),
                                      msg[:, u].rearrange("p c d -> p (c d)")).then_inc(msg_kept[u], 16)
                    if kind == "gin":
                        act.wait_ge(lin_done, i * 2 + u + 1)
                        wait(act, summed[u], i)
                        nc.scalar.activation(msg[:, u].rearrange("p c d -> p (c d)"), ps_lin[:, 0:CT * D],
                                             ACT.Relu).then_inc(msg_ready[u], 1)
                    if turned:
                        act.wait_ge(rt_done, i * 2 + u + 1)
                        wait(act, summed[1 - u], i + u)
                        for m in range(C):
                            for b, (lo, hi) in enumerate(parts):
                                ins = nc.scalar.copy(rt[:, m, lo:hi], ps_rt[:, m, b, 0:hi - lo])
                        ins.then_inc(rt_read, 1)
                    if wide:
                        act.wait_ge(summed[u], i + 1)
                        out_waits(act, i, u)
                        nc.scalar.copy(out[:, u].rearrange("p c w -> p (c w)"),
                                       ps_o[:, u].rearrange("p b w -> p (b w)")[:, 0:CT * W]).then_inc(out_ready[u], 1)
                    act.wait_ge(out_ready[u], i + 1)
                    if nodes:
                        act.dma_start(t.lasts[at, :].rearrange("(o c) w -> o c w", o=1)[:, :, 0:D], out[P - 1:P, u, :, 0:D]).then_inc(lasts_stored[u], 16)
                    else:
                        act.dma_start(target[bass.ds((i * 2 + u) * CH, CH), :].rearrange("(c p) w -> p c w", p=P),
                                      out[:, u]).then_inc(stored[u], 16)
            for u in range(2):
                if nodes:
                    act.wait_ge(lasts_stored[u], PAIRS * 16)
                else:
                    act.wait_ge(stored[u], PAIRS * 16)
                if kind == "cheb1":
                    act.wait_ge(msg_kept[u], PAIRS * 16)

        @block.tensor
        def _(pe):
            if kind == "gin":
                pe.wait_ge(setup, 17)
            @repeat(pe, PAIRS)
            def _(i):
                for u in range(2):
                    if kind == "gin":
                        pe.wait_ge(gathered[u], (i + 1) * 16 * CT)
                        wait(pe, gt_read, i * 2 + u)
                        pe.sem_inc(pe_passed, 1)
                        for c in range(CT):
                            ins = nc.tensor.transpose(ps_gt[0:D, c // 4, c % 4 * P:(c % 4 + 1) * P], got[:, u, c, :], t.ident[:])
                        ins.then_inc(gt_done, 1)
                        pe.wait_ge(gt_read, i * 2 + u + 1)
                        wait(pe, msg_ready[1 - u], i + u)
                        for c in range(CT):
                            ins = nc.tensor.matmul(ps_lin[:, c * D:(c + 1) * D], gt[:, u, c * P:(c + 1) * P], lin[:],
                                                   start=True, stop=True)
                        ins.then_inc(lin_done, 1)
                    if own_msg:
                        pe.wait_ge(msg_ready[u], i + 1)
                    else:
                        pe.wait_ge(gathered[u], (i + 1) * 16 * CT)
                    pe.wait_ge(eq_in[u], (i + 1) * 16)
                    src = msg if own_msg else got
                    if turned:
                        wait(pe, rt_read, i * 2 + u)
                        for m in range(C):
                            for c in range(CT):
                                ins = nc.tensor.matmul(ps_rt[:, m, c // 4, c % 4 * P:(c % 4 + 1) * P],
                                                       src[:, u, c, m * P:(m + 1) * P], eqs[:, u, c, :], start=True, stop=True)
                        ins.then_inc(rt_done, 1)
                        pe.wait_ge(rt_read, i * 2 + u + 1)
                        wait(pe, out_ready[u], i)
                        for c in range(CT):
                            for m in range(C):
                                rhs = t.wo_c[:, m, :] if kind == "heads_out" else t.cheb_c[:]
                                ins = nc.tensor.matmul(ps_o[:, u, 0, c * D:(c + 1) * D], rt[:, m, c * P:(c + 1) * P], rhs,
                                                       start=m == 0, stop=m == C - 1, skip_group_check=True)
                        ins.then_inc(summed[u], 1)
                    else:
                        wait(pe, out_ready[u], i)
                        flat = ps_o[:, u].rearrange("p b w -> p (b w)")
                        for c in range(CT):
                            ins = nc.tensor.matmul(flat[:, c * W:(c + 1) * W], eqs[:, u, c, :], src[:, u, c, :], start=True, stop=True)
                        ins.then_inc(summed[u], 1)


def carry_spans(nc, t, name, span, lasts, width, target, rows):
    W = target.shape[1]
    with ExitStack() as ctx:
        ends = ctx.enter_context(nc.sbuf_tensor(f"{name}_ends", [Q, 4, width], F32))
        add = ctx.enter_context(nc.sbuf_tensor(f"{name}_add", [Q, 4, W], F32))
        ps = ctx.enter_context(nc.psum_tensor(f"{name}_ps", [P, 4, 512], F32))
        loaded = ctx.enter_context(semaphore(nc, f"{name}_loaded"))
        summed = ctx.enter_context(semaphore(nc, f"{name}_summed"))
        ready = ctx.enter_context(semaphore(nc, f"{name}_ready"))
        added = ctx.enter_context(semaphore(nc, f"{name}_added"))
        block = ctx.enter_context(nc.Block())

        @block.sync
        def _(sp):
            sp.dma_start(ends[:], lasts).then_inc(loaded, 16)

        @block.tensor
        def _(pe):
            pe.wait_ge(loaded, 16)
            for g in range(4):
                for e in range(g + 1):
                    ins = nc.tensor.matmul(ps[0:Q, g, 0:width], span[:, e, g * Q:(g + 1) * Q], ends[:, e, :],
                                           start=e == 0, stop=e == g)
                ins.then_inc(summed, 1)

        @block.vector
        def _(dve):
            if W > width:
                nc.vector.memset(add[:, :, width:], 0.0)
            for g in range(4):
                dve.wait_ge(summed, g + 1)
                nc.vector.tensor_copy(add[:, g, 0:width], ps[0:Q, g, 0:width]).then_inc(ready, 1)

        @block.gpsimd
        def _(pool):
            for g in range(4):
                pool.wait_ge(ready, g + 1)
                pool.indirect_dma_start(out=target, out_offset=bass.IndirectOffsetOnAxis(rows[:, g:g + 1], 0),
                                        in_=add[:, g, :], in_offset=None, compute_op=ALU.add).then_inc(added, 16)
            pool.wait_ge(added, 64)


def attention(nc, t):
    recycle(nc)
    tables = (t.edges_a, t.edges_b)

    def tile_ends(tab):
        return tab[0:EP, :].rearrange("(c q p) w -> p q c w", c=4, q=Q)[P - 1]

    edge_pass(nc, t, "hop0", "heads", t.eq_s, target=tables[0])
    carry_spans(nc, t, "carry0", t.span_s, tile_ends(tables[0]), H * D, tables[0], t.fix_edge)
    for k in range(1, 4):
        recycle(nc)
        a, b = tables[(k - 1) % 2], tables[k % 2]
        edge_pass(nc, t, f"hop{k}", "heads", t.eq_s, table=a, idx=t.next_col, target=b)
        carry_spans(nc, t, f"carry{k}", t.span_s, tile_ends(b), H * D, b, t.fix_edge)
    recycle(nc)
    edge_pass(nc, t, "hop4", "heads_out", t.eq_s, table=tables[1], idx=t.next_col, put=t.put_s, target=t.sum0)
    carry_spans(nc, t, "carry4", t.span_s, node_ends(t), D, t.sum0, t.fix_node_s)


def node_ends(t):
    return t.lasts.rearrange("(c q) w -> q c w", c=4)[:, :, 0:D]


T = 14
TD = T * D
STEPS = J // (2 * T)
EPS = 1e-5


def chunk(table, i, u, width=D):
    return table[0:NP, :].rearrange("(p j) w -> p j w", p=P)[:, bass.ds((i * 2 + u) * T, T), 0:width]


def per_node(col):
    return col.unsqueeze(2).to_broadcast([P, T, D])


def per_feature(row):
    return row.unsqueeze(1).to_broadcast([P, T, D])


def dense_pass(nc, t, name, kind, src, add, weight, outs, bias=None, x1=None):
    gathered_in = kind in ("round", "join")
    with ExitStack() as ctx:
        def sb(n, shape, dt=F32):
            return ctx.enter_context(nc.sbuf_tensor(f"{name}_{n}", shape, dt))

        def sems(n):
            return [ctx.enter_context(semaphore(nc, f"{name}_{n}{u}")) for u in range(2)]

        A = add.shape[1]
        in0 = sb("in0", [P, 2, T, D])
        in1 = sb("in1", [P, 2, T, A])
        g = sb("g", [P, 2, T, D]) if gathered_in else in0
        gt = sb("gt", [P, 2, TD])
        v = sb("v", [P, 2, T, D])
        sq = sb("sq", [P, 2, T, D])
        stat = sb("stat", [P, 2, 4, T])
        y = sb("y", [P, 2, T, D]) if kind != "round" else None
        second = sb("second", [P, 2, T, D]) if kind != "cheb" else None
        if bias is not None:
            biases = 2 if kind == "join" else 1
            brow, split, rest = sb("brow", [3, 2, TD], BF16), sb("split", [3, 3, P], BF16), sb("rest", [3, 3, P])
            ones = sb("ones", [3, P], BF16)
            bias_chain = ctx.enter_context(semaphore(nc, f"{name}_bias_chain"))
        banks = 1 if kind == "join" else 2
        ps_t = ctx.enter_context(nc.psum_tensor(f"{name}_ps_t", [P, banks, 1024], F32))
        ps_v = ctx.enter_context(nc.psum_tensor(f"{name}_ps_v", [P, banks, 1024], F32))
        in0_ok, in1_ok, added, g_ready = sems("in0_ok"), sems("in1_ok"), sems("added"), sems("g_ready")
        turned, gt_ready, product = sems("turned"), sems("gt_ready"), sems("product")
        v_ready, sq_ready, summed, var_ready = sems("v_ready"), sems("sq_ready"), sems("summed"), sems("var_ready")
        root_ready, inv_ready, masked = sems("root_ready"), sems("inv_ready"), sems("masked")
        scaled, shifted, y_ready, second_ready = sems("scaled"), sems("shifted"), sems("y_ready"), sems("second_ready")
        y_stored, second_stored = sems("y_stored"), sems("second_stored")
        if kind == "join":
            in2 = sb("in2", [P, 2, T, D])
            r = sb("r", [P, 2, T, D])
            rsq = sb("rsq", [P, 2, T, D])
            rstat = sb("rstat", [P, 2, 4, T])
            gw, gmean, grow = sb("gw", [P, P]), sb("gmean", [P, 8]), sb("grow", [1, P])
            beta = sb("beta", [P, D])
            ps_g = ctx.enter_context(nc.psum_tensor(f"{name}_ps_g", [P, 2, 1024], F32))
            in2_ok, r_ready, g_product = sems("in2_ok"), sems("r_ready"), sems("g_product")
            folded = ctx.enter_context(semaphore(nc, f"{name}_folded"))
            rsq_ready, r_summed, r_var, r_root, r_inv = (sems("rsq_ready"), sems("r_summed"), sems("r_var"), sems("r_root"),
                                                         sems("r_inv"))
        bias_turned, bias_ok = (ctx.enter_context(semaphore(nc, f"{name}_{n}")) for n in ("bias_turned", "bias_ok"))
        sp_passed = ctx.enter_context(semaphore(nc, f"{name}_sp_passed"))
        block = ctx.enter_context(nc.Block())
        TURN, PROD, NORM, SHIFT, JOIN = (2, 3, 4, 5, 6) if gathered_in else (1, 2, 3, 4, None)
        deep = {"first": 5, "cheb": 5, "round": 7, "join": 9}[kind]

        @block.sync
        def _(sp):
            @skewed(sp, STEPS, deep)
            def _(ago):
                for i, u in ago(0):
                    if gathered_in:
                        wait(sp, added[u], i)
                    else:
                        wait(sp, turned[u], i)
                    sp.sem_inc(sp_passed, 1)
                    sp.dma_start(in0[:, u], chunk(src, i, u)).then_inc(in0_ok[u], 16)
                    if gathered_in:
                        sp.dma_start(in1[:, u], chunk(add, i, u, A)).then_inc(in1_ok[u], 16)
                if kind == "join":
                    for i, u in ago(SHIFT):
                        wait(sp, r_ready[u], i)
                        sp.sem_inc(sp_passed, 1)
                        sp.dma_start(in2[:, u], chunk(x1, i, u)).then_inc(in2_ok[u], 16)
                if kind != "round":
                    for i, u in ago(deep - 1):
                        sp.wait_ge(y_ready[u], i + 1)
                        sp.sem_inc(sp_passed, 1)
                        sp.dma_start(chunk(outs[0], i, u), y[:, u]).then_inc(y_stored[u], 16)
                if not gathered_in:
                    for i, u in ago(0):
                        wait(sp, v_ready[u], i)
                        sp.sem_inc(sp_passed, 1)
                        sp.dma_start(in1[:, u], chunk(add, i, u, A)).then_inc(in1_ok[u], 16)
                if kind != "cheb":
                    for i, u in ago(deep):
                        sp.wait_ge(second_ready[u], i + 1)
                        sp.sem_inc(sp_passed, 1)
                        sp.dma_start(chunk(outs[-1], i, u), second[:, u]).then_inc(second_stored[u], 16)
            for u in range(2):
                if kind != "round":
                    sp.wait_ge(y_stored[u], STEPS * 16)
                if kind != "cheb":
                    sp.wait_ge(second_stored[u], STEPS * 16)

        @block.gpsimd
        def _(pool):
            if kind == "cheb":
                return

            @skewed(pool, STEPS, SHIFT if kind != "join" else JOIN + 1)
            def _(ago):
                if kind != "round":
                    for i, u in ago(SHIFT if kind == "first" else JOIN + 1):
                        pool.wait_ge(y_ready[u], i + 1)
                        wait(pool, second_stored[u], i * 16)
                        col = (t.dis if kind == "first" else t.dinv)[:, bass.ds((i * 2 + u) * T, T)]
                        nc.gpsimd.tensor_tensor(second[:, u], y[:, u], per_node(col), ALU.mult).then_inc(second_ready[u], 1)
                if gathered_in:
                    for i, u in ago(SHIFT):
                        pool.wait_ge(scaled[u], i + 1)
                        nc.gpsimd.tensor_tensor(v[:, u], v[:, u], per_feature((beta if kind == "join" else t.beta1)[:]),
                                                ALU.add).then_inc(shifted[u], 1)
                    for i, u in ago(0):
                        pool.wait_ge(in0_ok[u], (i + 1) * 16)
                        pool.wait_ge(in1_ok[u], (i + 1) * 16)
                        wait(pool, turned[u], i)
                        nc.gpsimd.tensor_tensor(g[:, u], in0[:, u], in1[:, u], ALU.add).then_inc(added[u], 1)

        @block.vector
        def _(dve):
            if bias is not None:
                c = Chain(dve, bias_chain)
                if kind == "join":
                    f = Chain(dve, folded)
                    f.link(nc.vector.memset(gw[:], 0.0))
                    halves = [(slice(h * D, (h + 1) * D), slice(h * D, (h + 1) * D)) for h in range(2)]
                    blocks = [(gw[p, q], weight[p, q], t.gamma1[p], gmean[p, 0:1]) for p, q in halves]
                    blocks += [(grow[:, q], t.rows[0:1, bias, q], t.gamma1[0:1], gmean[0:1, 2 + n:3 + n])
                               for n, (_, q) in enumerate(halves)]
                    for made, given, gamma, mean in blocks:
                        f.link(nc.vector.tensor_tensor(made, given, gamma, ALU.mult))
                        f.link(nc.vector.tensor_reduce(mean, made, AX.X, ALU.add))
                        f.link(nc.vector.tensor_scalar(mean, mean, 1.0 / D, None, ALU.mult))
                        f.link(nc.vector.tensor_scalar(made, made, mean, None, ALU.subtract))
                    f.link(nc.vector.tensor_reduce(gmean[:, 1:2], t.beta1[:], AX.X, ALU.add))
                    f.link(nc.vector.tensor_scalar(gmean[:, 1:2], gmean[:, 1:2], 1.0 / D, None, ALU.mult))
                    f.link(nc.vector.tensor_scalar(beta[:], t.beta1[:], gmean[:, 1:2], None, ALU.subtract))
                c.link(nc.vector.memset(ones[:], 1.0))
                dve.wait_ge(bias_turned, 1)
                for m in range(biases):
                    c.link(nc.vector.tensor_copy(rest[:, 0, :], ps_t[0:3, 0, m * P:(m + 1) * P]))
                    for k in range(3):
                        c.link(nc.vector.tensor_copy(split[:, k, :], rest[:, k, :]))
                        if k < 2:
                            c.link(nc.vector.tensor_tensor(rest[:, k + 1, :], rest[:, k, :], split[:, k, :], ALU.subtract))
                    c.link(nc.vector.tensor_scalar(rest[:, 0, :], split[:, 0, :], t.ident[0:3, 0:1], None, ALU.mult))
                    for k in (1, 2):
                        c.link(nc.vector.scalar_tensor_tensor(rest[:, k, :], split[:, k, :], t.ident[0:3, k:k + 1],
                                                              rest[:, k - 1, :], ALU.mult, ALU.add))
                    for n in range(T // 2):
                        ins = nc.vector.tensor_copy(brow[:, m, n * P:(n + 1) * P], rest[:, 2, :])
                    c.link(ins)
                dve.sem_inc(bias_ok, 1)

            @skewed(dve, STEPS, {"first": NORM, "cheb": NORM, "round": SHIFT, "join": JOIN}[kind])
            def _(ago):
                for i, u in ago(NORM):
                    dve.wait_ge(sq_ready[u], i + 1)
                    nc.vector.tensor_reduce(stat[:, u, 0, :], sq[:, u], AX.X, ALU.add).then_inc(summed[u], 1)
                    dve.wait_ge(summed[u], i + 1)
                    nc.vector.tensor_scalar(stat[:, u, 1, :], stat[:, u, 0, :], 1.0 / D, EPS, ALU.mult, ALU.add).then_inc(var_ready[u], 1)
                if kind == "join":
                    for i, u in ago(JOIN):
                        dve.wait_ge(rsq_ready[u], i + 1)
                        nc.vector.tensor_reduce(rstat[:, u, 0, :], rsq[:, u], AX.X, ALU.add).then_inc(r_summed[u], 1)
                        dve.wait_ge(r_summed[u], i + 1)
                        nc.vector.tensor_scalar(rstat[:, u, 1, :], rstat[:, u, 0, :], 1.0 / D, EPS, ALU.mult, ALU.add).then_inc(r_var[u], 1)
                if gathered_in:
                    for i, u in ago(1):
                        dve.wait_ge(added[u], i + 1)
                        nc.vector.tensor_tensor(g[:, u], g[:, u], per_node(t.dis[:, bass.ds((i * 2 + u) * T, T)]),
                                                ALU.mult).then_inc(g_ready[u], 1)
                else:
                    for i, u in ago(PROD):
                        dve.wait_ge(product[u], i + 1)
                        dve.wait_ge(in1_ok[u], (i + 1) * 16)
                        wait(dve, sq_ready[u], i)
                        if kind == "first":
                            nc.vector.tensor_copy(t.deg[:, bass.ds((i * 2 + u) * T, T)], in1[:, u, :, D])
                        nc.vector.tensor_tensor(v[:, u], ps_v[:, u, 0:TD].rearrange("p (t d) -> p t d", t=T),
                                                in1[:, u, :, 0:D], ALU.add).then_inc(v_ready[u], 1)
                for i, u in ago(NORM):
                    dve.wait_ge(root_ready[u], i + 1)
                    nc.vector.reciprocal(stat[:, u, 3, :], stat[:, u, 2, :]).then_inc(inv_ready[u], 1)
                    dve.wait_ge(inv_ready[u], i + 1)
                    if kind == "cheb":
                        nc.vector.tensor_tensor(stat[:, u, 3, :], stat[:, u, 3, :], t.real[:, bass.ds((i * 2 + u) * T, T)],
                                                ALU.mult).then_inc(masked[u], 1)
                        dve.wait_ge(masked[u], i + 1)
                    if kind == "join":
                        dve.wait_ge(g_product[u], i + 1)
                        nc.vector.tensor_tensor(v[:, u], ps_g[:, u, 0:TD].rearrange("p (t d) -> p t d", t=T),
                                                per_node(stat[:, u, 3, :]), ALU.mult).then_inc(scaled[u], 1)
                    elif gathered_in:
                        nc.vector.tensor_tensor(v[:, u], ps_v[:, u, 0:TD].rearrange("p (t d) -> p t d", t=T),
                                                per_node(stat[:, u, 3, :]), ALU.mult).then_inc(v_ready[u], 1)
                        dve.wait_ge(v_ready[u], i + 1)
                        nc.vector.tensor_tensor(v[:, u], v[:, u], per_feature(t.gamma1[:]), ALU.mult).then_inc(scaled[u], 1)
                    else:
                        wait(dve, y_stored[u], i * 16)
                        if kind == "first":
                            wait(dve, second_ready[u], i)
                        nc.vector.tensor_tensor(y[:, u], v[:, u], per_node(stat[:, u, 3, :]), ALU.mult).then_inc(y_ready[u], 1)
                if kind == "round":
                    for i, u in ago(SHIFT):
                        dve.wait_ge(shifted[u], i + 1)
                        wait(dve, second_stored[u], i * 16)
                        nc.vector.tensor_tensor(second[:, u], v[:, u], per_node(t.dis[:, bass.ds((i * 2 + u) * T, T)]),
                                                ALU.mult).then_inc(second_ready[u], 1)
                if kind == "join":
                    for i, u in ago(JOIN):
                        dve.wait_ge(r_root[u], i + 1)
                        nc.vector.reciprocal(rstat[:, u, 3, :], rstat[:, u, 2, :]).then_inc(r_inv[u], 1)
                        dve.wait_ge(r_inv[u], i + 1)
                        wait(dve, y_stored[u], i * 16)
                        wait(dve, second_ready[u], i)
                        nc.vector.tensor_tensor(y[:, u], r[:, u], per_node(rstat[:, u, 3, :]), ALU.mult).then_inc(y_ready[u], 1)
                    for i, u in ago(SHIFT):
                        dve.wait_ge(shifted[u], i + 1)
                        dve.wait_ge(in2_ok[u], (i + 1) * 16)
                        nc.vector.tensor_tensor(r[:, u], v[:, u], in2[:, u], ALU.add).then_inc(r_ready[u], 1)

        @block.tensor
        def _(pe):
            if bias is not None:
                ins = nc.tensor.matmul(ps_t[0:3, 0, 0:P], t.ones[0:1, 0:3], t.rows[0:1, bias, :], start=True, stop=True)
                if kind == "join":
                    pe.wait_ge(folded, 20)
                    ins = nc.tensor.matmul(ps_t[0:3, 0, P:2 * P], t.ones[0:1, 0:3], grow[:], start=True, stop=True)
                ins.then_inc(bias_turned, 1)
                pe.wait_ge(bias_ok, 1)

            @skewed(pe, STEPS, PROD)
            def _(ago):
                for i, u in ago(TURN):
                    if gathered_in:
                        pe.wait_ge(g_ready[u], i + 1)
                    else:
                        pe.wait_ge(in0_ok[u], (i + 1) * 16)
                    if kind == "join":
                        wait(pe, gt_ready[1 - u], i + u)
                    else:
                        wait(pe, gt_ready[u], i)
                    for n in range(T // 2):
                        ins = nc.tensor.transpose(ps_t[:, u % banks, n * P:(n + 1) * P],
                                                  g[:, u, 2 * n:2 * n + 2, :].rearrange("p t d -> p (t d)"), t.ident[:])
                    ins.then_inc(turned[u], 1)
                for i, u in ago(PROD):
                    pe.wait_ge(gt_ready[u], i + 1)

                    def products(out, wts, which):
                        if bias is not None:
                            for lo, hi in ((0, 512), (512, TD)):
                                nc.tensor.matmul(out[:, lo:hi], ones[:], brow[:, which, lo:hi], start=True, stop=False,
                                                 skip_group_check=True)
                        for n in range(T // 2):
                            ins = nc.tensor.matmul(out[:, n * P:(n + 1) * P], gt[:, u, n * P:(n + 1) * P], wts[:],
                                                   start=bias is None, stop=True, skip_group_check=True)
                        return ins

                    if kind == "join":
                        wait(pe, sq_ready[1 - u], i + u)
                    else:
                        wait(pe, v_ready[u], i)
                    products(ps_v[:, u % banks], weight, 0).then_inc(product[u], 1)
                    if kind == "join":
                        wait(pe, scaled[u], i)
                        products(ps_g[:, u], gw, 1).then_inc(g_product[u], 1)

        @block.scalar
        def _(act):
            @skewed(act, STEPS, JOIN if kind == "join" else NORM)
            def _(ago):
                for i, u in ago(NORM):
                    act.wait_ge(var_ready[u], i + 1)
                    nc.scalar.activation(stat[:, u, 2, :], stat[:, u, 1, :], ACT.Sqrt).then_inc(root_ready[u], 1)
                if kind == "join":
                    for i, u in ago(JOIN):
                        act.wait_ge(r_var[u], i + 1)
                        nc.scalar.activation(rstat[:, u, 2, :], rstat[:, u, 1, :], ACT.Sqrt).then_inc(r_root[u], 1)
                for i, u in ago(TURN):
                    act.wait_ge(turned[u], i + 1)
                    wait(act, (g_product if kind == "join" else product)[u], i)
                    nc.scalar.copy(gt[:, u], ps_t[:, u % banks, 0:TD]).then_inc(gt_ready[u], 1)
                for i, u in ago(PROD):
                    if gathered_in:
                        act.wait_ge(product[u], i + 1)
                        squared = ps_v[:, u % banks, 0:TD]
                    else:
                        act.wait_ge(v_ready[u], i + 1)
                        squared = v[:, u].rearrange("p t d -> p (t d)")
                    wait(act, summed[u], i)
                    nc.scalar.activation(sq[:, u].rearrange("p t d -> p (t d)"), squared, ACT.Square).then_inc(sq_ready[u], 1)
                if kind == "join":
                    for i, u in ago(SHIFT):
                        act.wait_ge(r_ready[u], i + 1)
                        wait(act, r_summed[u], i)
                        nc.scalar.activation(rsq[:, u], r[:, u], ACT.Square).then_inc(rsq_ready[u], 1)


def node_degrees(nc, t, ctx, part):
    with ExitStack() as c2:
        n = f"deg{part}_"
        tmp = c2.enter_context(nc.sbuf_tensor(n + "tmp", [P, 2, J], F32))
        loaded = c2.enter_context(semaphore(nc, n + "loaded"))
        chain = c2.enter_context(semaphore(nc, n + "chain"))
        root = c2.enter_context(semaphore(nc, n + "root"))
        block = c2.enter_context(nc.Block())
        if part == 0:
            index = c2.enter_context(nc.sbuf_tensor(n + "index", [P, J], I32))

            @block.gpsimd
            def _(pool):
                nc.gpsimd.iota(index[:], [[1, J]], base=0, channel_multiplier=J).then_inc(root, 1)

            @block.sync
            def _(sp):
                sp.dma_start(tmp[:, 0, :], t.in_degree.rearrange("(p j) o -> p (j o)", p=P)).then_inc(loaded, 16)

            @block.vector
            def _(dve):
                c = Chain(dve, chain)
                dve.wait_ge(root, 1)
                dve.wait_ge(loaded, 16)
                c.link(nc.vector.tensor_scalar(t.real[:], index[:], float(N), None, ALU.is_lt))
                c.link(nc.vector.tensor_scalar(tmp[:, 0, :], tmp[:, 0, :], 1.0, None, ALU.add))
                dve.wait_ge(root, 2)
                nc.vector.reciprocal(t.dis[:], tmp[:, 1, :])

            @block.scalar
            def _(act):
                act.wait_ge(chain, 2)
                nc.scalar.activation(tmp[:, 1, :], tmp[:, 0, :], ACT.Sqrt).then_inc(root, 1)
        else:
            @block.vector
            def _(dve):
                inverse_root(Chain(dve, chain), nc, dve, t.deg[:], t.dinv[:], tmp[:, 0, :], root)

            @block.scalar
            def _(act):
                act.wait_ge(chain, 3)
                nc.scalar.activation(t.dinv[:], t.dinv[:], ACT.Sqrt).then_inc(root, 1)


def gin_first(nc, t, x3, add, z1t):
    with ExitStack() as ctx:
        def sb(n, shape, dt=F32):
            return ctx.enter_context(nc.sbuf_tensor(f"bn_{n}", shape, dt))

        def sem(n):
            return ctx.enter_context(semaphore(nc, f"bn_{n}"))

        def sems(n):
            return [sem(n + str(u)) for u in range(2)]

        in0, in1, g = sb("in0", [P, 2, T, D]), sb("in1", [P, 2, T, D]), sb("g", [P, 2, T, D])
        gt, z, junk = sb("gt", [P, 2, TD]), sb("z", [P, 2, TD]), sb("junk", [P, 2, TD])
        sums = sb("sums", [P, 2, 2 * STEPS])
        total, tot2, fold, tmp = sb("total", [P, 2]), sb("total2", [P, 2]), sb("fold", [P, P]), sb("tmp", [P, 4])
        ps_t = ctx.enter_context(nc.psum_tensor("bn_ps_t", [P, 2, 1024], F32))
        ps_z = ctx.enter_context(nc.psum_tensor("bn_ps_z", [P, 2, 1024], F32))
        loaded, g_ready, turned, gt_ready, product = sems("loaded"), sems("g_ready"), sems("turned"), sems("gt_ready"), sems("product")
        z_ready, squared, stored, sp_passed, chain, folded, root = sems("z_ready"), sems("squared"), sems("stored"), sem("sp_passed"), sem("chain"), sem("folded"), sem("root")
        block = ctx.enter_context(nc.Block())

        @block.sync
        def _(sp):
            @repeat(sp, STEPS)
            def _(i):
                for u in range(2):
                    wait(sp, g_ready[u], i)
                    sp.sem_inc(sp_passed, 1)
                    sp.dma_start(in0[:, u], chunk(x3, i, u)).then_inc(loaded[u], 16)
                    sp.dma_start(in1[:, u], chunk(add, i, u)).then_inc(loaded[u], 16)

        @block.vector
        def _(dve):
            @repeat(dve, STEPS)
            def _(i):
                for u in range(2):
                    dve.wait_ge(loaded[u], (i + 1) * 32)
                    wait(dve, turned[u], i)
                    nc.vector.scalar_tensor_tensor(g[:, u], in0[:, u], t.eps1[:], in1[:, u], ALU.mult, ALU.add).then_inc(g_ready[u], 1)
            c = Chain(dve, chain)
            for u in range(2):
                dve.wait_ge(squared[u], STEPS)
            for h in range(2):
                half = slice(h * D, (h + 1) * D)
                for k in range(2):
                    nc.vector.tensor_copy(fold[half, k * D:(k + 1) * D], t.ident[half, half])
            c.link(nc.vector.tensor_reduce(total[:], sums[:], AX.X, ALU.add))
            dve.wait_ge(folded, 1)
            c.link(nc.vector.tensor_scalar(tot2[:], ps_t[:, 0, 0:2], 1.0 / N, None, ALU.mult))
            c.link(nc.vector.tensor_tensor(tmp[:, 0:1], tot2[:, 0:1], tot2[:, 0:1], ALU.mult))
            c.link(nc.vector.scalar_tensor_tensor(tmp[:, 1:2], tot2[:, 1:2], EPS, tmp[:, 0:1], ALU.add, ALU.subtract))
            dve.wait_ge(root, 1)
            c.link(nc.vector.reciprocal(tmp[:, 3:4], tmp[:, 2:3]))
            c.link(nc.vector.tensor_tensor(t.bn[:, 0:1], t.gb3[:, 0:1], tmp[:, 3:4], ALU.mult))
            c.link(nc.vector.tensor_tensor(tmp[:, 0:1], tot2[:, 0:1], t.bn[:, 0:1], ALU.mult))
            c.link(nc.vector.tensor_tensor(t.bn[:, 1:2], t.gb3[:, 1:2], tmp[:, 0:1], ALU.subtract))

        @block.tensor
        def _(pe):
            @repeat(pe, STEPS)
            def _(i):
                for u in range(2):
                    pe.wait_ge(g_ready[u], i + 1)
                    wait(pe, gt_ready[u], i)
                    for n in range(T // 2):
                        ins = nc.tensor.transpose(ps_t[:, u, n * P:(n + 1) * P],
                                                  g[:, u, 2 * n:2 * n + 2, :].rearrange("p t d -> p (t d)"), t.ident[:])
                    ins.then_inc(turned[u], 1)
                for u in range(2):
                    pe.wait_ge(gt_ready[u], i + 1)
                    wait(pe, squared[u], i)
                    for lo, hi in ((0, 512), (512, TD)):
                        ins = nc.tensor.matmul(ps_z[:, u, lo:hi], t.dense3[:], gt[:, u, lo:hi], start=True, stop=True)
                    ins.then_inc(product[u], 1)
            pe.wait_ge(chain, 1)
            nc.tensor.matmul(ps_t[:, 0, 0:2], fold[:], total[:], start=True, stop=True).then_inc(folded, 1)

        @block.scalar
        def _(act):
            @repeat(act, STEPS)
            def _(i):
                for u in range(2):
                    act.wait_ge(turned[u], i + 1)
                    wait(act, product[u], i)
                    nc.scalar.copy(gt[:, u], ps_t[:, u, 0:TD]).then_inc(gt_ready[u], 1)
                for u in range(2):
                    c = bass.ds(i * 2 + u, 1)
                    act.wait_ge(product[u], i + 1)
                    wait(act, stored[u], i * 16)
                    nc.scalar.activation(z[:, u], ps_z[:, u, 0:TD], ACT.Identity, accum_out=sums[:, 0, c]).then_inc(z_ready[u], 1)
                    wait(act, squared[u], i)
                    nc.scalar.activation(junk[:, u], ps_z[:, u, 0:TD], ACT.Square, accum_out=sums[:, 1, c]).then_inc(squared[u], 1)
                    act.wait_ge(z_ready[u], i + 1)
                    act.dma_start(z1t[c].rearrange("o p e -> p (o e)"), z[:, u]).then_inc(stored[u], 16)
            for u in range(2):
                act.wait_ge(stored[u], STEPS * 16)
            act.wait_ge(chain, 4)
            nc.scalar.activation(tmp[:, 2:3], tmp[:, 1:2], ACT.Sqrt).then_inc(root, 1)


def gin_last(nc, t, x3, z1t, out):
    with ExitStack() as ctx:
        def sb(n, shape, dt=F32):
            return ctx.enter_context(nc.sbuf_tensor(f"last_{n}", shape, dt))

        def sem(n):
            return ctx.enter_context(semaphore(nc, f"last_{n}"))

        def sems(n):
            return [sem(n + str(u)) for u in range(2)]

        in0, v, sq, y = (sb(n, [P, 2, T, D]) for n in ("in0", "v", "sq", "y"))
        z, r, stat = sb("z", [P, 2, TD]), sb("r", [P, 2, TD]), sb("stat", [P, 2, 4, T])
        ps_v = ctx.enter_context(nc.psum_tensor("last_ps_v", [P, 2, 1024], F32))
        z_ok, x_ok, r_ready, product, v_ready = sems("z_ok"), sems("x_ok"), sems("r_ready"), sems("product"), sems("v_ready")
        sq_ready, summed, var_ready, root_ready = sems("sq_ready"), sems("summed"), sems("var_ready"), sems("root_ready")
        inv_ready, y_ready, stored, sp_passed = sems("inv_ready"), sems("y_ready"), sems("stored"), sem("sp_passed")
        block = ctx.enter_context(nc.Block())

        @block.sync
        def _(sp):
            @skewed(sp, STEPS, 4)
            def _(ago):
                for i, u in ago(0):
                    wait(sp, r_ready[u], i)
                    sp.sem_inc(sp_passed, 1)
                    sp.dma_start(z[:, u], z1t[bass.ds(i * 2 + u, 1)].rearrange("o p e -> p (o e)")).then_inc(z_ok[u], 16)
                for i, u in ago(4):
                    sp.wait_ge(y_ready[u], i + 1)
                    sp.sem_inc(sp_passed, 1)
                    sp.dma_start(chunk(out, i, u), y[:, u]).then_inc(stored[u], 16)
                for i, u in ago(0):
                    wait(sp, v_ready[u], i)
                    sp.sem_inc(sp_passed, 1)
                    sp.dma_start(in0[:, u], chunk(x3, i, u)).then_inc(x_ok[u], 16)
            for u in range(2):
                sp.wait_ge(stored[u], STEPS * 16)

        @block.scalar
        def _(act):
            @skewed(act, STEPS, 3)
            def _(ago):
                for i, u in ago(3):
                    act.wait_ge(var_ready[u], i + 1)
                    nc.scalar.activation(stat[:, u, 2, :], stat[:, u, 1, :], ACT.Sqrt).then_inc(root_ready[u], 1)
                for i, u in ago(0):
                    act.wait_ge(z_ok[u], (i + 1) * 16)
                    wait(act, product[u], i)
                    nc.scalar.activation(r[:, u], z[:, u], ACT.Relu, scale=t.bn[:, 0:1], bias=t.bn[:, 1:2]).then_inc(r_ready[u], 1)
                for i, u in ago(2):
                    act.wait_ge(v_ready[u], i + 1)
                    wait(act, summed[u], i)
                    nc.scalar.activation(sq[:, u], v[:, u], ACT.Square).then_inc(sq_ready[u], 1)

        @block.tensor
        def _(pe):
            @skewed(pe, STEPS, 1)
            def _(ago):
                for i, u in ago(1):
                    pe.wait_ge(r_ready[u], i + 1)
                    wait(pe, v_ready[u], i)
                    for n in range(T // 2):
                        ins = nc.tensor.matmul(ps_v[:, u, n * P:(n + 1) * P], r[:, u, n * P:(n + 1) * P], t.out3[:], start=True, stop=True)
                    ins.then_inc(product[u], 1)

        @block.vector
        def _(dve):
            @skewed(dve, STEPS, 3)
            def _(ago):
                for i, u in ago(3):
                    dve.wait_ge(sq_ready[u], i + 1)
                    nc.vector.tensor_reduce(stat[:, u, 0, :], sq[:, u], AX.X, ALU.add).then_inc(summed[u], 1)
                    dve.wait_ge(summed[u], i + 1)
                    nc.vector.tensor_scalar(stat[:, u, 1, :], stat[:, u, 0, :], 1.0 / D, EPS, ALU.mult, ALU.add).then_inc(var_ready[u], 1)
                for i, u in ago(2):
                    dve.wait_ge(product[u], i + 1)
                    dve.wait_ge(x_ok[u], (i + 1) * 16)
                    wait(dve, sq_ready[u], i)
                    nc.vector.tensor_tensor(v[:, u], ps_v[:, u, 0:TD].rearrange("p (t d) -> p t d", t=T), in0[:, u], ALU.add).then_inc(v_ready[u], 1)
                for i, u in ago(3):
                    dve.wait_ge(root_ready[u], i + 1)
                    nc.vector.reciprocal(stat[:, u, 3, :], stat[:, u, 2, :]).then_inc(inv_ready[u], 1)
                    dve.wait_ge(inv_ready[u], i + 1)
                    wait(dve, stored[u], i * 16)
                    nc.vector.tensor_tensor(y[:, u], v[:, u], per_node(stat[:, u, 3, :]), ALU.mult).then_inc(y_ready[u], 1)


def node_tensors(nc, ctx, t):
    def sb(name, shape, dt=F32):
        return ctx.enter_context(nc.sbuf_tensor(name, shape, dt))

    def dram(name, shape, dt=F32):
        return nc.dram_tensor(name, shape, dt).ap()

    t.dis = sb("dis", [P, J])
    t.deg = sb("deg", [P, J])
    t.dinv = sb("dinv", [P, J])
    t.real = sb("real", [P, J])
    t.bn = sb("bn", [P, 2])
    t.x1 = dram("x1", [NP, D])
    t.xt = dram("xt", [NP, D])
    t.x2 = dram("x2", [NP, D])
    t.xs = dram("xs", [NP, D])
    t.x3 = dram("x3", [NP, D])
    t.z1t = dram("z1t", [2 * STEPS, P, TD])


def four_layers(nc, w, out):
    SPENT.clear()
    with ExitStack() as ctx:
        t = tensors(nc, ctx)
        add_tensors(nc, ctx, t)
        node_tensors(nc, ctx, t)
        constants(nc, t)
        sort_edges(nc, t, w["src"], w["dst"], w["etype"], w["weight"])
        edge_fields(nc, t)
        spans(nc, t, 0, t.row_s[0], t.span_s, t.fix_edge[:], t.fix_node_s[:])
        spans(nc, t, 1, t.row_t[0], t.span_t, None, t.fix_node_t[:])
        weights(nc, ctx, t, w)
        edge_scores(nc, t, w["x"])
        edge_softmax(nc, t)
        attention(nc, t)
        recycle(nc)
        node_degrees(nc, t, ctx, 0)
        dense_pass(nc, t, "first", "first", w["x"], t.sum0, t.dense0, [t.x1, t.xt])
        node_degrees(nc, t, ctx, 1)
        for k in range(4):
            recycle(nc)
            edge_pass(nc, t, f"gcn{k}", "plain", t.eq_t, table=t.xt, idx=t.t_row_s, put=t.put_t, target=t.sum_t)
            carry_spans(nc, t, f"gcn_carry{k}", t.span_t, node_ends(t), D, t.sum_t, t.fix_node_t)
            if k < 3:
                dense_pass(nc, t, f"round{k}", "round", t.xt, t.sum_t, t.dense1, [t.xt], bias=0)
            else:
                dense_pass(nc, t, "join", "join", t.xt, t.sum_t, t.dense1, [t.x2, t.xs], bias=0, x1=t.x1)
        recycle(nc)
        edge_pass(nc, t, "cheb1", "cheb1", t.eq_s, table=t.xs, idx=t.t_col, target=t.cheb_rows)
        ends = t.cheb_rows[0:EP, :].rearrange("(c q p) w -> p q c w", c=4, q=Q)[P - 1]
        carry_spans(nc, t, "cheb_carry1", t.span_s, ends, D, t.cheb_rows, t.fix_edge)
        edge_pass(nc, t, "cheb2", "cheb2", t.eq_s, table=t.cheb_rows, idx=t.next_col, put=t.put_s, target=t.sum_s)
        carry_spans(nc, t, "cheb_carry2", t.span_s, node_ends(t), D, t.sum_s, t.fix_node_s)
        recycle(nc)
        dense_pass(nc, t, "chebd", "cheb", t.x2, t.sum_s, t.dense2, [t.x3], bias=1)
        edge_pass(nc, t, "gin", "gin", t.eq_s, table=t.x3, idx=t.t_col, put=t.put_s, target=t.sum_s)
        carry_spans(nc, t, "gin_carry", t.span_s, node_ends(t), D, t.sum_s, t.fix_node_s)
        recycle(nc)
        gin_first(nc, t, t.x3, t.sum_s, t.z1t)
        gin_last(nc, t, t.x3, t.z1t, out)


def kernel(**inputs):
    import numpy as np
    import concourse.bacc as bacc
    from concourse.bass_utils import run_bass_kernel_spmd

    a = {k: np.asarray(v) for k, v in inputs.items()}

    def tile_major(v, pad):
        out = np.full(EP, pad, v.dtype)
        out[:E] = v
        return np.ascontiguousarray(out.reshape(TILES, P).T)

    x = np.zeros((NP, D), a["x"].dtype)
    x[:N] = a["x"]
    arrays = {"x": x, "src": tile_major(a["src"], N), "dst": tile_major(a["dst"], N),
              "etype": tile_major(a["edge_type_200"], 0), "weight": tile_major(a["edge_weight"], 0)}
    for k, v in a.items():
        if k.startswith("L"):
            if k in ("L3_gnn_W_lin", "L3_gnn_W1", "L3_gnn_W2"):
                arrays[k + "_T"] = np.ascontiguousarray(v.T)
            else:
                arrays[k] = np.ascontiguousarray(v.reshape(1, -1) if v.ndim == 1 else v)
    nc = bacc.Bacc("TRN2", target_bir_lowering=False, num_devices=1)
    w = {}
    for name, v in arrays.items():
        w[name] = nc.dram_tensor(f"in_{name}", v.shape, mybir.dt.from_np(v.dtype), kind="ExternalInput").ap()
    out = nc.dram_tensor("out", [NP, D], F32, kind="ExternalOutput").ap()
    four_layers(nc, w, out)
    r = run_bass_kernel_spmd(nc, [{f"in_{name}": v for name, v in arrays.items()}], core_ids=[0])
    return r.results[0]["out"][:N]
```
